# Optimizing a Trainium2 kernel written in Bass

```python
import numpy as np
import jax
import jax.numpy as jnp

def _softmax(x, axis=-1):
    return jax.nn.softmax(x, axis=axis)

def _gelu(x):
    return jax.nn.gelu(x, approximate=True)

def _silu(x):
    return jax.nn.silu(x)

def _sigmoid(x):
    return jax.nn.sigmoid(x)

def _layernorm(x, axis=-1, eps=1e-05):
    m = jnp.mean(x, axis=axis, keepdims=True)
    v = jnp.var(x, axis=axis, keepdims=True)
    return (x - m) / jnp.sqrt(v + eps)

def _scatter_add(tgt, idx, src, axis=0):
    return tgt.at[idx].add(src)

def _segment_sum(src, seg, n):
    return jax.ops.segment_sum(src, seg, n)
kernel_name = 'mk_flamingo_gated_d2_seqx_r8_ff81c3'

def setup_inputs(seed: int=0):
    np.random.seed(seed)
    _w = jnp.asarray

    def _rec_inputs():
        import jax
        import jax.numpy as jnp
        _rk = jax.random.key(seed)
        x = -0.000125 + 0.9999 * jax.random.normal(jax.random.fold_in(_rk, 1), (16, 128, 256), jnp.float32)
        _lenS = 128 - jax.random.randint(jax.random.fold_in(_rk, 7), (16,), 0, max(1, 128 // 4) + 1, jnp.int32)
        _lenS2 = 128 - jax.random.randint(jax.random.fold_in(_rk, 8), (16,), 0, max(1, 128 // 4) + 1, jnp.int32)
        _ctx_2048P = jax.random.normal(jax.random.fold_in(_rk, 11), (16, 16, 256), jnp.float32)
        _ctx_2048c = jax.random.dirichlet(jax.random.fold_in(_rk, 511), 0.3 * jnp.ones((16,), jnp.float32), (16, 128))
        _ctx_2048t = jnp.einsum('bsk,bkd->bsd', _ctx_2048c, _ctx_2048P)
        _ctx_2048t = _ctx_2048t * jax.lax.rsqrt(jnp.mean(jnp.square(_ctx_2048t)) + 1e-12) * 0.953939
        ctx_2048 = -1.52775e-05 + 0.999936 * (_ctx_2048t + 0.3 * jax.random.normal(jax.random.fold_in(_rk, 611), (16, 128, 256), jnp.float32))
        _g = jax.random.normal(jax.random.fold_in(_rk, 9001), (2, 2), jnp.float32)
        _g = jnp.sign(_g) * jnp.maximum(jnp.abs(_g), 1.0) + (_g == 0) * 1.0
        g_xattn = _g[0]
        g_ffn = _g[1]
        return (x, ctx_2048, g_xattn, g_ffn)
    x, ctx_2048, g_xattn, g_ffn = _rec_inputs()

    def _L0_xattn_setup():
        import jax, jax.numpy as jnp
        import numpy as np
        B, DIM1, DIM2, LATENT, T = (16, 128, 128, 64, 256)
        LN_EPS = 1e-05
        key = jax.random.key(seed)
        ks = jax.random.split(key, 8)

        def xavier(k, shape):
            fan_out, fan_in = shape
            std = float(np.sqrt(2.0 / (fan_in + fan_out)))
            return jax.random.normal(k, shape, dtype=jnp.float32) * std
        return {'input1': jax.random.normal(ks[0], (B, DIM1, T), dtype=jnp.float32), 'input2': jax.random.normal(ks[1], (B, DIM2, T), dtype=jnp.float32), 'theta_w': xavier(ks[2], (LATENT, DIM2)), 'theta_b': jnp.zeros((LATENT,), jnp.float32), 'phi_w': xavier(ks[3], (LATENT, DIM1)), 'phi_b': jnp.zeros((LATENT,), jnp.float32), 'g_w': xavier(ks[4], (LATENT, DIM1)), 'g_b': jnp.zeros((LATENT,), jnp.float32), 'ln_gamma': jnp.ones((LATENT, T), jnp.float32), 'ln_beta': jnp.zeros((LATENT, T), jnp.float32), 'out_w': xavier(ks[5], (DIM2, LATENT)), 'out_b': jnp.zeros((DIM2,), jnp.float32)}
    _L0_xattn_all = _L0_xattn_setup()
    _L0_xattn_in = {k: v for k, v in _L0_xattn_all.items() if k in ('theta_w', 'theta_b', 'phi_w', 'phi_b', 'g_w', 'g_b', 'ln_gamma', 'ln_beta', 'out_w', 'out_b')}
    del _L0_xattn_all

    def _L0_ffn_setup():
        import jax, jax.numpy as jnp
        import numpy as np
        DIM = 256
        EXPERT_DIM = 128
        N_EXPERTS = 16
        TOPK = 2
        N_SHARED = 1
        B, T = (4, 256)
        key = jax.random.key(seed)
        ks = jax.random.split(key, 9)
        s = 0.02
        return {'x': jax.random.normal(ks[0], (B, T, DIM), jnp.float32), 'router_w': jax.random.normal(ks[1], (N_EXPERTS, DIM), jnp.float32) * s, 'router_bias': jnp.zeros((N_EXPERTS,), jnp.float32), 'Wu': jax.random.normal(ks[2], (N_EXPERTS, DIM, EXPERT_DIM), jnp.float32) * s, 'Wg': jax.random.normal(ks[3], (N_EXPERTS, DIM, EXPERT_DIM), jnp.float32) * s, 'Wd': jax.random.normal(ks[4], (N_EXPERTS, EXPERT_DIM, DIM), jnp.float32) * s, 'Su': jax.random.normal(ks[5], (N_SHARED, DIM, EXPERT_DIM * TOPK), jnp.float32) * s, 'Sg': jax.random.normal(ks[6], (N_SHARED, DIM, EXPERT_DIM * TOPK), jnp.float32) * s, 'Sd': jax.random.normal(ks[7], (N_SHARED, EXPERT_DIM * TOPK, DIM), jnp.float32) * s}
    _L0_ffn_all = _L0_ffn_setup()
    _L0_ffn_in = {k: v for k, v in _L0_ffn_all.items() if k in ('router_w', 'router_bias', 'Wu', 'Wg', 'Wd', 'Su', 'Sg', 'Sd')}
    del _L0_ffn_all

    def _L1_xattn_setup():
        import jax, jax.numpy as jnp
        import numpy as np
        N_HEAD = 8
        key = jax.random.key(seed)
        k1, k2, k3 = jax.random.split(key, 3)
        B, D, L = (4, 128, 256)
        q = jax.random.normal(k1, (B, D, L), dtype=jnp.float32)
        k = jax.random.normal(k2, (B, D, L), dtype=jnp.float32)
        v = jax.random.normal(k3, (B, D, L), dtype=jnp.float32)
        gamma = jnp.ones((), dtype=jnp.float32)
        return {'q': q, 'k': k, 'v': v, 'gamma': gamma}
    _L1_xattn_all = _L1_xattn_setup()
    _L1_xattn_in = {k: v for k, v in _L1_xattn_all.items() if k in ('gamma',)}
    del _L1_xattn_all

    def _L1_ffn_setup():
        import jax, jax.numpy as jnp
        import numpy as np
        B, S, D = (4, 128, 256)
        H = 512
        NE = 8
        TOPK = 2
        key = jax.random.key(seed)
        ks = jax.random.split(key, 9)
        s = lambda fan_in: 1.0 / np.sqrt(fan_in)
        return {'x': jax.random.normal(ks[0], (B, S, D), dtype=jnp.float32), 'W1': jax.random.normal(ks[1], (NE, D, H), dtype=jnp.float32) * s(D), 'b1': jnp.zeros((NE, H), dtype=jnp.float32), 'W2': jax.random.normal(ks[2], (NE, H, H), dtype=jnp.float32) * s(H), 'b2': jnp.zeros((NE, H), dtype=jnp.float32), 'W3': jax.random.normal(ks[3], (NE, H, D), dtype=jnp.float32) * s(H), 'b3': jnp.zeros((NE, D), dtype=jnp.float32), 'Wg': jax.random.normal(ks[4], (D, NE), dtype=jnp.float32) * s(D), 'bg': jnp.zeros((NE,), dtype=jnp.float32)}
    _L1_ffn_all = _L1_ffn_setup()
    _L1_ffn_in = {k: v for k, v in _L1_ffn_all.items() if k in ('W1', 'b1', 'W2', 'b2', 'W3', 'b3', 'Wg', 'bg')}
    del _L1_ffn_all
    return {'x': x, 'ctx_2048': ctx_2048, 'g_xattn': g_xattn, 'g_ffn': g_ffn, 'L0_xattn_theta_w': _L0_xattn_in['theta_w'], 'L0_xattn_theta_b': _L0_xattn_in['theta_b'], 'L0_xattn_phi_w': _L0_xattn_in['phi_w'], 'L0_xattn_phi_b': _L0_xattn_in['phi_b'], 'L0_xattn_g_w': _L0_xattn_in['g_w'], 'L0_xattn_g_b': _L0_xattn_in['g_b'], 'L0_xattn_ln_gamma': _L0_xattn_in['ln_gamma'], 'L0_xattn_ln_beta': _L0_xattn_in['ln_beta'], 'L0_xattn_out_w': _L0_xattn_in['out_w'], 'L0_xattn_out_b': _L0_xattn_in['out_b'], 'L0_ffn_router_w': _L0_ffn_in['router_w'], 'L0_ffn_router_bias': _L0_ffn_in['router_bias'], 'L0_ffn_Wu': _L0_ffn_in['Wu'], 'L0_ffn_Wg': _L0_ffn_in['Wg'], 'L0_ffn_Wd': _L0_ffn_in['Wd'], 'L0_ffn_Su': _L0_ffn_in['Su'], 'L0_ffn_Sg': _L0_ffn_in['Sg'], 'L0_ffn_Sd': _L0_ffn_in['Sd'], 'L1_xattn_gamma': _L1_xattn_in['gamma'], 'L1_ffn_W1': _L1_ffn_in['W1'], 'L1_ffn_b1': _L1_ffn_in['b1'], 'L1_ffn_W2': _L1_ffn_in['W2'], 'L1_ffn_b2': _L1_ffn_in['b2'], 'L1_ffn_W3': _L1_ffn_in['W3'], 'L1_ffn_b3': _L1_ffn_in['b3'], 'L1_ffn_Wg': _L1_ffn_in['Wg'], 'L1_ffn_bg': _L1_ffn_in['bg']}

def reference(x, ctx_2048, g_xattn, g_ffn, L0_xattn_theta_w, L0_xattn_theta_b, L0_xattn_phi_w, L0_xattn_phi_b, L0_xattn_g_w, L0_xattn_g_b, L0_xattn_ln_gamma, L0_xattn_ln_beta, L0_xattn_out_w, L0_xattn_out_b, L0_ffn_router_w, L0_ffn_router_bias, L0_ffn_Wu, L0_ffn_Wg, L0_ffn_Wd, L0_ffn_Su, L0_ffn_Sg, L0_ffn_Sd, L1_xattn_gamma, L1_ffn_W1, L1_ffn_b1, L1_ffn_W2, L1_ffn_b2, L1_ffn_W3, L1_ffn_b3, L1_ffn_Wg, L1_ffn_bg):
    import jax
    import jax.numpy as jnp

    def _L0_xattn_ref(input1, input2, theta_w, theta_b, phi_w, phi_b, g_w, g_b, ln_gamma, ln_beta, out_w, out_b):
        import jax, jax.numpy as jnp
        import numpy as np
        B, DIM1, DIM2, LATENT, T = (16, 128, 128, 64, 256)
        LN_EPS = 1e-05
        theta_x = jnp.einsum('ld,bdt->btl', theta_w, input2) + theta_b
        phi_x = jnp.einsum('ld,bdt->blt', phi_w, input1) + phi_b[:, None]
        scores = jnp.einsum('btl,bls->bts', theta_x, phi_x)
        p = jax.nn.softmax(scores, axis=-1)
        g_x = jnp.einsum('ld,bdt->btl', g_w, input1) + g_b
        t_x = jnp.einsum('bts,bsl->blt', p, g_x)
        mu = jnp.mean(t_x, axis=(1, 2), keepdims=True)
        var = jnp.var(t_x, axis=(1, 2), keepdims=True)
        h = (t_x - mu) * jax.lax.rsqrt(var + LN_EPS) * ln_gamma + ln_beta
        h = jax.nn.relu(h)
        w_t = jnp.einsum('ol,blt->bot', out_w, h) + out_b[None, :, None]
        return w_t + input2

    def _L0_ffn_ref(x, router_w, router_bias, Wu, Wg, Wd, Su, Sg, Sd):
        import jax, jax.numpy as jnp
        import numpy as np
        DIM = 256
        EXPERT_DIM = 128
        N_EXPERTS = 16
        TOPK = 2
        N_SHARED = 1
        B, T = (4, 256)
        Bx, Tx, D = x.shape
        flat = x.reshape(Bx * Tx, D)
        logits = flat @ router_w.T
        scores = jax.nn.softmax(logits, axis=-1)
        _, topk_idx = jax.lax.top_k(logits + router_bias, TOPK)
        topk_scores = jnp.take_along_axis(scores, topk_idx, axis=-1)
        topk_scores = topk_scores / topk_scores.sum(-1, keepdims=True)
        combine = jnp.einsum('nk,nke->ne', topk_scores, jax.nn.one_hot(topk_idx, N_EXPERTS, dtype=scores.dtype))
        out = jnp.zeros_like(flat)
        for e in range(N_EXPERTS):
            h = jax.nn.silu(flat @ Wu[e]) * (flat @ Wg[e])
            out = out + combine[:, e:e + 1] * (h @ Wd[e])
        for s in range(N_SHARED):
            out = out + jax.nn.silu(flat @ Su[s]) * (flat @ Sg[s]) @ Sd[s]
        return out.reshape(Bx, Tx, D)

    def _L1_xattn_ref(q, k, v, gamma):
        import jax, jax.numpy as jnp
        import numpy as np
        N_HEAD = 8
        B, Dq, Lq = q.shape
        Dv, Lk = (v.shape[-2], v.shape[-1])
        h = N_HEAD
        dq = Dq // h
        dv = Dv // h
        qh = q.reshape(B, h, dq, Lq)
        kh = k.reshape(B, h, dq, Lk)
        vh = v.reshape(B, h, dv, Lk)
        scale = 1.0 / jnp.sqrt(jnp.asarray(dq, dtype=q.dtype))
        qk = jnp.einsum('bhdq,bhdl->bhql', qh, kh) * scale
        sm = jax.nn.softmax(qk, axis=-1)
        ret = jnp.einsum('bhql,bhdl->bhdq', sm, vh)
        ret = ret.reshape(B, Dv, Lq)
        return gamma * ret

    def _L1_ffn_ref(x, W1, b1, W2, b2, W3, b3, Wg, bg):
        import jax, jax.numpy as jnp
        import numpy as np
        B, S, D = (4, 128, 256)
        H = 512
        NE = 8
        TOPK = 2
        gate_logits = jnp.einsum('bsd,dn->bsn', x, Wg) + bg
        gate_weights = jax.nn.softmax(gate_logits, axis=-1)
        topv, topi = jax.lax.top_k(gate_weights, TOPK)
        h = jax.nn.gelu(jnp.einsum('bsd,ndh->nbsh', x, W1) + b1[:, None, None, :], approximate=False)
        h = jax.nn.gelu(jnp.einsum('nbsh,nhf->nbsf', h, W2) + b2[:, None, None, :], approximate=False)
        eo = jnp.einsum('nbsf,nfd->nbsd', h, W3) + b3[:, None, None, :]
        comb = jnp.sum(jax.nn.one_hot(topi, NE, dtype=x.dtype) * topv[..., None], axis=-2)
        out = jnp.einsum('nbsd,bsn->bsd', eo, comb)
        return out
    x = x + jnp.tanh(g_xattn[0]) * _L0_xattn_ref(_layernorm(x, axis=-1), ctx_2048, L0_xattn_theta_w, L0_xattn_theta_b, L0_xattn_phi_w, L0_xattn_phi_b, L0_xattn_g_w, L0_xattn_g_b, L0_xattn_ln_gamma, L0_xattn_ln_beta, L0_xattn_out_w, L0_xattn_out_b)
    x = x + jnp.tanh(g_ffn[0]) * _L0_ffn_ref(_layernorm(x, axis=-1), L0_ffn_router_w, L0_ffn_router_bias, L0_ffn_Wu, L0_ffn_Wg, L0_ffn_Wd, L0_ffn_Su, L0_ffn_Sg, L0_ffn_Sd)
    x = x + jnp.tanh(g_xattn[1]) * _L1_xattn_ref(_layernorm(x, axis=-1), ctx_2048, ctx_2048, L1_xattn_gamma)
    x = x + jnp.tanh(g_ffn[1]) * _L1_ffn_ref(_layernorm(x, axis=-1), L1_ffn_W1, L1_ffn_b1, L1_ffn_W2, L1_ffn_b2, L1_ffn_W3, L1_ffn_b3, L1_ffn_Wg, L1_ffn_bg)
    return x

_drawn_inputs = setup_inputs


def setup_inputs(seed=0):
    import zlib

    import numpy as np

    out = dict(_drawn_inputs(seed))
    spreads = {'g_ffn': (-1.0, 0.6),
     'L0_xattn_theta_b': (0.0, 0.1),
     'L0_xattn_phi_b': (0.0, 2.0),
     'L0_xattn_g_b': (0.0, 0.1),
     'L0_xattn_ln_gamma': (1.0, 0.2),
     'L0_xattn_ln_beta': (0.0, 0.1),
     'L0_xattn_out_b': (0.0, 0.512),
     'L0_ffn_router_bias': (0.0, 0.8),
     'L1_ffn_b1': (0.0, 2.0),
     'L1_ffn_b2': (0.0, 1.441),
     'L1_ffn_b3': (0.0, 0.8),
     'L1_ffn_bg': (0.0, 1.185)}
    factors = {'L0_ffn_router_w': 8.0,
     'L0_ffn_Wu': 7.527,
     'L0_ffn_Wg': 8.0,
     'L0_ffn_Wd': 8.0,
     'L0_ffn_Su': 4.511,
     'L0_ffn_Sg': 4.511,
     'L0_ffn_Sd': 4.533}
    for name, (base, spread) in spreads.items():
        noise = np.random.default_rng([zlib.crc32(name.encode()), seed]).standard_normal(out[name].shape)
        drawn = base * np.exp(spread * noise) if base else spread * noise
        out[name] = jnp.asarray(drawn.astype(out[name].dtype))
    for name, factor in factors.items():
        out[name] = (out[name] * factor).astype(out[name].dtype)
    return out
```

```python
from contextlib import ExitStack

import numpy as np

import concourse.bass as bass
from concourse import mybir

P = 128
ALU = mybir.AluOpType
ACT = mybir.ActivationFunctionType
AX = mybir.AxisListType.X
F32 = mybir.dt.float32
F32R = mybir.dt.float32r
BF16 = mybir.dt.bfloat16
I32 = mybir.dt.int32
U32 = mybir.dt.uint32
LN_EPS = 1e-5
GA = 4
GC = 2
GE = 4
NLINK = 36


class Links:

    def __init__(self, eng, sems):
        self.eng, self.sems, self.counts = eng, sems, [0] * len(sems)

    def turn(self, g):
        self.g, self.k, self.values = g, 0, {}

    def then(self, ins):
        k, self.k = self.k, self.k + 1
        before = self.counts[k] + 1
        if before not in self.values:
            self.values[before] = self.eng.snap(self.g + before) if not isinstance(self.g, int) else self.g + before
        ins.then_inc(self.sems[k], 1)
        self.eng.wait_ge(self.sems[k], self.values[before])

    def end(self, turns):
        for k in range(self.k):
            self.counts[k] += turns


def flamingo_kernel(nc, x, ctx, g_xattn, g_ffn, theta_wT, theta_b, phi_wT, phi_b, g_wT, g_b, ln_gamma, ln_beta,
                    out_wT, out_b, router_wT, router_bias, Wu0, Wg0, Wd0, Su, Sg, Sd, gamma1,
                    W1, b1, W2, b2, W3, b3, gate_w, gate_b, out):
    B, S, D = x.shape
    LAT = theta_wT.shape[1]
    E0, _, F0 = Wu0.shape
    E1, _, H1 = W1.shape
    KD = D // P
    KH = H1 // P
    TOK = B * S
    CAP = TOK + P
    NT0 = (2 * TOK + E0 * (P - 1)) // P
    NT1 = (2 * TOK + E1 * (P - 1)) // P
    NT0 += NT0 % 2
    NT1 += NT1 % 2
    NGA, NGC, NGE = B // GA, B // GC, B // GE
    NH, DH = 8, S // 8

    x_v = x.rearrange("b p d -> p b d")
    ctx_v = ctx.rearrange("b p d -> p b d")
    out_v = out.rearrange("b p d -> p b d")
    xg0 = nc.dram_tensor("xg0", [E0 * CAP, D], F32, kind="Internal").ap()
    yg0 = nc.dram_tensor("yg0", [NT0 * P, D], F32, kind="Internal").ap()
    xg1 = nc.dram_tensor("xg1", [E1 * CAP, D], F32, kind="Internal").ap()
    yg1 = nc.dram_tensor("yg1", [NT1 * P, D], F32, kind="Internal").ap()
    kscr = nc.dram_tensor("kscr", [2, TOK, D], F32, kind="Internal").ap()
    qscr = nc.dram_tensor("qscr", [2, TOK, D], F32, kind="Internal").ap()

    with ExitStack() as es:
        def sb(name, shape, dt=F32):
            return es.enter_context(nc.sbuf_tensor(name, shape, dt))

        def sem(name):
            return es.enter_context(nc.semaphore(name))

        xs = sb("xs", [P, B, D])
        W1s = sb("W1s", [P, E1, KD, H1])
        W3s = sb("W3s", [P, E1, KH, D])
        with nc.sbuf_tensor("QK", [P, 2, GC * 8 * D], F32R) as QK:
            pass
        R2 = sb("R2", [P, E1 * KH * H1])
        W2s = R2[:, :].rearrange("p (e k h) -> p e k h", e=E1, k=KH)
        n = E0 * KD * F0
        Wug = R2[:, 0:2 * n].rearrange("p (e k a f) -> p e k a f", e=E0, k=KD, a=2)
        Wds = R2[:, 2 * n:3 * n].rearrange("p (e d) -> p e d", e=E0)
        F2 = Su.shape[2]
        m = 3 * n
        Sus = R2[:, m:m + KD * F2].rearrange("p (k f) -> p k f", k=KD)
        Sgs = R2[:, m + KD * F2:m + 2 * KD * F2].rearrange("p (k f) -> p k f", k=KD)
        Sds = R2[:, m + 2 * KD * F2:m + 3 * KD * F2].rearrange("p (k d) -> p k d", k=KD)
        m += 3 * KD * F2
        xl = R2[:, m:m + GA * D].rearrange("p (j d) -> p j d", j=GA)
        m += GA * D
        gS, tx = (R2[:, m + k * GA * 2 * LAT:m + (k + 1) * GA * 2 * LAT].rearrange("p (j c l) -> p j c l", j=GA, c=2) for k in range(2))
        assert m + 2 * GA * 2 * LAT <= E1 * KH * H1
        ident = sb("ident", [P, P])
        ones = sb("ones", [P, P])
        tri_f = sb("tri_f", [P, P])
        tri = sb("tri", [P, P], BF16)
        ones_b = sb("ones_b", [P, P], BF16)
        iota_i = sb("iota_i", [P, 64], I32)
        iota_f = sb("iota_f", [P, 64])
        iota_pi = sb("iota_pi", [P, 1], I32)
        iota_p = sb("iota_p", [P, 1])
        zeros = sb("zeros", [P, D])
        gates = sb("gates", [P, 5])
        tg = sb("tg", [P, 4])
        tgg = sb("tgg", [P, 1])
        thw = sb("thw", [P, LAT])
        phw = sb("phw", [P, LAT])
        gw = sb("gw", [P, LAT])
        thb = sb("thb", [LAT, 1])
        phb = sb("phb", [LAT, 1])
        gb_bc = sb("gb_bc", [P, LAT])
        gbT = sb("gbT", [P, 2, KD, LAT])
        ow = sb("ow", [LAT, P])
        ob = sb("ob", [P, 1])
        rw = sb("rw", [P, KD, E0])
        rb_bc = sb("rb_bc", [P, E0])
        gwt = sb("gwt", [P, KD, E1])
        gbs = sb("gbs", [P, E1])
        b1T = sb("b1T", [P, E1, KH])
        b2T = sb("b2T", [P, E1, KH])
        b3bc = sb("b3bc", [P, E1, D])
        wts = sb("wts", [P, B, 2])
        idxf = sb("idxf", [P, B, 2])
        slotf = sb("slotf", [P, B, 2])
        yslot = sb("yslot", [P, B, 2], U32)
        base = {E0: sb("base0", [P, E0]), E1: sb("base1", [P, E1])}
        cnt = sb("cnt", [P, E0])
        meta = sb("meta", [P, 9, E0])
        tabf = sb("tabf", [P, NT0, 4])
        tab = sb("tab", [1, NT0, 2], I32)
        ztail = sb("ztail", [P, E0], U32)

        cx = sb("cx", [P, GA, D])
        xn = sb("xn", [P, GA, D])
        st6 = sb("st6", [P, GA, 6])
        st2 = sb("st2", [P, GA, 2])
        rstd = sb("rstd", [P, GA])
        veps = sb("veps", [P, GA])
        nhalf = sb("nhalf", [P, GA])
        Q1 = sb("Q1", [P, GA * 2 * D])
        Q2 = sb("Q2", [P, GA * 2 * D])
        xT = sb("xT", [P, KD, GA * P])
        thS = sb("thS", [LAT, GA, D])
        nm = sb("nm", [P, GA, 2])
        rsum = sb("rsum", [P, GA, 2])
        rrec = sb("rrec", [P, GA, 2])
        sums = sb("sums", [P, 2, GA])
        mom = sb("mom", [P, 4, GA])
        lb = sb("lb", [P, GA, E0])
        lmx = sb("lmx", [P, GA])
        ex = sb("ex", [P, GA, E0])
        key = sb("key", [P, GA, E0])
        v8 = sb("v8", [P, GA, 8])
        i8 = sb("i8", [P, GA, 8], U32)
        oh = sb("oh", [P, GA, 2, E0])
        ohx = sb("ohx", [P, GA, 2, E0])
        mask = sb("mask", [P, GA + 1, E0], BF16)
        rk = sb("rk", [P, GA, E0])
        sel = sb("sel", [P, GA, 2])
        den = sb("den", [P, GA])
        slotu = sb("slotu", [P, GA, 2], U32)
        ps = es.enter_context(nc.psum_tensor("ps", [P, 8, 512], F32))

        gam_n = Q1[0:LAT, 0:2 * D].rearrange("p (a d) -> p a d", a=2)
        phS = Q2[0:LAT, 0:GA * D].rearrange("p (j d) -> p j d", j=GA)
        big1 = Q2[:, 2 * GA * P:2 * GA * P + NT0 * E0]
        hS = thS
        txq = gS
        tmp = Q1[:, 0:GA * D].rearrange("p (j d) -> p j d", j=GA)
        hs = Q2[:, 0:2 * GA * P].rearrange("p (f t) -> p f t", f=2)
        Pm = Q1[:, :].rearrange("p (j c s) -> p j c s", j=GA, c=2)
        PTm = Q2[:, :].rearrange("p (j c t) -> p j c t", j=GA, c=2)
        Xin = Q1[:, 0:2 * D].rearrange("p (n d) -> p n d", n=2)
        Yt = Q1[:, 4 * D:6 * D].rearrange("p (n d) -> p n d", n=2)
        XTt = Q2[:, 0:2 * D].rearrange("p (n d) -> p n d", n=2)
        su_t = Q2[:, 2 * D:3 * D].rearrange("p (n d) -> p n d", n=2)
        h0_t = Q2[:, 3 * D:4 * D].rearrange("p (n d) -> p n d", n=2)
        h0T = Q2[:, 4 * D:5 * D].rearrange("p (n d) -> p n d", n=2)
        pre1, pre2 = Q1[:, 2 * D:4 * D], Q1[:, 6 * D:8 * D]
        Ha = Q2[:, 4 * D:6 * D].rearrange("p (k t) -> p k t", k=KH)
        Hb = Q2[:, 6 * D:8 * D].rearrange("p (k t) -> p k t", k=KH)
        NK = 3 * DH
        QS = QK[:, 0, :].rearrange("p (a t) -> p a t", a=GC * NH)
        KS = QK[:, 1, :].rearrange("p (a t) -> p a t", a=GC * NH)
        split = sb("split", [P, 2, GC, D], F32R)
        nmr = sb("nmr", [P, 2, GC * NH * 2], F32R)
        mraw = sb("mraw", [P, GC * NH, 2])
        mT = sb("mT", [2 * GC * NH * 2, P], F32R)
        PTb = Q1[:, 0:2 * 2 * D].rearrange("p (n c q) -> p n c q", n=2, c=2)
        VT = Q2[:, 0:GC * 2 * NH * (DH + 1)].rearrange("p (j c h e) -> p j c h e", j=GC, c=2, h=NH)
        q2 = GC * 2 * NH * (DH + 1)
        oN = Q2[:, q2:q2 + GC * D].rearrange("p (j d) -> p j d", j=GC)
        q2 += GC * D
        orec = Q2[:, q2:q2 + GC * 2 * NH].rearrange("p (j c h) -> p j c h", j=GC, c=2)
        gC = Q1[:, 4 * D:8 * D].rearrange("p (j k d) -> p j k d", j=GC, k=2)
        gE = Q1[:, :].rearrange("p (j k d) -> p j k d", j=GE, k=2)
        idxg = sb("idxg", [P, GE, 2], U32)

        links = [sem(f"vector_step{k}") for k in range(NLINK)]
        names = ("x_loaded ctx_split ctx_split_stored setup_pool setup_dve tanh_done gb_t_ready w0_loaded w1_loaded w2_loaded "
                 "xl_ready theta_ready theta_copied phi_ready phi_copied gt_ready gt_copied "
                 "scores_ready max_ready p_ready pt_ready pt_copied_v pt_copied_a pv_ready sums_ready tot_ready "
                 "h_ready ht_ready ht_copied proj_ready xn_ready xnt_ready xnt_copied logits_ready "
                 "dif_ready ex_ready mask_ready rank_ready slots_ready scattered u_ready silu_ready "
                 "hs_ready y_ready x2_ready tails_ready tails_zeroed table_ready yslots_ready "
                 "tile_loaded0 tile_loaded1 tile_turned tile_copied ug_ready tile_silu tile_h tile_y tile_out tile_stored0 tile_stored1 "
                 "l1_h1_ready l1_h1_copied l1_h1_turned l1_h1_gelu l1_h2_ready l1_h2_copied l1_h2_turned l1_h2_gelu "
                 "tile_ht tile_ht_copied var_ready var_eps rstd_ready alone "
                 "idx_copied gathered gather_used q_ready q_stored q_stacked k_stacked v_loaded vt_ready vt_copied "
                 "s_ready s_max m_ready mt_ready mt_copied m_stacked st_ready st_exp o_ready o_norm ot_ready "
                 "consts_loaded out_summed xn_free pool_a phase_done out_ready out_stored x1_used").split()
        s = {nm_: sem(nm_) for nm_ in names}

        def alone(eng):
            eng.sem_inc(s["alone"], 1)

        blk = es.enter_context(nc.Block())

        def tile_io(sp, nt, xg, yg, before):
            def load(t, b):
                row = sp.value_load(tab[0:1, t, 1:2], min_val=0, max_val=xg.shape[0] - P)
                sp.dma_start(Xin[:, b, :], xg[bass.ds(row, P), :]).then_inc(s[f"tile_loaded{b}"], 16)

            def store(t, b):
                sp.wait_ge(s["tile_out"], before + t + 1)
                alone(sp)
                sp.dma_start(yg[bass.ds(t * P, P), :], Yt[:, b, :]).then_inc(s[f"tile_stored{b}"], 16)

            load(0, 0)
            load(1, 1)
            with sp.Fori(0, (nt - 2) // 2) as i:
                for b in range(2):
                    t = 2 * i + b
                    sp.wait_ge(s["tile_turned"], before + t + 1)
                    alone(sp)
                    load(t + 2, b)
                    store(t, b)
            for b in range(2):
                store(nt - 2 + b, b)

        N_CONST = 17
        @blk.sync
        def _(sp):
            n_c = 0

            def const(dst, src):
                nonlocal n_c
                sp.dma_start(dst, src).then_inc(s["consts_loaded"], 16)
                n_c += 1

            const(gates[:, 0:2], g_xattn.unsqueeze(0).to_broadcast((P, 2)))
            const(gates[:, 2:4], g_ffn.unsqueeze(0).to_broadcast((P, 2)))
            const(gates[:, 4:5], gamma1.to_broadcast((P, 1)))
            const(thw[:], theta_wT)
            const(phw[:], phi_wT)
            const(gw[:], g_wT)
            const(thb[:], theta_b.unsqueeze(1))
            const(phb[:], phi_b.unsqueeze(1))
            const(gb_bc[:], g_b.unsqueeze(0).to_broadcast((P, LAT)))
            const(gam_n[:, 0, :], ln_gamma)
            const(gam_n[:, 1, :], ln_beta)
            const(ow[:], out_wT)
            const(ob[:], out_b.unsqueeze(1))
            const(rw[:], router_wT.rearrange("(k p) e -> p k e", p=P))
            const(rb_bc[:], router_bias.unsqueeze(0).to_broadcast((P, E0)))
            const(gwt[:], gate_w.rearrange("(k p) e -> p k e", p=P))
            const(gbs[:], gate_b.unsqueeze(0).to_broadcast((P, E1)))
            assert n_c == N_CONST
            with sp.Fori(0, NGA) as g:
                sp.dma_start(xs[:, bass.ds(g * GA, GA), :], x_v[:, bass.ds(g * GA, GA), :]).then_inc(s["x_loaded"], 16)
                sp.wait_ge(s["x1_used"], g + 1)
                sp.dma_start(cx[:], ctx_v[:, bass.ds(g * GA, GA), :]).then_inc(s["x_loaded"], 16)
                with_value = (g + 1) * 32
                sp.wait_ge(s["x_loaded"], with_value)
                for c in range(GA // GC):
                    sp.wait_ge(s["ctx_split"], g * (GA // GC) + c + 1)
                    for t in range(2):
                        sp.dma_start(kscr[t, bass.ds(g * GA * P + c * GC * P, GC * P), :].rearrange("(j p) d -> p j d", p=P),
                                     split[:, t, :, :].bitcast(F32)).then_inc(s["ctx_split_stored"], 16)
            sp.wait_ge(s["table_ready"], 1)
            sp.wait_ge(s["tails_zeroed"], 16 * E0)
            sp.wait_ge(s["scattered"], 16 * 2 * B)
            tile_io(sp, NT0, xg0, yg0, 0)
            sp.wait_ge(s["ctx_split_stored"], NGC * 2 * 16)
            with sp.Fori(0, NGC) as g:
                rows = bass.ds(g * GC * P, GC * P)
                sp.wait_ge(s["q_ready"], g + 1)
                for t in range(2):
                    sp.dma_start(qscr[t, rows, :].rearrange("(j p) d -> p j d", p=P), split[:, t, :, :].bitcast(F32)).then_inc(s["q_stored"], 16)
                sp.dma_start(cx[:, 0:GC, :], ctx_v[:, bass.ds(g * GC, GC), :]).then_inc(s["v_loaded"], 16)
                for i, t in enumerate((0, 1, 0)):
                    sp.dma_start(KS[i * DH:(i + 1) * DH, :, :].bitcast(F32), kscr[t, rows, :].rearrange("(a d) t -> d a t", d=DH)).then_inc(s["k_stacked"], 16)
                sp.wait_ge(s["q_stored"], (g + 1) * 32)
                for i, t in enumerate((0, 0, 1)):
                    sp.dma_start(QS[i * DH:(i + 1) * DH, :, :].bitcast(F32), qscr[t, rows, :].rearrange("(a d) t -> d a t", d=DH)).then_inc(s["q_stacked"], 16)
                sp.wait_ge(s["mt_copied"], g + 1)
                for t in range(2):
                    half = GC * NH * 2
                    sp.dma_start(QS[NK + t:NK + t + 1, :, :].rearrange("o a (c q) -> o (a c) q", c=2).bitcast(F32),
                                 mT[t * half:(t + 1) * half, :].bitcast(F32)).then_inc(s["m_stacked"], 16)
            sp.wait_ge(s["table_ready"], 2)
            sp.wait_ge(s["tails_zeroed"], 16 * (E0 + E1))
            sp.wait_ge(s["scattered"], 16 * 4 * B)
            tile_io(sp, NT1, xg1, yg1, NT0)
            with sp.Fori(0, NGE) as g:
                sp.wait_ge(s["out_ready"], g + 1)
                sp.dma_start(out_v[:, bass.ds(g * GE, GE), :], xs[:, bass.ds(g * GE, GE), :]).then_inc(s["out_stored"], 16)
            sp.wait_ge(s["out_stored"], NGE * 16)

        @blk.gpsimd
        def _(pool):
            nc.gpsimd.memset(ones[:], 1.0).then_inc(s["pool_a"], 1)
            nc.gpsimd.memset(ident[:], 0.0).then_inc(s["pool_a"], 1)
            nc.gpsimd.memset(zeros[:], 0.0).then_inc(s["pool_a"], 1)
            nc.gpsimd.memset(nhalf[:], -0.5).then_inc(s["pool_a"], 1)
            nc.gpsimd.iota(iota_i[:], pattern=[[1, 64]], base=0, channel_multiplier=0).then_inc(s["pool_a"], 1)
            nc.gpsimd.iota(iota_pi[:], pattern=[[0, 1]], base=0, channel_multiplier=1).then_inc(s["pool_a"], 1)
            pool.wait_ge(s["pool_a"], 6)
            nc.gpsimd.affine_select(out=ident[:], in_=ident[:], compare_op=ALU.not_equal, fill=1.0, base=0,
                                    pattern=[[-1, P]], channel_multiplier=1).then_inc(s["setup_pool"], 1)
            nc.gpsimd.affine_select(out=tri_f[:], in_=ones[:], compare_op=ALU.is_gt, fill=0.0, base=0,
                                    pattern=[[1, P]], channel_multiplier=-1).then_inc(s["setup_pool"], 1)
            for dst, src in ((Sus, Su[0].rearrange("(k p) f -> p k f", p=P)), (Sgs, Sg[0].rearrange("(k p) f -> p k f", p=P)),
                             (Sds, Sd[0].rearrange("(k p) d -> p k d", p=P)),
                             (Wug[:, :, 0, 0, :], Wu0[:, 0:P, :].rearrange("e p f -> p e f")),
                             (Wug[:, :, 1, 0, :], Wu0[:, P:2 * P, :].rearrange("e p f -> p e f")),
                             (Wug[:, :, 0, 1, :], Wg0[:, 0:P, :].rearrange("e p f -> p e f")),
                             (Wug[:, :, 1, 1, :], Wg0[:, P:2 * P, :].rearrange("e p f -> p e f")),
                             (Wds, Wd0.rearrange("e f d -> f e d"))):
                pool.dma_start(dst, src).then_inc(s["w0_loaded"], 16)
            for dst, src in ((b1T[:], b1), (b2T[:], b2),
                             (b3bc[:], b3.unsqueeze(0).to_broadcast((P, E1, D)))):
                pool.dma_start(dst, src).then_inc(s["w1_loaded"], 16)
            for e in range(E1):
                pool.dma_start(W1s[:, e], W1[e].rearrange("(k p) h -> p k h", p=P)).then_inc(s["w1_loaded"], 16)
                pool.dma_start(W3s[:, e], W3[e].rearrange("(k p) d -> p k d", p=P)).then_inc(s["w1_loaded"], 16)

            def root(n, src, turn):
                pool.wait_ge(s["var_ready"], turn)
                alone(pool)
                dst = mom[:, 2, :] if src is None else rstd[:, 0:n]
                nc.gpsimd.tensor_scalar(veps[:, 0:n], mom[:, 3, :] if src is None else src, LN_EPS, None, ALU.add).then_inc(s["var_eps"], 1)
                pool.wait_ge(s["var_eps"], turn)
                nc.gpsimd.tensor_tensor(dst, veps[:, 0:n], nhalf[:, 0:n], ALU.pow).then_inc(s["rstd_ready"], 1)

            def scatter(turn, n, xg, total):
                pool.wait_ge(s["slots_ready"], turn)
                alone(pool)
                for j in range(n):
                    for k in range(2):
                        pool.indirect_dma_start(xg[:, :], bass.IndirectOffsetOnAxis(ap=slotu[:, j, k:k + 1], axis=0),
                                                xn[:, j, :], None).then_inc(s["scattered"], 16)
                pool.wait_ge(s["scattered"], total)
                pool.sem_inc(s["xn_free"], 1)

            def zero_tails(turn, E, xg):
                pool.wait_ge(s["tails_ready"], turn)
                for e in range(E):
                    pool.indirect_dma_start(xg[:, :], bass.IndirectOffsetOnAxis(ap=ztail[:, e:e + 1], axis=0),
                                            zeros[:, :], None).then_inc(s["tails_zeroed"], 16)

            def gather(g, n, yg, turn, buf):
                pool.wait_ge(s["gather_used"], turn)
                nc.gpsimd.tensor_copy(idxg[:, 0:n, :], yslot[:, bass.ds(g * n, n), :]).then_inc(s["idx_copied"], 1)
                pool.wait_ge(s["idx_copied"], turn)
                alone(pool)
                for j in range(n):
                    for k in range(2):
                        pool.indirect_dma_start(buf[:, j, k, :], None, yg[:, :],
                                                bass.IndirectOffsetOnAxis(ap=idxg[:, j, k:k + 1], axis=0)).then_inc(s["gathered"], 16)

            pool.sem_inc(s["xn_free"], 1)
            with pool.Fori(0, NGA) as g:
                root(GA, st2[:, 0:GA, 1], 3 * g + 1)
                root(GA, None, 3 * g + 2)
                root(GA, st2[:, 0:GA, 1], 3 * g + 3)
                scatter(pool.snap(g + 1), GA, xg0, (g + 1) * (GA * 2 * 16))
            zero_tails(1, E0, xg0)
            for b in range(2):
                pool.wait_ge(s[f"tile_stored{b}"], NT0 // 2 * 16)
            pool.wait_ge(s["yslots_ready"], 1)
            with pool.Fori(0, NGC) as g:
                gather(g, GC, yg0, pool.snap(g + 1), gC)
                root(GC, st2[:, 0:GC, 1], 2 * g + (3 * NGA + 1))
                root(GC, st2[:, 0:GC, 1], 2 * g + (3 * NGA + 2))
                scatter(pool.snap(g + (NGA + 1)), GC, xg1, (g + 1) * (GC * 2 * 16) + 2 * B * 16)
            zero_tails(2, E1, xg1)
            pool.wait_ge(s["ot_ready"], NGC)
            for e in range(E1):
                pool.dma_start(W2s[:, e], W2[e].rearrange("(k p) h -> p k h", p=P)).then_inc(s["w2_loaded"], 16)
                pool.wait_ge(s["w2_loaded"], 16 * (e + 1))
            for b in range(2):
                pool.wait_ge(s[f"tile_stored{b}"], (NT0 + NT1) // 2 * 16)
            pool.wait_ge(s["yslots_ready"], 2)
            with pool.Fori(0, NGE) as g:
                gather(g, GE, yg1, pool.snap(g + (NGC + 1)), gE)

        @blk.vector
        def _(dve):
            v = nc.vector

            def layernorm(lk, src, dst, n, turn):
                alone(dve)
                for j in range(n):
                    i = v.bn_stats(st6[:, j, :], src[:, j, :])
                lk.then(i)
                alone(dve)
                for j in range(n):
                    i = v.bn_aggr(st2[:, j, :], st6[:, j, :])
                i.then_inc(s["var_ready"], 1)
                dve.wait_ge(s["rstd_ready"], turn)
                for j in range(n):
                    i = v.tensor_scalar(dst[:, j, :], src[:, j, :], st2[:, j, 0:1], rstd[:, j:j + 1], ALU.subtract, ALU.mult)
                return i

            def route(lk, g, n, E, turn, value, psR, psK):
                l_, k_, e_ = lb[:, 0:n, 0:E], key[:, 0:n, 0:E], ex[:, 0:n, 0:E]
                o_, ox = oh[:, 0:n, :, 0:E], ohx[:, 0:n, :, 0:E]
                bias = rb_bc if E == E0 else gbs
                dve.wait_ge(s["logits_ready"], turn)
                lk.then(v.tensor_tensor(l_, psR, bias[:, 0:E].unsqueeze(1).to_broadcast((P, n, E)), ALU.add))
                lg = psR if E == E0 else l_
                lk.then(v.tensor_reduce(lmx[:, 0:n], lg, AX, ALU.max))
                v.tensor_tensor(e_, lg, lmx[:, 0:n].unsqueeze(2).to_broadcast((P, n, E)), ALU.subtract).then_inc(s["dif_ready"], 1)
                if E == E1:
                    dve.wait_ge(s["ex_ready"], turn)
                    lk.then(v.tensor_reduce(den[:, 0:n], e_, AX, ALU.add))
                    lk.then(v.reciprocal(den[:, 0:n], den[:, 0:n]))
                    lk.then(v.tensor_tensor(k_, e_, den[:, 0:n].unsqueeze(2).to_broadcast((P, n, E)), ALU.mult))
                kk = l_ if E == E0 else k_
                alone(dve)
                for j in range(n):
                    i = v.max(v8[:, j, :], kk[:, j, :])
                lk.then(i)
                alone(dve)
                for j in range(n):
                    i = v.max_index(i8[:, j, :], v8[:, j, :], kk[:, j, :])
                lk.then(i)
                ig = idxf[:, bass.ds(g * n, n), :]
                alone(dve)
                lk.then(v.tensor_copy(ig, i8[:, 0:n, 0:2]))
                lk.then(v.tensor_tensor(o_, iota_f[:, 0:E].unsqueeze(1).unsqueeze(1).to_broadcast((P, n, 2, E)),
                                        ig.unsqueeze(3).to_broadcast((P, n, 2, E)), ALU.is_equal))
                v.tensor_tensor(mask[:, 0:n, 0:E], o_[:, :, 0, :], o_[:, :, 1, :], ALU.add).then_inc(s["mask_ready"], 1)
                if E == E0:
                    dve.wait_ge(s["ex_ready"], turn)
                w = e_ if E == E0 else k_
                lk.then(v.tensor_tensor(ox, o_, w.unsqueeze(2).to_broadcast((P, n, 2, E)), ALU.mult))
                lk.then(v.tensor_reduce(sel[:, 0:n, :], ox, AX, ALU.add))
                wg_ = wts[:, bass.ds(g * n, n), :]
                if E == E0:
                    lk.then(v.tensor_tensor(den[:, 0:n], sel[:, 0:n, 0], sel[:, 0:n, 1], ALU.add))
                    lk.then(v.reciprocal(den[:, 0:n], den[:, 0:n]))
                    lk.then(v.tensor_tensor(sel[:, 0:n, :], sel[:, 0:n, :], den[:, 0:n].unsqueeze(2).to_broadcast((P, n, 2)), ALU.mult))
                lk.then(v.tensor_scalar(wg_, sel[:, 0:n, :], tg[:, (2 if E == E0 else 3):(3 if E == E0 else 4)], None, ALU.mult))
                dve.wait_ge(s["rank_ready"], turn)
                c_ = cnt[:, 0:E]
                lk.then(v.tensor_tensor(rk[:, 0:n, 0:E], psK[:, 0:n, :], c_.unsqueeze(1).to_broadcast((P, n, E)), ALU.add))
                lk.then(v.tensor_tensor(c_, psK[:, n, :], c_, ALU.add))
                lk.then(v.tensor_tensor(ox, o_, rk[:, 0:n, 0:E].unsqueeze(2).to_broadcast((P, n, 2, E)), ALU.mult))
                sg = slotf[:, bass.ds(g * n, n), :]
                lk.then(v.tensor_reduce(sg, ox, AX, ALU.add))
                alone(dve)
                v.tensor_copy(slotu[:, 0:n, :], sg).then_inc(s["slots_ready"], 1)

            def tables(lk, E, NT):
                c_ = cnt[:, 0:E]
                v.tensor_scalar(ztail[:, 0:E], c_, iota_p[:, 0:1], None, ALU.add).then_inc(s["tails_ready"], 1)
                n_e, nt, end, off, dlt = (meta[:, k, 0:E] for k in range(5))
                lk.then(v.tensor_tensor(n_e, c_, base[E][:], ALU.subtract))
                NJ = TOK // P
                cmp = big1[:, 0:E * NJ].rearrange("p (e j) -> p e j", e=E)
                lk.then(v.tensor_scalar(tabf[:, 0:NJ, 0], iota_f[:, 0:NJ], float(P), None, ALU.mult))
                lk.then(v.tensor_tensor(cmp, n_e.unsqueeze(2).to_broadcast((P, E, NJ)),
                                        tabf[:, 0:NJ, 0].unsqueeze(1).to_broadcast((P, E, NJ)), ALU.is_gt))
                lk.then(v.tensor_reduce(nt, cmp, AX, ALU.add))
                le = big1[:, 0:E * E].rearrange("p (e f) -> p e f", e=E)
                lk.then(v.tensor_tensor(le, iota_f[:, 0:E].unsqueeze(2).to_broadcast((P, E, E)),
                                        iota_f[:, 0:E].unsqueeze(1).to_broadcast((P, E, E)), ALU.is_ge))
                lk.then(v.tensor_tensor(le, le, nt.unsqueeze(1).to_broadcast((P, E, E)), ALU.mult))
                lk.then(v.tensor_reduce(end, le, AX, ALU.add))
                lk.then(v.tensor_tensor(off, end, nt, ALU.subtract))
                ge = big1[:, 0:NT * E].rearrange("p (t e) -> p t e", e=E)
                lk.then(v.tensor_tensor(ge, iota_f[:, 0:NT].unsqueeze(2).to_broadcast((P, NT, E)),
                                        end.unsqueeze(1).to_broadcast((P, NT, E)), ALU.is_ge))
                lk.then(v.tensor_reduce(tabf[:, 0:NT, 0], ge, AX, ALU.add))
                lk.then(v.tensor_scalar(tabf[:, 0:NT, 0], tabf[:, 0:NT, 0], float(E - 1), None, ALU.min))
                lk.then(v.tensor_tensor(ge, ge, nt.unsqueeze(1).to_broadcast((P, NT, E)), ALU.mult))
                lk.then(v.tensor_reduce(tabf[:, 0:NT, 1], ge, AX, ALU.add))
                lk.then(v.tensor_tensor(tabf[:, 0:NT, 1], iota_f[:, 0:NT], tabf[:, 0:NT, 1], ALU.subtract))
                lk.then(v.tensor_scalar(tabf[:, 0:NT, 2], iota_f[:, 0:NT], end[:, E - 1:E], float(P), ALU.is_lt, ALU.mult))
                lk.then(v.tensor_tensor(tabf[:, 0:NT, 1], tabf[:, 0:NT, 1], tabf[:, 0:NT, 2], ALU.mult))
                lk.then(v.scalar_tensor_tensor(tabf[:, 0:NT, 1], tabf[:, 0:NT, 0], float(CAP), tabf[:, 0:NT, 1], ALU.mult, ALU.add))
                lk.then(v.scalar_tensor_tensor(dlt, off, float(P), base[E][:], ALU.mult, ALU.subtract))
                v.tensor_copy(tab[0:1, 0:NT, :], tabf[0:1, 0:NT, 0:2]).then_inc(s["table_ready"], 1)
                bo = big1[:, 0:B * 2 * E].rearrange("p (b k e) -> p b k e", b=B, k=2)
                lk.then(v.tensor_tensor(bo, iota_f[:, 0:E].unsqueeze(1).unsqueeze(1).to_broadcast((P, B, 2, E)),
                                        idxf[:].unsqueeze(3).to_broadcast((P, B, 2, E)), ALU.is_equal))
                lk.then(v.tensor_tensor(bo, bo, dlt.unsqueeze(1).unsqueeze(1).to_broadcast((P, B, 2, E)), ALU.mult))
                lk.then(v.tensor_reduce(idxf[:], bo, AX, ALU.add))
                lk.then(v.tensor_tensor(slotf[:], slotf[:], idxf[:], ALU.add))
                v.tensor_copy(yslot[:], slotf[:]).then_inc(s["yslots_ready"], 1)

            dve.wait_ge(s["setup_pool"], 2)
            v.tensor_copy(tri[:], tri_f[:]).then_inc(s["setup_dve"], 1)
            v.tensor_copy(ones_b[:], ones[:]).then_inc(s["setup_dve"], 1)
            v.tensor_copy(iota_f[:], iota_i[:]).then_inc(s["setup_dve"], 1)
            v.tensor_copy(iota_p[:], iota_pi[:]).then_inc(s["setup_dve"], 1)
            dve.wait_ge(s["setup_dve"], 4)
            v.tensor_scalar(base[E0][:], iota_f[:, 0:E0], float(CAP), None, ALU.mult).then_inc(s["setup_dve"], 1)
            v.tensor_scalar(base[E1][:], iota_f[:, 0:E1], float(CAP), None, ALU.mult).then_inc(s["setup_dve"], 1)
            dve.wait_ge(s["setup_dve"], 6)
            v.tensor_copy(cnt[:], base[E0][:]).then_inc(s["setup_dve"], 1)
            dve.wait_ge(s["gb_t_ready"], 1)
            v.tensor_copy(gbT[:], ps[:, 7, 0:4 * LAT].rearrange("p (a c l) -> p a c l", a=2, c=KD)).then_inc(s["setup_dve"], 1)
            dve.wait_ge(s["tanh_done"], 1)
            v.tensor_tensor(tgg[:], tg[:, 1:2], gates[:, 4:5], ALU.mult).then_inc(s["setup_dve"], 1)
            v.memset(mask[:], 0.0).then_inc(s["setup_dve"], 1)
            dve.wait_ge(s["setup_dve"], 10)
            dve.sem_inc(s["x1_used"], 1)
            dve.sem_inc(s["gather_used"], 1)
            dve.sem_inc(s["x2_ready"], 1)
            lk = Links(dve, links)
            with dve.Fori(0, NGA) as g:
                t1 = dve.snap(g + 1)
                lk.turn(g)
                X = xs[:, bass.ds(g * GA, GA), :]
                dve.wait_ge(s["x_loaded"], dve.snap((g + 1) * 32))
                layernorm(lk, X, xl, GA, 3 * g + 1).then_inc(s["xl_ready"], 1)
                for c in range(GA // GC):
                    hi, lo, src = split[:, 0, :, :], split[:, 1, :, :], cx[:, c * GC:(c + 1) * GC, :]
                    lk.then(v.tensor_copy(hi, src))
                    v.tensor_tensor(lo, src, hi.bitcast(F32), ALU.subtract).then_inc(s["ctx_split"], 1)
                    dve.wait_ge(s["ctx_split_stored"], (g * (GA // GC) + c + 1) * 32)
                dve.wait_ge(s["phi_ready"], t1)
                v.tensor_scalar(phS[:], ps[0:LAT, 2:4, :].rearrange("p n (j d) -> p (n j) d", d=D), phb[:, 0:1], None, ALU.add).then_inc(s["phi_copied"], 1)
                dve.wait_ge(s["gt_ready"], t1)
                v.tensor_tensor(gS[:].rearrange("p j c l -> p (j c) l"), ps[:, 4, :].rearrange("p (n l) -> p n l", l=LAT),
                                gb_bc[:].unsqueeze(1).to_broadcast((P, GA * 2, LAT)), ALU.add).then_inc(s["gt_copied"], 1)
                for j in range(GA):
                    dve.wait_ge(s["scores_ready"], g * GA + (j + 1))
                    v.tensor_reduce(nm[:, j, :], ps[:, j, :].rearrange("p (c s) -> p c s", c=2), AX, ALU.max, negate=True).then_inc(s["max_ready"], 1)
                for j in range(0, GA, 2):
                    dve.wait_ge(s["pt_ready"], g * GA + (j + 1))
                    v.tensor_copy(Q2[:, j * 2 * D:(j + 1) * 2 * D], ps[:, j, :]).then_inc(s["pt_copied_v"], 1)
                dve.wait_ge(s["p_ready"], (g + 1) * GA * 2)
                lk.then(v.reciprocal(rrec[:], rsum[:]))
                dve.wait_ge(s["pv_ready"], t1)
                lk.then(v.tensor_tensor(tx[:], ps[:, 4, :].rearrange("p (j c l) -> p j c l", j=GA, c=2),
                                        rrec[:].unsqueeze(3).to_broadcast((P, GA, 2, LAT)), ALU.mult))
                v.tensor_reduce(sums[:, 0, :], tx[:].rearrange("p j c l -> p j (c l)"), AX, ALU.add)
                lk.then(v.tensor_tensor(txq[:], tx[:], tx[:], ALU.mult))
                v.tensor_reduce(sums[:, 1, :], txq[:].rearrange("p j c l -> p j (c l)"), AX, ALU.add).then_inc(s["sums_ready"], 1)
                dve.wait_ge(s["tot_ready"], t1)
                inv = 1.0 / (LAT * D)
                lk.then(v.tensor_scalar(mom[:, 0:2, :], ps[:, 5, 0:2 * GA].rearrange("p (a j) -> p a j", a=2), inv, None, ALU.mult))
                lk.then(v.tensor_tensor(mom[:, 2, :], mom[:, 0, :], mom[:, 0, :], ALU.mult))
                v.tensor_tensor(mom[:, 3, :], mom[:, 1, :], mom[:, 2, :], ALU.subtract).then_inc(s["var_ready"], 1)
                dve.wait_ge(s["rstd_ready"], 3 * g + 2)
                for j in range(GA):
                    i = v.tensor_scalar(tx[:, j, :, :], tx[:, j, :, :], mom[:, 0, j:j + 1], mom[:, 2, j:j + 1], ALU.subtract, ALU.mult)
                lk.then(i)
                lk.then(v.tensor_tensor(tx[:], tx[:], gbT[:, 0, :, :].unsqueeze(1).to_broadcast((P, GA, KD, LAT)), ALU.mult))
                v.tensor_tensor(tx[:], tx[:], gbT[:, 1, :, :].unsqueeze(1).to_broadcast((P, GA, KD, LAT)), ALU.add).then_inc(s["h_ready"], 1)
                dve.wait_ge(s["proj_ready"], t1)
                lk.then(v.scalar_tensor_tensor(tmp[:], ps[:, 0:2, :].rearrange("p n (j d) -> p (n j) d", d=D), ob[:, 0:1], cx[:], ALU.add, ALU.add))
                lk.then(v.scalar_tensor_tensor(X, tmp[:], tg[:, 0:1], X, ALU.mult, ALU.add))
                dve.sem_inc(s["x1_used"], 1)
                dve.wait_ge(s["xn_free"], t1)
                layernorm(lk, X, xn, GA, 3 * g + 3).then_inc(s["xn_ready"], 1)
                route(lk, g, GA, E0, t1, t1, ps[:, 4, 0:GA * E0].rearrange("p (j e) -> p j e", e=E0),
                      ps[:, 5, 0:(GA + 1) * E0].rearrange("p (j e) -> p j e", e=E0))
                for f in range(2):
                    dve.wait_ge(s["silu_ready"], 2 * g + (f + 1))
                    v.tensor_tensor(hs[:, f, :], hs[:, f, :], ps[:, 6 + f, :], ALU.mult).then_inc(s["hs_ready"], 1)
                dve.wait_ge(s["y_ready"], t1)
                lk.then(v.scalar_tensor_tensor(X, ps[:, 2:4, :].rearrange("p n (j d) -> p (n j) d", d=D), tg[:, 2:3], X, ALU.mult, ALU.add))
                dve.sem_inc(s["x2_ready"], 1)
            lk.end(NGA)
            lk.turn(0)
            tables(lk, E0, NT0)
            lk.end(1)

            def b_copy(t, b):
                dve.wait_ge(s["tile_turned"], t + 1)
                v.tensor_copy(XTt[:, b, :], ps[:, b, 0:D]).then_inc(s["tile_copied"], 1)

            def b_h(t, b):
                dve.wait_ge(s["tile_silu"], t + 1)
                v.tensor_tensor(h0_t[:, b, :], su_t[:, b, :], ps[:, 2 + b, P:2 * P], ALU.mult).then_inc(s["tile_h"], 1)

            b_copy(0, 0)
            b_copy(1, 1)
            b_h(0, 0)
            with dve.Fori(0, (NT0 - 2) // 2) as i:
                for k in range(2):
                    b_copy(2 * i + (k + 2), k)
                    b_h(2 * i + (k + 1), 1 - k)
            b_h(NT0 - 1, 1)

            v.tensor_copy(cnt[:, 0:E1], base[E1][:]).then_inc(s["setup_dve"], 1)
            v.memset(mask[:], 0.0).then_inc(s["setup_dve"], 1)
            v.memset(Q2[:, 0:GC * 2 * NH * (DH + 1)], 1.0).then_inc(s["setup_dve"], 1)
            v.memset(QK[:, 1, :].bitcast(F32), 1.0).then_inc(s["setup_dve"], 1)
            dve.wait_ge(s["setup_dve"], 14)
            dve.sem_inc(s["phase_done"], 1)
            with dve.Fori(0, NGC) as g:
                t1 = dve.snap(g + 1)
                lk.turn(g)
                X = xs[:, bass.ds(g * GC, GC), :]
                dve.wait_ge(s["gathered"], (g + 1) * (GC * 2 * 16))
                for k in range(2):
                    for j in range(GC):
                        i = v.scalar_tensor_tensor(xs[:, bass.ds(g * GC + j, 1), :].rearrange("p a d -> p (a d)"), gC[:, j, k, :],
                                                   wts[:, bass.ds(g * GC + j, 1), k:k + 1].rearrange("p a d -> p (a d)"),
                                                   xs[:, bass.ds(g * GC + j, 1), :].rearrange("p a d -> p (a d)"), ALU.mult, ALU.add)
                    lk.then(i)
                dve.sem_inc(s["gather_used"], 1)
                lk.then(layernorm(lk, X, xl, GC, 2 * g + (3 * NGA + 1)))
                lk.then(v.tensor_copy(split[:, 0, :, :], xl[:, 0:GC, :]))
                v.tensor_tensor(split[:, 1, :, :], xl[:, 0:GC, :], split[:, 0, :, :].bitcast(F32), ALU.subtract).then_inc(s["q_ready"], 1)
                dve.wait_ge(s["vt_ready"], t1)
                v.tensor_copy(VT[:, :, :, :, 0:DH], ps[:, 6, :].rearrange("p (j c h d) -> p j c h d", j=GC, c=2, h=NH)).then_inc(s["vt_copied"], 1)
                for a in range(GC * NH):
                    dve.wait_ge(s["s_ready"], g * (GC * NH) + (a + 1))
                    i = v.tensor_reduce(mraw[:, a, :], ps[:, a % 2, :].rearrange("p (c l) -> p c l", c=2), AX, ALU.max)
                    i.then_inc(s["s_max"], 1)
                dve.wait_ge(s["s_max"], (g + 1) * (GC * NH))
                mr = mraw[:].rearrange("p a c -> p (a c)")
                lk.then(v.tensor_scalar(nmr[:, 0, :], mr, -1.0, None, ALU.mult))
                v.scalar_tensor_tensor(nmr[:, 1, :], mr, -1.0, nmr[:, 0, :].bitcast(F32), ALU.mult, ALU.subtract).then_inc(s["m_ready"], 1)
                dve.wait_ge(s["mt_ready"], t1)
                v.tensor_copy(mT[:], ps[0:2 * GC * NH * 2, 7, 0:P]).then_inc(s["mt_copied"], 1)
                for j in range(GC):
                    dve.wait_ge(s["o_ready"], g * GC + (j + 1))
                    o5 = ps[:, 4 + j, 0:2 * NH * (DH + 1)].rearrange("p (c h e) -> p c h e", c=2, h=NH)
                    lk.then(v.reciprocal(orec[:, j], o5[:, :, :, DH]))
                    v.tensor_tensor(oN[:, j, :].rearrange("p (c h d) -> p c h d", c=2, h=NH), o5[:, :, :, 0:DH],
                                    orec[:, j].unsqueeze(3).to_broadcast((P, 2, NH, DH)), ALU.mult).then_inc(s["o_norm"], 1)
                dve.wait_ge(s["ot_ready"], t1)
                lk.then(v.scalar_tensor_tensor(X, ps[:, 6, :].rearrange("p (j q) -> p j q", j=GC), tgg[:, 0:1], X, ALU.mult, ALU.add))
                dve.wait_ge(s["xn_free"], g + (NGA + 1))
                layernorm(lk, X, xn, GC, 2 * g + (3 * NGA + 2)).then_inc(s["xn_ready"], 1)
                route(lk, g, GC, E1, dve.snap(g + (NGA + 1)), None, ps[:, 7, 0:GC * E1].rearrange("p (j e) -> p j e", e=E1),
                      ps[:, 5, 0:(GC + 1) * E1].rearrange("p (j e) -> p j e", e=E1))
            lk.end(NGC)
            lk.turn(0)
            tables(lk, E1, NT1)

            def d_copy(t, b):
                dve.wait_ge(s["tile_turned"], NT0 + t + 1)
                v.tensor_copy(XTt[:, b, :], ps[:, b, 0:D]).then_inc(s["tile_copied"], 1)

            def d_out(t, b, i):
                e = dve.value_load(tab[0:1, t, 0:1], min_val=0, max_val=E1 - 1)
                dve.wait_ge(s["tile_y"], NT0 + t + 1)
                dve.wait_ge(s[f"tile_stored{b}"], (NT0 // 2 + i) * 16)
                v.tensor_tensor(Yt[:, b, :], ps[:, 6 + b, 0:D], b3bc[:, bass.ds(e, 1), :].rearrange("p a d -> p (a d)"), ALU.add).then_inc(s["tile_out"], 1)

            dve.wait_ge(s["w1_loaded"], 16 * (3 + 2 * E1))
            def d_pre(t, which):
                pre, bank = (pre1, 2) if which == 1 else (pre2, 4)
                dve.wait_ge(s[f"l1_h{which}_ready"], t + 1)
                v.tensor_copy(pre, ps[:, bank, :]).then_inc(s[f"l1_h{which}_copied"], 1)

            d_copy(0, 0)
            d_copy(1, 1)
            d_pre(0, 1)
            with dve.Fori(0, NT1 // 2 - 1) as i:
                for k in range(2):
                    d_pre(2 * i + k, 2)
                    d_pre(2 * i + (k + 1), 1)
                    d_copy(2 * i + (k + 2), k)
                    d_out(2 * i + k, k, i)
            d_pre(NT1 - 2, 2)
            d_pre(NT1 - 1, 1)
            d_out(NT1 - 2, 0, NT1 // 2 - 1)
            d_pre(NT1 - 1, 2)
            d_out(NT1 - 1, 1, NT1 // 2 - 1)

            with dve.Fori(0, NGE) as g:
                dve.wait_ge(s["gathered"], g * (GE * 2 * 16) + (2 * B * 16 + GE * 2 * 16))
                for k in range(2):
                    for j in range(GE):
                        xj = xs[:, bass.ds(g * GE + j, 1), :].rearrange("p a d -> p (a d)")
                        i = v.scalar_tensor_tensor(xj, gE[:, j, k, :], wts[:, bass.ds(g * GE + j, 1), k:k + 1].rearrange("p a d -> p (a d)"),
                                                   xj, ALU.mult, ALU.add)
                    i.then_inc(s["out_summed"], 1)
                    dve.wait_ge(s["out_summed"], 2 * g + (k + 1))
                dve.sem_inc(s["gather_used"], 1)
                dve.sem_inc(s["out_ready"], 1)

        @blk.scalar
        def _(act):
            a = nc.scalar
            act.wait_ge(s["consts_loaded"], 16 * N_CONST)
            a.activation(tg[:], gates[:, 0:4], ACT.Tanh).then_inc(s["tanh_done"], 1)

            def routing_side(n, E, turn):
                act.wait_ge(s["xnt_ready"], turn)
                if E == E0:
                    a.copy(xT[:], ps[:, 2:4, :]).then_inc(s["xnt_copied"], 1)
                else:
                    a.copy(xT[:, :, 0:n * P], ps[:, 6, :].rearrange("p (k t) -> p k t", k=KD)).then_inc(s["xnt_copied"], 1)
                act.wait_ge(s["dif_ready"], turn)
                a.activation(ex[:, 0:n, 0:E], ex[:, 0:n, 0:E], ACT.Exp).then_inc(s["ex_ready"], 1)

            with act.Fori(0, NGA) as g:
                t1 = act.snap(g + 1)
                act.wait_ge(s["theta_ready"], t1)
                a.activation(thS[:], ps[0:LAT, 0:2, :].rearrange("p n (j d) -> p (n j) d", d=D), ACT.Identity, bias=thb[:, 0:1]).then_inc(s["theta_copied"], 1)
                for j in range(GA):
                    act.wait_ge(s["max_ready"], g * GA + (j + 1))
                    for c in range(2):
                        a.activation(Pm[:, j, c, :], ps[:, j, c * D:(c + 1) * D], ACT.Exp, bias=nm[:, j, c:c + 1],
                                     accum_out=rsum[:, j, c:c + 1]).then_inc(s["p_ready"], 1)
                for j in range(1, GA, 2):
                    act.wait_ge(s["pt_ready"], g * GA + (j + 1))
                    a.copy(PTm[:, j].rearrange("p c t -> p (c t)"), ps[:, j, :]).then_inc(s["pt_copied_a"], 1)
                act.wait_ge(s["ht_ready"], t1)
                a.activation(hS[:], ps[0:LAT, 6:8, :].rearrange("p n (j d) -> p (n j) d", d=D), ACT.Relu).then_inc(s["ht_copied"], 1)
                routing_side(GA, E0, t1)
                for f in range(2):
                    act.wait_ge(s["u_ready"], 2 * g + (f + 1))
                    a.activation(hs[:, f, :], ps[:, f, :], ACT.Silu).then_inc(s["silu_ready"], 1)

            def silu(t, b):
                act.wait_ge(s["ug_ready"], t + 1)
                a.activation(su_t[:, b, :], ps[:, 2 + b, 0:P], ACT.Silu).then_inc(s["tile_silu"], 1)

            def tile_out(t, b, i):
                act.wait_ge(s["tile_y"], t + 1)
                if i is not None:
                    act.wait_ge(s[f"tile_stored{b}"], i * 16)
                a.copy(Yt[:, b, :], ps[:, 4 + b, 0:D]).then_inc(s["tile_out"], 1)

            def hidden_out(t, b):
                act.wait_ge(s["tile_ht"], t + 1)
                a.copy(h0T[:, b, :], ps[:, 6 + b, 0:P]).then_inc(s["tile_ht_copied"], 1)

            silu(0, 0)
            for k in range(2):
                hidden_out(k, k)
                silu(k + 1, 1 - k)
                tile_out(k, k, None)
            with act.Fori(1, (NT0 - 2) // 2) as i:
                for k in range(2):
                    hidden_out(2 * i + k, k)
                    silu(2 * i + (k + 1), 1 - k)
                    tile_out(2 * i + k, k, i)
            hidden_out(NT0 - 2, 0)
            silu(NT0 - 1, 1)
            tile_out(NT0 - 2, 0, NT0 // 2 - 1)
            hidden_out(NT0 - 1, 1)
            tile_out(NT0 - 1, 1, NT0 // 2 - 1)

            with act.Fori(0, NGC) as g:
                for h in range(GC * NH):
                    act.wait_ge(s["st_ready"], g * (GC * NH) + (h + 1))
                    a.activation(PTb[:, h % 2].rearrange("p c q -> p (c q)"), ps[:, 2 + h % 2, :], ACT.Exp,
                                 scale=DH ** -0.5).then_inc(s["st_exp"], 1)
                routing_side(GC, E1, act.snap(g + (NGA + 1)))

            def gelu(t, e, which, bias):
                src, dst = (3, Ha) if which == 1 else (5, Hb)
                act.wait_ge(s[f"l1_h{which}_turned"], t + 1)
                for f in range(KH):
                    a.activation(dst[:, f, :], ps[:, src, f * P:(f + 1) * P], ACT.Gelu,
                                 bias=bias[:, bass.ds(e, 1), f:f + 1].rearrange("p a b -> p (a b)")).then_inc(s[f"l1_h{which}_gelu"], 1)

            def expert(t):
                return act.value_load(tab[0:1, t, 0:1], min_val=0, max_val=E1 - 1)

            act.wait_ge(s["w1_loaded"], 16 * (3 + 2 * E1))
            act.wait_ge(s["table_ready"], 2)
            gelu(0, expert(0), 1, b1T)
            with act.Fori(0, NT1 - 1) as t:
                gelu(t, expert(t), 2, b2T)
                gelu(t + 1, expert(t + 1), 1, b1T)
            gelu(NT1 - 1, expert(NT1 - 1), 2, b2T)

        @blk.tensor
        def _(pe):
            mm, tr = nc.tensor.matmul, nc.tensor.transpose
            pe.wait_ge(s["setup_pool"], 2)
            pe.wait_ge(s["consts_loaded"], 16 * N_CONST)
            for q in range(2):
                for c in range(KD):
                    o = (q * 2 + c) * LAT
                    i = tr(ps[:, 7, o:o + LAT], gam_n[:, q, c * P:(c + 1) * P], ident[0:LAT, 0:LAT])
            i.then_inc(s["gb_t_ready"], 1)
            pe.wait_ge(s["setup_dve"], 10)

            def ranks(n, E, turn):
                pe.wait_ge(s["xnt_copied"], turn)
                bank, w = (4, rw) if E == E0 else (7, gwt)
                for j in range(n):
                    for k in range(KD):
                        i = mm(ps[:, bank, j * E:(j + 1) * E], xT[:, k, j * P:(j + 1) * P], w[:, k, :], start=(k == 0), stop=(k == KD - 1))
                i.then_inc(s["logits_ready"], 1)
                pe.wait_ge(s["mask_ready"], turn)
                r = ps[:, 5, 0:(n + 1) * E].rearrange("p (j e) -> p j e", e=E)
                mm(r, tri[:], mask[:, 0:n + 1, 0:E], start=True, stop=False)
                for j in range(n):
                    i = mm(r[:, j + 1:n + 1, :], ones_b[:], mask[:, j, 0:E].unsqueeze(1).to_broadcast((P, n - j, E)),
                           start=False, stop=(j == n - 1))
                i.then_inc(s["rank_ready"], 1)

            with pe.Fori(0, NGA) as g:
                t1 = pe.snap(g + 1)
                pe.wait_ge(s["x_loaded"], (g + 1) * 32)
                pe.wait_ge(s["x2_ready"], t1)
                for q in range(2):
                    i = mm(ps[0:LAT, q, :], thw[:], cx[:, 2 * q:2 * q + 2, :], start=True, stop=True)
                i.then_inc(s["theta_ready"], 1)
                pe.wait_ge(s["xl_ready"], t1)
                for q in range(2):
                    i = mm(ps[0:LAT, 2 + q, :], phw[:], xl[:, 2 * q:2 * q + 2, :], start=True, stop=True)
                i.then_inc(s["phi_ready"], 1)
                for j in range(GA):
                    for c in range(2):
                        o = (j * 2 + c) * LAT
                        i = mm(ps[:, 4, o:o + LAT], xl[:, j, c * P:(c + 1) * P], gw[:], start=True, stop=True)
                i.then_inc(s["gt_ready"], 1)
                pe.wait_ge(s["theta_copied"], t1)
                pe.wait_ge(s["phi_copied"], t1)
                for j in range(GA):
                    for c in range(2):
                        i = mm(ps[:, j, c * D:(c + 1) * D], thS[:, j, c * P:(c + 1) * P], phS[:, j, :], start=True, stop=True)
                    i.then_inc(s["scores_ready"], 1)
                for j in range(GA):
                    pe.wait_ge(s["p_ready"], g * (GA * 2) + (2 * j + 2))
                    for sc in range(2):
                        for c in range(2):
                            o = sc * D + c * P
                            i = tr(ps[:, j, o:o + P], Pm[:, j, c, sc * P:(sc + 1) * P], ident[:])
                    i.then_inc(s["pt_ready"], 1)
                pe.wait_ge(s["pt_copied_v"], (g + 1) * 2)
                pe.wait_ge(s["pt_copied_a"], (g + 1) * 2)
                pe.wait_ge(s["gt_copied"], t1)
                for j in range(GA):
                    for c in range(2):
                        o = (j * 2 + c) * LAT
                        for sc in range(2):
                            i = mm(ps[:, 4, o:o + LAT], PTm[:, j, sc, c * P:(c + 1) * P], gS[:, j, sc, :], start=(sc == 0), stop=(sc == 1))
                i.then_inc(s["pv_ready"], 1)
                pe.wait_ge(s["sums_ready"], t1)
                mm(ps[:, 5, 0:2 * GA], ones[:], sums[:].rearrange("p a j -> p (a j)"), start=True, stop=True).then_inc(s["tot_ready"], 1)
                pe.wait_ge(s["h_ready"], t1)
                alone(pe)
                for j in range(GA):
                    for c in range(2):
                        o = (j % 2) * D + c * P
                        i = tr(ps[0:LAT, 6 + j // 2, o:o + P], tx[:, j, c, :], ident[:])
                i.then_inc(s["ht_ready"], 1)
                pe.wait_ge(s["ht_copied"], t1)
                for q in range(2):
                    i = mm(ps[:, q, :], ow[:], hS[:, 2 * q:2 * q + 2, :], start=True, stop=True)
                i.then_inc(s["proj_ready"], 1)
                pe.wait_ge(s["xn_ready"], t1)
                for k in range(KD):
                    for j in range(GA):
                        i = tr(ps[:, 2 + k, j * P:(j + 1) * P], xn[:, j, k * P:(k + 1) * P], ident[:])
                i.then_inc(s["xnt_ready"], 1)
                ranks(GA, E0, t1)
                pe.wait_ge(s["w0_loaded"], 8 * 16)
                for f in range(2):
                    for w, bank in ((Sus, f), (Sgs, 6 + f)):
                        for k in range(KD):
                            i = mm(ps[:, bank, :], w[:, k, f * P:(f + 1) * P], xT[:, k, :], start=(k == 0), stop=(k == KD - 1))
                    i.then_inc(s["u_ready"], 1)
                pe.wait_ge(s["hs_ready"], 2 * (g + 1))
                for j in range(GA):
                    for f in range(2):
                        o = (j % 2) * D
                        i = mm(ps[:, 2 + j // 2, o:o + D], hs[:, f, j * P:(j + 1) * P], Sds[:, f, :], start=(f == 0), stop=(f == 1))
                i.then_inc(s["y_ready"], 1)

            def turn_tile(t, b, before, i, first=False):
                pe.wait_ge(s[f"tile_loaded{b}"], (before // 2 + i + 1) * 16)
                if not first:
                    pe.wait_ge(s["tile_copied"], before + t - 1)
                for k in range(KD):
                    i = tr(ps[:, b, k * P:(k + 1) * P], Xin[:, b, k * P:(k + 1) * P], ident[:])
                i.then_inc(s["tile_turned"], 1)

            def expert0(t):
                return pe.value_load(tab[0:1, t, 0:1], min_val=0, max_val=E0 - 1)

            def up_gate(t, b):
                e = expert0(t)
                pe.wait_ge(s["tile_copied"], t + 1)
                for k in range(KD):
                    i = mm(ps[:, 2 + b, 0:2 * F0], XTt[:, b, k * P:(k + 1) * P],
                           Wug[:, bass.ds(e, 1), k, :, :].rearrange("p x a f -> p (x a f)"), start=(k == 0), stop=(k == KD - 1))
                i.then_inc(s["ug_ready"], 1)

            def turn_hidden(t, b):
                pe.wait_ge(s["tile_h"], t + 1)
                tr(ps[:, 6 + b, 0:P], h0_t[:, b, :], ident[:]).then_inc(s["tile_ht"], 1)

            def down(t, b):
                e = expert0(t)
                pe.wait_ge(s["tile_ht_copied"], t + 1)
                mm(ps[:, 4 + b, 0:D], h0T[:, b, :], Wds[:, bass.ds(e, 1), :].rearrange("p a d -> p (a d)"),
                   start=True, stop=True).then_inc(s["tile_y"], 1)

            pe.wait_ge(s["table_ready"], 1)
            turn_tile(0, 0, 0, 0, first=True)
            turn_tile(1, 1, 0, 0, first=True)
            up_gate(0, 0)
            with pe.Fori(0, (NT0 - 2) // 2) as i2:
                for k in range(2):
                    turn_hidden(2 * i2 + k, k)
                    turn_tile(2 * i2 + (k + 2), k, 0, i2 + 1)
                    up_gate(2 * i2 + (k + 1), 1 - k)
                    down(2 * i2 + k, k)
            turn_hidden(NT0 - 2, 0)
            up_gate(NT0 - 1, 1)
            down(NT0 - 2, 0)
            turn_hidden(NT0 - 1, 1)
            down(NT0 - 1, 1)

            pe.wait_ge(s["phase_done"], 1)
            NS = GC * NH
            with pe.Fori(0, NGC) as g:
                t1 = pe.snap(g + 1)
                pe.wait_ge(s["v_loaded"], t1 * 16)
                for j in range(GC):
                    for c in range(2):
                        o = (j * 2 + c) * P
                        i = tr(ps[:, 6, o:o + P], cx[:, j, c * P:(c + 1) * P], ident[:])
                i.then_inc(s["vt_ready"], 1)
                pe.wait_ge(s["k_stacked"], t1 * 48)
                pe.wait_ge(s["q_stacked"], t1 * 48)
                for h in range(NS):
                    if h >= 2:
                        pe.wait_ge(s["s_max"], g * NS + (h - 1))
                    for c in range(2):
                        i = mm(ps[:, h % 2, c * D:(c + 1) * D], QS[0:NK, h, c * P:(c + 1) * P], KS[0:NK, h, :], start=True, stop=True)
                    i.then_inc(s["s_ready"], 1)
                pe.wait_ge(s["m_ready"], t1)
                alone(pe)
                tr(ps[0:4 * NS, 7, 0:P], nmr[:].bitcast(F32).rearrange("p t a -> p (t a)"), ident[:]).then_inc(s["mt_ready"], 1)
                pe.wait_ge(s["m_stacked"], t1 * 32)
                pe.wait_ge(s["vt_copied"], t1)

                def values(h):
                    j, hh = h // NH, h % NH
                    pe.wait_ge(s["st_exp"], g * NS + (h + 1))
                    for c in range(2):
                        o = (c * NH + hh) * (DH + 1)
                        for lc in range(2):
                            i = mm(ps[:, 4 + j, o:o + DH + 1], PTb[:, h % 2, lc, c * P:(c + 1) * P], VT[:, j, lc, hh, :],
                                   start=(lc == 0), stop=(lc == 1))
                    if hh == NH - 1:
                        i.then_inc(s["o_ready"], 1)

                for h in range(NS):
                    for lc in range(2):
                        i = mm(ps[:, 2 + h % 2, lc * D:(lc + 1) * D], KS[0:NK + 2, h, lc * P:(lc + 1) * P], QS[0:NK + 2, h, :], start=True, stop=True)
                    i.then_inc(s["st_ready"], 1)
                    if h >= 1:
                        values(h - 1)
                values(NS - 1)
                pe.wait_ge(s["o_norm"], t1 * GC)
                for j in range(GC):
                    for c in range(2):
                        o = j * D + c * P
                        i = tr(ps[:, 6, o:o + P], oN[:, j, c * P:(c + 1) * P], ident[:])
                i.then_inc(s["ot_ready"], 1)
                pe.wait_ge(s["xn_ready"], g + (NGA + 1))
                for k in range(KD):
                    for j in range(GC):
                        o = k * D + j * P
                        i = tr(ps[:, 6, o:o + P], xn[:, j, k * P:(k + 1) * P], ident[:])
                i.then_inc(s["xnt_ready"], 1)
                ranks(GC, E1, pe.snap(g + (NGA + 1)))

            def expert1(t):
                return pe.value_load(tab[0:1, t, 0:1], min_val=0, max_val=E1 - 1)

            def hidden1(t, b):
                e = expert1(t)
                pe.wait_ge(s["tile_copied"], NT0 + t + 1)
                for k in range(KD):
                    i = mm(ps[:, 2, :], XTt[:, b, k * P:(k + 1) * P], W1s[:, bass.ds(e, 1), k, :].rearrange("p a f -> p (a f)"),
                           start=(k == 0), stop=(k == KD - 1))
                i.then_inc(s["l1_h1_ready"], 1)

            def hidden2(t):
                e = expert1(t)
                pe.wait_ge(s["w2_loaded"], (e + 1) * 16)
                for k in range(KH):
                    pe.wait_ge(s["l1_h1_gelu"], 4 * t + (k + 1))
                    i = mm(ps[:, 4, :], Ha[:, k, :], W2s[:, bass.ds(e, 1), k, :].rearrange("p a f -> p (a f)"),
                           start=(k == 0), stop=(k == KH - 1))
                i.then_inc(s["l1_h2_ready"], 1)

            def turn_pre(t, which):
                pre, bank = (pre1, 3) if which == 1 else (pre2, 5)
                pe.wait_ge(s[f"l1_h{which}_copied"], t + 1)
                for f in range(KH):
                    i = tr(ps[:, bank, f * P:(f + 1) * P], pre[:, f * P:(f + 1) * P], ident[:])
                i.then_inc(s[f"l1_h{which}_turned"], 1)

            def hidden3(t, b):
                e = expert1(t)
                pe.wait_ge(s["tile_out"], NT0 + t - 1)
                for k in range(KH):
                    pe.wait_ge(s["l1_h2_gelu"], 4 * t + (k + 1))
                    i = mm(ps[:, 6 + b, 0:D], Hb[:, k, :], W3s[:, bass.ds(e, 1), k, :].rearrange("p a d -> p (a d)"),
                           start=(k == 0), stop=(k == KH - 1))
                i.then_inc(s["tile_y"], 1)

            pe.wait_ge(s["table_ready"], 2)
            pe.wait_ge(s["w1_loaded"], 16 * (3 + 2 * E1))
            turn_tile(0, 0, NT0, 0)
            turn_tile(1, 1, NT0, 0)
            hidden1(0, 0)
            turn_pre(0, 1)
            with pe.Fori(0, (NT1 - 2) // 2) as i2:
                for k in range(2):
                    hidden2(2 * i2 + k)
                    hidden1(2 * i2 + (k + 1), 1 - k)
                    turn_pre(2 * i2 + k, 2)
                    turn_pre(2 * i2 + (k + 1), 1)
                    turn_tile(2 * i2 + (k + 2), k, NT0, i2 + 1)
                    hidden3(2 * i2 + k, k)
            hidden2(NT1 - 2)
            hidden1(NT1 - 1, 1)
            turn_pre(NT1 - 2, 2)
            turn_pre(NT1 - 1, 1)
            hidden3(NT1 - 2, 0)
            hidden2(NT1 - 1)
            turn_pre(NT1 - 1, 2)
            hidden3(NT1 - 1, 1)




def kernel(**inputs):
    import numpy as _np
    import concourse.bacc as _bacc
    from concourse import mybir as _mybir
    from concourse.bass_utils import run_bass_kernel_spmd as _run

    i = {k: _np.asarray(v) for k, v in inputs.items()}

    def by_feature(b):
        return b.reshape(b.shape[0], -1, P).transpose(2, 0, 1)

    arrays = {
        "x": i["x"], "ctx": i["ctx_2048"], "g_xattn": i["g_xattn"], "g_ffn": i["g_ffn"],
        "theta_wT": i["L0_xattn_theta_w"].T, "theta_b": i["L0_xattn_theta_b"],
        "phi_wT": i["L0_xattn_phi_w"].T, "phi_b": i["L0_xattn_phi_b"],
        "g_wT": i["L0_xattn_g_w"].T, "g_b": i["L0_xattn_g_b"],
        "ln_gamma": i["L0_xattn_ln_gamma"], "ln_beta": i["L0_xattn_ln_beta"],
        "out_wT": i["L0_xattn_out_w"].T, "out_b": i["L0_xattn_out_b"],
        "router_wT": i["L0_ffn_router_w"].T, "router_bias": i["L0_ffn_router_bias"],
        "Wu0": i["L0_ffn_Wu"], "Wg0": i["L0_ffn_Wg"], "Wd0": i["L0_ffn_Wd"],
        "Su": i["L0_ffn_Su"], "Sg": i["L0_ffn_Sg"], "Sd": i["L0_ffn_Sd"],
        "gamma1": i["L1_xattn_gamma"].reshape(1, 1),
        "W1": i["L1_ffn_W1"], "b1": by_feature(i["L1_ffn_b1"]), "W2": i["L1_ffn_W2"], "b2": by_feature(i["L1_ffn_b2"]),
        "W3": i["L1_ffn_W3"], "b3": i["L1_ffn_b3"], "gate_w": i["L1_ffn_Wg"], "gate_b": i["L1_ffn_bg"],
    }
    arrays = {k: _np.ascontiguousarray(v) for k, v in arrays.items()}
    nc = _bacc.Bacc("TRN2", target_bir_lowering=False, num_devices=1)
    args = {k: nc.dram_tensor(f"in_{k}", v.shape, _mybir.dt.from_np(v.dtype), kind="ExternalInput").ap()
            for k, v in arrays.items()}
    out = nc.dram_tensor("out", i["x"].shape, _mybir.dt.float32, kind="ExternalOutput").ap()
    flamingo_kernel(nc, **args, out=out)
    r = _run(nc, [{f"in_{k}": v for k, v in arrays.items()}], core_ids=[0])
    return r.results[0]["out"]
```

```python
from contextlib import ExitStack

import numpy as np

import concourse.bass as bass
from concourse import mybir

P = 128
ALU = mybir.AluOpType
ACT = mybir.ActivationFunctionType
AX = mybir.AxisListType.X
F32 = mybir.dt.float32
F32R = mybir.dt.float32r
BF16 = mybir.dt.bfloat16
I32 = mybir.dt.int32
U32 = mybir.dt.uint32
LN_EPS = 1e-5
GA = 4
NC = 4
GE = 2
NX = 4


class Steps:

    def __init__(self, eng, sem):
        self.eng, self.sem, self.before = eng, sem, 0

    def turn(self, g, per_turn, k=0):
        self.g, self.per_turn, self.k = g, per_turn, k

    def step(self, k):
        return self.g * self.per_turn + (self.before + k)

    def mark(self, ins):
        self.k += 1
        ins.then_inc(self.sem, 1)
        return self.step(self.k)

    def then(self, ins):
        self.eng.wait_ge(self.sem, self.mark(ins))

    def end(self, turns):
        assert self.per_turn in (self.k, 0), self.k
        self.before += turns * self.k


def flamingo_kernel(nc, x, ctx, g_xattn, g_ffn, theta_wT, theta_b, phi_wT, phi_b, g_wT, g_b, ln_gamma, ln_beta,
                    out_wT, out_b, router_wT, router_bias, Wu0, Wg0, Wd0, Su, Sg, Sd, gamma1,
                    W1, b1, W2, b2, W3, b3, gate_w, gate_b, out):
    B, S, D = x.shape
    LAT = theta_wT.shape[1]
    E0, _, F0 = Wu0.shape
    E1, _, H1 = W1.shape
    KD = D // P
    KH = H1 // P
    TOK = B * S
    CAP = TOK + P
    NT0 = (2 * TOK + E0 * (P - 1)) // P
    NT1 = (2 * TOK + E1 * (P - 1)) // P
    NT0 += -NT0 % NX
    NT1 += -NT1 % NX
    NGA, NGE = B // GA, B // GE
    NH, DH = 8, S // 8

    x_v = x.rearrange("b p d -> p b d")
    ctx_v = ctx.rearrange("b p d -> p b d")
    out_v = out.rearrange("b p d -> p b d")
    xg0 = nc.dram_tensor("xg0", [E0 * CAP, D], F32, kind="Internal").ap()
    yg0 = nc.dram_tensor("yg0", [NT0 * P, D], F32, kind="Internal").ap()
    xg1 = nc.dram_tensor("xg1", [E1 * CAP, D], F32, kind="Internal").ap()
    yg1 = nc.dram_tensor("yg1", [NT1 * P, D], F32, kind="Internal").ap()
    kscr = nc.dram_tensor("kscr", [2, TOK, D], F32, kind="Internal").ap()
    qscr = nc.dram_tensor("qscr", [2, TOK, D], F32, kind="Internal").ap()

    with ExitStack() as es:
        def sb(name, shape, dt=F32):
            return es.enter_context(nc.sbuf_tensor(name, shape, dt))

        def sem(name):
            return es.enter_context(nc.semaphore(name))

        xs = sb("xs", [P, B, D])
        WX = KD * H1 + KH * H1 + KH * D
        RING = 3
        with nc.sbuf_tensor("QK", [P, 2, NC * 8 * D], F32R) as QK:
            pass
        with nc.sbuf_tensor("WR", [P, RING * 2 * WX], F32R) as WR:
            with nc.sbuf_tensor("wraw", [P, WX], F32) as wraw:
                pass
        R2 = sb("R2", [P, 2 * RING * WX + WX])
        n = E0 * KD * F0
        Wug = R2[:, 0:2 * n].rearrange("p (e k a f) -> p e k a f", e=E0, k=KD, a=2)
        Wds = R2[:, 2 * n:3 * n].rearrange("p (e d) -> p e d", e=E0)
        F2 = Su.shape[2]
        m = 3 * n
        Sus = R2[:, m:m + KD * F2].rearrange("p (k f) -> p k f", k=KD)
        Sgs = R2[:, m + KD * F2:m + 2 * KD * F2].rearrange("p (k f) -> p k f", k=KD)
        Sds = R2[:, m + 2 * KD * F2:m + 3 * KD * F2].rearrange("p (k d) -> p k d", k=KD)
        m += 3 * KD * F2
        gS, tx = (R2[:, m + k * GA * 2 * LAT:m + (k + 1) * GA * 2 * LAT].rearrange("p (j c l) -> p j c l", j=GA, c=2) for k in range(2))
        assert 2 * NC * 8 * D <= 2 * (RING - 1) * WX and m + 2 * GA * 2 * LAT <= 2 * RING * WX + WX
        ident = sb("ident", [P, P])
        ones = sb("ones", [P, P])
        tri_f = sb("tri_f", [P, P])
        tri = sb("tri", [P, P], BF16)
        ones_b = sb("ones_b", [P, P], BF16)
        iota_i = sb("iota_i", [P, 64], I32)
        iota_f = sb("iota_f", [P, 64])
        iota_pi = sb("iota_pi", [P, 1], I32)
        iota_p = sb("iota_p", [P, 1])
        zeros = sb("zeros", [P, D])
        gates = sb("gates", [P, 5])
        tg = sb("tg", [P, 4])
        tgg = sb("tgg", [P, 1])
        thw = sb("thw", [P, LAT])
        phw = sb("phw", [P, LAT])
        gw = sb("gw", [P, LAT])
        thb = sb("thb", [LAT, 1])
        phb = sb("phb", [LAT, 1])
        gb_bc = sb("gb_bc", [P, LAT])
        gbT = sb("gbT", [P, 2, KD, LAT])
        ow = sb("ow", [LAT, P])
        ob = sb("ob", [P, 1])
        rw = sb("rw", [P, KD, E0])
        rb_bc = sb("rb_bc", [P, E0])
        gwt = sb("gwt", [P, KD, E1])
        gbs = sb("gbs", [P, E1])
        b1T = sb("b1T", [P, E1, KH])
        b2T = sb("b2T", [P, E1, KH])
        b3bc = sb("b3bc", [P, E1, D])
        wts = sb("wts", [P, B, 2])
        idxf = sb("idxf", [P, B, 2])
        slotf = sb("slotf", [P, B, 2])
        yslot = sb("yslot", [P, B, 2], U32)
        base = {E0: sb("base0", [P, E0]), E1: sb("base1", [P, E1])}
        cnt = sb("cnt", [P, E0])
        meta = sb("meta", [P, 9, E0])
        tabf = sb("tabf", [P, NT0, 4])
        tab = sb("tab", [1, NT0, 3], I32)
        endi = sb("endi", [1, E0], I32)
        ztail = sb("ztail", [P, E0], U32)

        cx = sb("cx", [P, GA, D])
        xl = sb("xl", [P, GA, D])
        xn = sb("xn", [P, GA, D])
        st6 = sb("st6", [P, GA, 6])
        st2 = sb("st2", [P, GA, 2])
        rstd = sb("rstd", [P, GA])
        veps = sb("veps", [P, GA])
        nhalf = sb("nhalf", [P, GA])
        Q1 = sb("Q1", [P, GA * 2 * D])
        Q2 = sb("Q2", [P, GA * 2 * D])
        xT = sb("xT", [P, KD, GA * P])
        thS = sb("thS", [LAT, GA, D])
        nm = sb("nm", [P, GA, 2])
        rsum = sb("rsum", [P, GA, 2])
        rrec = sb("rrec", [P, GA, 2])
        sums = sb("sums", [P, 2, GA])
        mom = sb("mom", [P, 4, GA])
        lb = sb("lb", [P, GA, E0])
        lmx = sb("lmx", [P, GA])
        ex = sb("ex", [P, GA, E0])
        key = sb("key", [P, GA, E0])
        v8 = sb("v8", [P, GA, 8])
        i8 = sb("i8", [P, GA, 8], U32)
        oh = sb("oh", [P, GA, 2, E0])
        ohx = sb("ohx", [P, GA, 2, E0])
        mask = sb("mask", [P, GA + 1, E0], BF16)
        rk = sb("rk", [P, GA, E0])
        sel = sb("sel", [P, GA, 2])
        den = sb("den", [P, GA])
        slotu = sb("slotu", [P, GA, 2], U32)
        ps = es.enter_context(nc.psum_tensor("ps", [P, 8, 512], F32))

        gam_n = Q1[0:LAT, 0:2 * D].rearrange("p (a d) -> p a d", a=2)
        phS = Q2[0:LAT, 0:GA * D].rearrange("p (j d) -> p j d", j=GA)
        big1 = Q2[:, 2 * GA * P:2 * GA * P + NT0 * E0]
        hS = thS
        txq = gS
        tmp = Q1[:, 0:GA * D].rearrange("p (j d) -> p j d", j=GA)
        hs = Q2[:, 0:2 * GA * P].rearrange("p (f t) -> p f t", f=2)
        Pm = Q1[:, :].rearrange("p (j c s) -> p j c s", j=GA, c=2)
        PTm = Q2[:, :].rearrange("p (j c t) -> p j c t", j=GA, c=2)
        Xin = Q1[:, 0:NX * D].rearrange("p (n d) -> p n d", n=NX)
        Yt = Q1[:, 4 * D:6 * D].rearrange("p (n d) -> p n d", n=2)
        XTt = Q2[:, 0:2 * D].rearrange("p (n d) -> p n d", n=2)
        su_t = Q2[:, 2 * D:3 * D].rearrange("p (n d) -> p n d", n=2)
        h0_t = Q2[:, 3 * D:4 * D].rearrange("p (n d) -> p n d", n=2)
        h0T = Q2[:, 4 * D:5 * D].rearrange("p (n d) -> p n d", n=2)
        pre1, pre2 = Q1[:, 6 * D:8 * D], Q2[:, 0:2 * D]
        Ha = Q2[:, 2 * D:4 * D].rearrange("p (k t) -> p k t", k=KH)
        Hb = Q2[:, 4 * D:6 * D].rearrange("p (k t) -> p k t", k=KH)
        XTp = sb("XTp", [P, 2, D], F32R)
        Hap = sb("Hap", [P, 2, KH, P], F32R)
        Hbp = sb("Hbp", [P, 2, KH, P], F32R)
        NK = 3 * DH
        QS = QK[:, 0, :].rearrange("p (n a t) -> p n a t", n=NC, a=NH)
        KS = QK[:, 1, :].rearrange("p (n a t) -> p n a t", n=NC, a=NH)
        split = sb("split", [P, 2, 2, D], F32R)
        csplit = [split[:], Hap[:].rearrange("p a k t -> p a (k t)").rearrange("p a (j d) -> p a j d", j=2)]
        mraw = sb("mraw", [P, 2, NH, 2])
        nmr = sb("nmr", [P, 2, NH * 2], F32R)
        mT = sb("mT", [2 * NH * 2, P], F32R)
        PTb = Q1[:, :].rearrange("p (n c q) -> p n c q", n=4, c=2)
        gC = sb("gC", [P, 2, 2, D])
        VE = 32
        VT = Q2[:, 0:2 * 2 * NH * VE].rearrange("p (n c h e) -> p n c h e", n=2, c=2, h=NH)
        q2 = 2 * 2 * NH * VE
        oU = Q2[:, q2:q2 + 2 * D]
        q2 += 2 * D
        oN = Q2[:, q2:q2 + D]
        q2 += D
        orec = Q2[:, q2:q2 + 2 * NH].rearrange("p (c h) -> p c h", c=2)
        gE = Q1[:, :].rearrange("p (n j k d) -> p n j k d", n=2, j=GE, k=2)
        idxg = sb("idxg", [P, 2, GE, 2], U32)

        names = ("vector_steps x_loaded ctx_high ctx_split ctx_split_stored0 ctx_split_stored1 setup_pool setup_dve tanh_done gb_t_ready w0_loaded w1_loaded wraw_loaded w_high w_split l1_h1_split l1_h2_split h1_high h2_high x_high "
                 "xl_ready theta_ready theta_copied phi_ready phi_copied gt_ready gt_copied "
                 "scores_ready max_ready p_ready pt_ready pt_copied_v pt_copied_a pv_ready sums_ready tot_ready "
                 "h_ready ht_ready ht_copied proj_ready xn_ready xnt_ready xnt_copied logits_ready "
                 "dif_ready ex_ready mask_ready rank_ready slots_ready scattered scattered0 scattered1 u_ready silu_ready "
                 "hs_ready y_ready x2_ready tails_ready tails_zeroed table_ready yslots_ready "
                 "tile_loaded0 tile_loaded1 tile_loaded2 tile_loaded3 tile_turned tile_copied ug_ready tile_silu tile_h tile_y tile_out tile_stored0 tile_stored1 output_stored0 output_stored1 "
                 "l1_h1_ready l1_h1_copied l1_h1_turned l1_h1_gelu l1_h2_ready l1_h2_copied l1_h2_turned l1_h2_gelu "
                 "tile_ht tile_ht_copied var_ready var_eps rstd_ready alone "
                 "idx_copied gathered0 gathered1 gather_used q_ready q_stored0 q_stored1 q_stacked0 q_stacked1 k_stacked0 k_stacked1 v_loaded0 v_loaded1 vt_ready vt_copied "
                 "s_ready s_max m_high m_ready mt_copied m_stacked st_ready st_exp o_ready o_copied o_turned o_inverse o_norm ot_ready row_sum0 row_sum1 row_stats q_high x_sum x_stats x_var x_eps x_rstd "
                 "consts_loaded out_summed xn_free pool_a phase_done out_ready out_stored x1_used").split()
        s = {nm_: sem(nm_) for nm_ in names}

        def alone(eng):
            eng.sem_inc(s["alone"], 1)

        def is_tile(t):
            return not isinstance(t, int) or 0 <= t < NT1

        def item(t):
            return not isinstance(t, int) or 0 <= t < B

        def item_turns(eng, turn):
            for t in range(-4, 3):
                turn(t, t % NC)
            full = (B - 8) // NC
            with eng.Fori(0, full) as i:
                for k in range(3, NC + 3):
                    turn(NC * i + k, k % NC)
            for t in range(NC * full + 3, B + 3):
                turn(t, t % NC)

        def tile_turns(eng, turn):
            for t in range(-3, 3):
                turn(t, t % NX)
            full = (NT1 - 6) // NX
            with eng.Fori(0, full) as i:
                for k in range(3, NX + 3):
                    turn(NX * i + k, k % NX)
            for t in range(NX * full + 3, NT1 + 2):
                turn(t, t % NX)

        blk = es.enter_context(nc.Block())

        def load_tiles(sp, nt, xg, before):
            def load(t, b):
                row = sp.value_load(tab[0:1, t, 1:2], min_val=0, max_val=xg.shape[0] - P)
                sp.dma_start(Xin[:, b, :], xg[bass.ds(row, P), :]).then_inc(s[f"tile_loaded{b}"], 16)

            for b in range(NX):
                load(b, b)
            with sp.Fori(0, nt // NX - 1) as i:
                for b in range(NX):
                    sp.wait_ge(s["tile_turned"], NX * i + (before + b + 1))
                    alone(sp)
                    load(NX * i + (b + NX), b)

        def store_tiles(pool, nt, yg, before):
            with pool.Fori(0, nt // 2) as i:
                for b in range(2):
                    pool.wait_ge(s["tile_out"], 2 * i + (before + b + 1))
                    alone(pool)
                    pool.dma_start(yg[bass.ds((2 * i + b) * P, P), :], Yt[:, b, :]).then_inc(s[f"tile_stored{b}"], 16)

        N_CONST = 17
        @blk.sync
        def _(sp):
            n_c = 0

            def const(dst, src):
                nonlocal n_c
                sp.dma_start(dst, src).then_inc(s["consts_loaded"], 16)
                n_c += 1

            const(gates[:, 0:2], g_xattn.unsqueeze(0).to_broadcast((P, 2)))
            const(gates[:, 2:4], g_ffn.unsqueeze(0).to_broadcast((P, 2)))
            const(gates[:, 4:5], gamma1.to_broadcast((P, 1)))
            const(thw[:], theta_wT)
            const(phw[:], phi_wT)
            const(gw[:], g_wT)
            const(thb[:], theta_b.unsqueeze(1))
            const(phb[:], phi_b.unsqueeze(1))
            const(gb_bc[:], g_b.unsqueeze(0).to_broadcast((P, LAT)))
            const(gam_n[:, 0, :], ln_gamma)
            const(gam_n[:, 1, :], ln_beta)
            const(ow[:], out_wT)
            const(ob[:], out_b.unsqueeze(1))
            const(rw[:], router_wT.rearrange("(k p) e -> p k e", p=P))
            const(rb_bc[:], router_bias.unsqueeze(0).to_broadcast((P, E0)))
            const(gwt[:], gate_w.rearrange("(k p) e -> p k e", p=P))
            const(gbs[:], gate_b.unsqueeze(0).to_broadcast((P, E1)))
            assert n_c == N_CONST
            with sp.Fori(0, NGA) as g:
                sp.dma_start(xs[:, bass.ds(g * GA, GA), :], x_v[:, bass.ds(g * GA, GA), :]).then_inc(s["x_loaded"], 16)
                sp.wait_ge(s["x1_used"], g + 1)
                sp.dma_start(cx[:], ctx_v[:, bass.ds(g * GA, GA), :]).then_inc(s["x_loaded"], 16)
                for c in range(2):
                    sp.wait_ge(s["ctx_split"], 2 * g + (c + 1))
                    for p in range(2):
                        sp.dma_start(kscr[p, bass.ds((2 * g + c) * 2 * P, 2 * P), :].rearrange("(j p) d -> p j d", p=P),
                                     csplit[c][:, p].bitcast(F32)).then_inc(s[f"ctx_split_stored{c}"], 16)
            sp.wait_ge(s["table_ready"], 1)
            sp.wait_ge(s["tails_zeroed"], 16 * E0)
            sp.wait_ge(s["scattered"], 16 * 2 * B)
            load_tiles(sp, NT0, xg0, 0)
            for c in range(2):
                sp.wait_ge(s[f"ctx_split_stored{c}"], NGA * 32)

            def stack(S_, scratch, t, n, parts, done):
                for i, part in enumerate(parts):
                    sp.dma_start(S_[i * DH:(i + 1) * DH, n].bitcast(F32),
                                 scratch[part, bass.ds(t * P, P), :].rearrange("(a d) t -> d a t", d=DH)).then_inc(s[done], 16)

            def sp_turn(t, k):
                if item(t + 2):
                    sp.wait_ge(s["vt_ready"], t - 1) if item(t - 2) else None
                    n, b = (k + 2) % NC, k % 2
                    sp.dma_start(cx[:, n, :], ctx_v[:, bass.ds(t + 2, 1), :].rearrange("p a d -> p (a d)")).then_inc(s[f"v_loaded{b}"], 16)
                if item(t + 3):
                    n, b = (k + 3) % NC, (k + 1) % 2
                    sp.wait_ge(s["o_ready"], t) if item(t - 1) else sp.wait_ge(s["phase_done"], 1)
                    alone(sp)
                    stack(KS, kscr, t + 3, n, (0, 1, 0), f"k_stacked{b}")
                    sp.wait_ge(s[f"q_stored{b}"], (t + 3) // 2 * 32 + 32)
                    alone(sp)
                    stack(QS, qscr, t + 3, n, (0, 0, 1), f"q_stacked{b}")
                if item(t + 1):
                    n = (k + 1) % NC
                    sp.wait_ge(s["mt_copied"], t + 2)
                    for p in range(2):
                        sp.dma_start(QS[NK + p:NK + p + 1, n].rearrange("o a (c q) -> o (a c) q", c=2).bitcast(F32),
                                     mT[p * 2 * NH:(p + 1) * 2 * NH, :].bitcast(F32)).then_inc(s["m_stacked"], 16)
                if item(t + 4):
                    sp.wait_ge(s["q_ready"], t + 5)
                    alone(sp)
                    for p in range(2):
                        sp.dma_start(qscr[p, bass.ds((t + 4) * P, P), :], split[:, k % 2, p, :].bitcast(F32)).then_inc(s[f"q_stored{k % 2}"], 16)

            item_turns(sp, sp_turn)
            sp.wait_ge(s["table_ready"], 2)
            sp.wait_ge(s["tails_zeroed"], 16 * (E0 + E1))
            for b in range(2):
                sp.wait_ge(s[f"scattered{b}"], 16 * B)
            load_tiles(sp, NT1, xg1, NT0)
            with sp.Fori(0, NGE) as g:
                sp.wait_ge(s["out_ready"], g + 1)
                sp.dma_start(out_v[:, bass.ds(g * GE, GE), :], xs[:, bass.ds(g * GE, GE), :]).then_inc(s["out_stored"], 16)
            sp.wait_ge(s["out_stored"], NGE * 16)

        @blk.gpsimd
        def _(pool):
            nc.gpsimd.memset(ones[:], 1.0).then_inc(s["pool_a"], 1)
            nc.gpsimd.memset(ident[:], 0.0).then_inc(s["pool_a"], 1)
            nc.gpsimd.memset(zeros[:], 0.0).then_inc(s["pool_a"], 1)
            nc.gpsimd.memset(nhalf[:], -0.5).then_inc(s["pool_a"], 1)
            nc.gpsimd.iota(iota_i[:], pattern=[[1, 64]], base=0, channel_multiplier=0).then_inc(s["pool_a"], 1)
            nc.gpsimd.iota(iota_pi[:], pattern=[[0, 1]], base=0, channel_multiplier=1).then_inc(s["pool_a"], 1)
            pool.wait_ge(s["pool_a"], 6)
            nc.gpsimd.affine_select(out=ident[:], in_=ident[:], compare_op=ALU.not_equal, fill=1.0, base=0,
                                    pattern=[[-1, P]], channel_multiplier=1).then_inc(s["setup_pool"], 1)
            nc.gpsimd.affine_select(out=tri_f[:], in_=ones[:], compare_op=ALU.is_gt, fill=0.0, base=0,
                                    pattern=[[1, P]], channel_multiplier=-1).then_inc(s["setup_pool"], 1)
            for dst, src in ((Sus, Su[0].rearrange("(k p) f -> p k f", p=P)), (Sgs, Sg[0].rearrange("(k p) f -> p k f", p=P)),
                             (Sds, Sd[0].rearrange("(k p) d -> p k d", p=P)),
                             (Wug[:, :, 0, 0, :], Wu0[:, 0:P, :].rearrange("e p f -> p e f")),
                             (Wug[:, :, 1, 0, :], Wu0[:, P:2 * P, :].rearrange("e p f -> p e f")),
                             (Wug[:, :, 0, 1, :], Wg0[:, 0:P, :].rearrange("e p f -> p e f")),
                             (Wug[:, :, 1, 1, :], Wg0[:, P:2 * P, :].rearrange("e p f -> p e f")),
                             (Wds, Wd0.rearrange("e f d -> f e d"))):
                pool.dma_start(dst, src).then_inc(s["w0_loaded"], 16)
            for dst, src in ((b1T[:], b1), (b2T[:], b2),
                             (b3bc[:], b3.unsqueeze(0).to_broadcast((P, E1, D)))):
                pool.dma_start(dst, src).then_inc(s["w1_loaded"], 16)

            def root(n, src, turn):
                pool.wait_ge(s["var_ready"], turn)
                alone(pool)
                dst = mom[:, 2, :] if src is None else rstd[:, 0:n]
                nc.gpsimd.tensor_scalar(veps[:, 0:n], mom[:, 3, :] if src is None else src, LN_EPS, None, ALU.add).then_inc(s["var_eps"], 1)
                pool.wait_ge(s["var_eps"], turn)
                nc.gpsimd.tensor_tensor(dst, veps[:, 0:n], nhalf[:, 0:n], ALU.pow).then_inc(s["rstd_ready"], 1)

            def load_weights(e):
                at = 0
                for W, k_ in ((W1, KD), (W2, KH), (W3, KH)):
                    w = W[e:e + 1] if isinstance(e, int) else W[bass.ds(e, 1)]
                    size = k_ * W.shape[2]
                    pool.dma_start(wraw[:, at:at + size].rearrange("p (x n) -> p x n", x=k_),
                                   w.rearrange("a (k p) n -> p (a k) n", p=P)).then_inc(s["wraw_loaded"], 16)
                    at += size

            def split_weights(e, place, last):
                def half(k):
                    at = place * (2 * WX) + k * WX
                    return WR[:, at:at + WX] if isinstance(at, int) else WR[:, bass.ds(at, WX)]

                if last is not None:
                    done = pool.value_load(endi[0:1, last:last + 1] if isinstance(last, int) else endi[0:1, bass.ds(last, 1)],
                                           min_val=0, max_val=NT1)
                    pool.wait_ge(s["tile_y"], done + NT0)
                pool.wait_ge(s["wraw_loaded"], (e + 1) * 48)
                alone(pool)
                nc.gpsimd.tensor_copy(half(0), wraw[:, :]).then_inc(s["w_high"], 1)
                pool.wait_ge(s["w_high"], e + 1)
                alone(pool)
                nc.gpsimd.tensor_tensor(half(1), wraw[:, :], half(0).bitcast(F32), ALU.subtract).then_inc(s["w_split"], 1)
                pool.wait_ge(s["w_split"], e + 1)
                alone(pool)

            def scatter(turn, n, xg, total):
                pool.wait_ge(s["slots_ready"], turn)
                alone(pool)
                for j in range(n):
                    for k in range(2):
                        pool.indirect_dma_start(xg[:, :], bass.IndirectOffsetOnAxis(ap=slotu[:, j, k:k + 1], axis=0),
                                                xn[:, j, :], None).then_inc(s["scattered"], 16)
                pool.wait_ge(s["scattered"], total)
                pool.sem_inc(s["xn_free"], 1)

            def zero_tails(turn, E, xg):
                pool.wait_ge(s["tails_ready"], turn)
                for e in range(E):
                    pool.indirect_dma_start(xg[:, :], bass.IndirectOffsetOnAxis(ap=ztail[:, e:e + 1], axis=0),
                                            zeros[:, :], None).then_inc(s["tails_zeroed"], 16)

            def gather(items, n, yg, turn, buf, ix, done):
                nc.gpsimd.tensor_copy(idxg[:, ix, 0:n], yslot[:, items, :]).then_inc(s["idx_copied"], 1)
                pool.wait_ge(s["idx_copied"], turn)
                alone(pool)
                for j in range(n):
                    for k in range(2):
                        pool.indirect_dma_start(buf[:, 2 * j + k, :], None, yg[:, :],
                                                bass.IndirectOffsetOnAxis(ap=idxg[:, ix, j, k:k + 1], axis=0)).then_inc(s[done], 16)

            load_weights(0)
            pool.sem_inc(s["xn_free"], 1)
            with pool.Fori(0, NGA) as g:
                root(GA, st2[:, 0:GA, 1], 3 * g + 1)
                pool.wait_ge(s["x_loaded"], (g + 1) * 32)
                for c in range(2):
                    pool.wait_ge(s[f"ctx_split_stored{c}"], g * 32)
                    alone(pool)
                    src = cx[:, 2 * c:2 * c + 2, :]
                    nc.gpsimd.tensor_copy(csplit[c][:, 0], src).then_inc(s["ctx_high"], 1)
                    pool.wait_ge(s["ctx_high"], 2 * g + (c + 1))
                    nc.gpsimd.tensor_tensor(csplit[c][:, 1], src, csplit[c][:, 0].bitcast(F32), ALU.subtract).then_inc(s["ctx_split"], 1)
                root(GA, None, 3 * g + 2)
                root(GA, st2[:, 0:GA, 1], 3 * g + 3)
                scatter(pool.snap(g + 1), GA, xg0, (g + 1) * (GA * 2 * 16))
            zero_tails(1, E0, xg0)
            split_weights(0, 2, None)
            load_weights(1)
            store_tiles(pool, NT0, yg0, 0)
            for b in range(2):
                pool.wait_ge(s[f"tile_stored{b}"], NT0 // 2 * 16)
            pool.wait_ge(s["yslots_ready"], 1)

            def item_root(col, ready, eps, done, turn):
                pool.wait_ge(s[ready], turn)
                alone(pool)
                nc.gpsimd.tensor_scalar(veps[:, col:col + 1], st2[:, col, 1:2], LN_EPS, None, ALU.add).then_inc(s[eps], 1)
                pool.wait_ge(s[eps], turn)
                nc.gpsimd.tensor_tensor(rstd[:, col:col + 1], veps[:, col:col + 1], nhalf[:, col:col + 1], ALU.pow).then_inc(s[done], 1)

            def c_gather(t, b):
                pool.wait_ge(s["gather_used"], t - 1) if item(t - 2) else None
                gather(bass.ds(t, 1), 1, yg0, t + 1, gC[:, b], b, f"gathered{b}")

            def c_pool_turn(t, k):
                if item(t + 4):
                    item_root(0, "var_ready", "var_eps", "rstd_ready", t + (3 * NGA + 5))
                if item(t - 1):
                    item_root(1, "x_var", "x_eps", "x_rstd", t)
                if item(t + 5):
                    c_gather(t + 5, (k + 1) % 2)
                if k % 2 == 0 and item(t - 3):
                    pair = (t - 4) // 2
                    pool.wait_ge(s["slots_ready"], pair + (NGA + 1))
                    alone(pool)
                    for j in range(k, k + 2):
                        for x in range(2):
                            pool.indirect_dma_start(xg1[:, :], bass.IndirectOffsetOnAxis(ap=slotu[:, j, x:x + 1], axis=0),
                                                    xn[:, j, :], None).then_inc(s[f"scattered{(k // 2) % 2}"], 16)

            c_gather(0, 0)
            item_turns(pool, c_pool_turn)
            zero_tails(2, E1, xg1)
            pool.wait_ge(s["ot_ready"], B)
            for e in range(1, RING):
                split_weights(e, (e + 2) % RING, None)
                load_weights(e + 1)
            pool.wait_ge(s["table_ready"], 2)
            with pool.Fori(RING, E1 - 1) as e:
                split_weights(e, (e + 2) % RING, e - RING)
                load_weights(e + 1)
            split_weights(E1 - 1, (E1 + 1) % RING, E1 - 1 - RING)
            for b in range(2):
                pool.wait_ge(s[f"output_stored{b}"], NT1 // 2 * 16)
            pool.wait_ge(s["yslots_ready"], 2)
            with pool.Fori(0, NGE // 2) as g:
                for k in range(2):
                    if k == 0:
                        pool.wait_ge(s["gather_used"], 2 * g + (B - 1))
                    else:
                        pool.wait_ge(s["gather_used"], 2 * g + B)
                    gather(bass.ds((2 * g + k) * GE, GE), GE, yg1, 2 * g + (B + k + 1), gE[:, k].rearrange("p j k d -> p (j k) d"), k, f"gathered{k}")

        @blk.vector
        def _(dve):
            v = nc.vector

            def layernorm(lk, src, dst, n, turn):
                alone(dve)
                for j in range(n):
                    i = v.bn_stats(st6[:, j, :], src[:, j, :])
                lk.then(i)
                alone(dve)
                for j in range(n):
                    i = v.bn_aggr(st2[:, j, :], st6[:, j, :])
                i.then_inc(s["var_ready"], 1)
                dve.wait_ge(s["rstd_ready"], turn)
                for j in range(n):
                    i = v.tensor_scalar(dst[:, j, :], src[:, j, :], st2[:, j, 0:1], rstd[:, j:j + 1], ALU.subtract, ALU.mult)
                return i

            def route(lk, g, n, E, turn, value, psR, psK):
                l_, k_, e_ = lb[:, 0:n, 0:E], key[:, 0:n, 0:E], ex[:, 0:n, 0:E]
                o_, ox = oh[:, 0:n, :, 0:E], ohx[:, 0:n, :, 0:E]
                bias = rb_bc if E == E0 else gbs
                dve.wait_ge(s["logits_ready"], turn)
                lk.then(v.tensor_tensor(l_, psR, bias[:, 0:E].unsqueeze(1).to_broadcast((P, n, E)), ALU.add))
                lg = psR if E == E0 else l_
                lk.then(v.tensor_reduce(lmx[:, 0:n], lg, AX, ALU.max))
                v.tensor_tensor(e_, lg, lmx[:, 0:n].unsqueeze(2).to_broadcast((P, n, E)), ALU.subtract).then_inc(s["dif_ready"], 1)
                if E == E1:
                    dve.wait_ge(s["ex_ready"], turn)
                    lk.then(v.tensor_reduce(den[:, 0:n], e_, AX, ALU.add))
                    lk.then(v.reciprocal(den[:, 0:n], den[:, 0:n]))
                    lk.then(v.tensor_tensor(k_, e_, den[:, 0:n].unsqueeze(2).to_broadcast((P, n, E)), ALU.mult))
                kk = l_ if E == E0 else k_
                alone(dve)
                for j in range(n):
                    i = v.max(v8[:, j, :], kk[:, j, :])
                lk.then(i)
                alone(dve)
                for j in range(n):
                    i = v.max_index(i8[:, j, :], v8[:, j, :], kk[:, j, :])
                lk.then(i)
                ig = idxf[:, bass.ds(g * n, n), :]
                alone(dve)
                lk.then(v.tensor_copy(ig, i8[:, 0:n, 0:2]))
                lk.then(v.tensor_tensor(o_, iota_f[:, 0:E].unsqueeze(1).unsqueeze(1).to_broadcast((P, n, 2, E)),
                                        ig.unsqueeze(3).to_broadcast((P, n, 2, E)), ALU.is_equal))
                v.tensor_tensor(mask[:, 0:n, 0:E], o_[:, :, 0, :], o_[:, :, 1, :], ALU.add).then_inc(s["mask_ready"], 1)
                if E == E0:
                    dve.wait_ge(s["ex_ready"], turn)
                w = e_ if E == E0 else k_
                lk.then(v.tensor_tensor(ox, o_, w.unsqueeze(2).to_broadcast((P, n, 2, E)), ALU.mult))
                lk.then(v.tensor_reduce(sel[:, 0:n, :], ox, AX, ALU.add))
                wg_ = wts[:, bass.ds(g * n, n), :]
                if E == E0:
                    lk.then(v.tensor_tensor(den[:, 0:n], sel[:, 0:n, 0], sel[:, 0:n, 1], ALU.add))
                    lk.then(v.reciprocal(den[:, 0:n], den[:, 0:n]))
                    lk.then(v.tensor_tensor(sel[:, 0:n, :], sel[:, 0:n, :], den[:, 0:n].unsqueeze(2).to_broadcast((P, n, 2)), ALU.mult))
                lk.then(v.tensor_scalar(wg_, sel[:, 0:n, :], tg[:, (2 if E == E0 else 3):(3 if E == E0 else 4)], None, ALU.mult))
                dve.wait_ge(s["rank_ready"], turn)
                c_ = cnt[:, 0:E]
                lk.then(v.tensor_tensor(rk[:, 0:n, 0:E], psK[:, 0:n, :], c_.unsqueeze(1).to_broadcast((P, n, E)), ALU.add))
                lk.then(v.tensor_tensor(c_, psK[:, n, :], c_, ALU.add))
                lk.then(v.tensor_tensor(ox, o_, rk[:, 0:n, 0:E].unsqueeze(2).to_broadcast((P, n, 2, E)), ALU.mult))
                sg = slotf[:, bass.ds(g * n, n), :]
                lk.then(v.tensor_reduce(sg, ox, AX, ALU.add))
                alone(dve)
                v.tensor_copy(slotu[:, 0:n, :], sg).then_inc(s["slots_ready"], 1)

            def tables(lk, E, NT):
                c_ = cnt[:, 0:E]
                v.tensor_scalar(ztail[:, 0:E], c_, iota_p[:, 0:1], None, ALU.add).then_inc(s["tails_ready"], 1)
                n_e, nt, end, off, dlt = (meta[:, k, 0:E] for k in range(5))
                lk.then(v.tensor_tensor(n_e, c_, base[E][:], ALU.subtract))
                NJ = TOK // P
                cmp = big1[:, 0:E * NJ].rearrange("p (e j) -> p e j", e=E)
                lk.then(v.tensor_scalar(tabf[:, 0:NJ, 0], iota_f[:, 0:NJ], float(P), None, ALU.mult))
                lk.then(v.tensor_tensor(cmp, n_e.unsqueeze(2).to_broadcast((P, E, NJ)),
                                        tabf[:, 0:NJ, 0].unsqueeze(1).to_broadcast((P, E, NJ)), ALU.is_gt))
                lk.then(v.tensor_reduce(nt, cmp, AX, ALU.add))
                le = big1[:, 0:E * E].rearrange("p (e f) -> p e f", e=E)
                lk.then(v.tensor_tensor(le, iota_f[:, 0:E].unsqueeze(2).to_broadcast((P, E, E)),
                                        iota_f[:, 0:E].unsqueeze(1).to_broadcast((P, E, E)), ALU.is_ge))
                lk.then(v.tensor_tensor(le, le, nt.unsqueeze(1).to_broadcast((P, E, E)), ALU.mult))
                lk.then(v.tensor_reduce(end, le, AX, ALU.add))
                lk.then(v.tensor_tensor(off, end, nt, ALU.subtract))
                ge = big1[:, 0:NT * E].rearrange("p (t e) -> p t e", e=E)
                lk.then(v.tensor_tensor(ge, iota_f[:, 0:NT].unsqueeze(2).to_broadcast((P, NT, E)),
                                        end.unsqueeze(1).to_broadcast((P, NT, E)), ALU.is_ge))
                lk.then(v.tensor_reduce(tabf[:, 0:NT, 0], ge, AX, ALU.add))
                lk.then(v.tensor_scalar(tabf[:, 0:NT, 0], tabf[:, 0:NT, 0], float(E - 1), None, ALU.min))
                lk.then(v.tensor_tensor(ge, ge, nt.unsqueeze(1).to_broadcast((P, NT, E)), ALU.mult))
                lk.then(v.tensor_reduce(tabf[:, 0:NT, 1], ge, AX, ALU.add))
                lk.then(v.tensor_tensor(tabf[:, 0:NT, 1], iota_f[:, 0:NT], tabf[:, 0:NT, 1], ALU.subtract))
                lk.then(v.tensor_scalar(tabf[:, 0:NT, 2], iota_f[:, 0:NT], end[:, E - 1:E], float(P), ALU.is_lt, ALU.mult))
                lk.then(v.tensor_tensor(tabf[:, 0:NT, 1], tabf[:, 0:NT, 1], tabf[:, 0:NT, 2], ALU.mult))
                lk.then(v.scalar_tensor_tensor(tabf[:, 0:NT, 1], tabf[:, 0:NT, 0], float(CAP), tabf[:, 0:NT, 1], ALU.mult, ALU.add))
                lk.then(v.scalar_tensor_tensor(dlt, off, float(P), base[E][:], ALU.mult, ALU.subtract))
                lk.then(v.tensor_scalar(tabf[:, 0:NT, 2], tabf[:, 0:NT, 0], 2.0, None, ALU.add))
                for _ in range(E1 // RING + 1):
                    lk.then(v.tensor_scalar(tabf[:, 0:NT, 3], tabf[:, 0:NT, 2], float(RING), -float(RING), ALU.is_ge, ALU.mult))
                    lk.then(v.tensor_tensor(tabf[:, 0:NT, 2], tabf[:, 0:NT, 2], tabf[:, 0:NT, 3], ALU.add))
                lk.then(v.tensor_copy(endi[0:1, 0:E], end[0:1, :]))
                v.tensor_copy(tab[0:1, 0:NT, :], tabf[0:1, 0:NT, 0:3]).then_inc(s["table_ready"], 1)
                bo = big1[:, 0:B * 2 * E].rearrange("p (b k e) -> p b k e", b=B, k=2)
                lk.then(v.tensor_tensor(bo, iota_f[:, 0:E].unsqueeze(1).unsqueeze(1).to_broadcast((P, B, 2, E)),
                                        idxf[:].unsqueeze(3).to_broadcast((P, B, 2, E)), ALU.is_equal))
                lk.then(v.tensor_tensor(bo, bo, dlt.unsqueeze(1).unsqueeze(1).to_broadcast((P, B, 2, E)), ALU.mult))
                lk.then(v.tensor_reduce(idxf[:], bo, AX, ALU.add))
                lk.then(v.tensor_tensor(slotf[:], slotf[:], idxf[:], ALU.add))
                v.tensor_copy(yslot[:], slotf[:]).then_inc(s["yslots_ready"], 1)

            dve.wait_ge(s["setup_pool"], 2)
            v.tensor_copy(tri[:], tri_f[:]).then_inc(s["setup_dve"], 1)
            v.tensor_copy(ones_b[:], ones[:]).then_inc(s["setup_dve"], 1)
            v.tensor_copy(iota_f[:], iota_i[:]).then_inc(s["setup_dve"], 1)
            v.tensor_copy(iota_p[:], iota_pi[:]).then_inc(s["setup_dve"], 1)
            dve.wait_ge(s["setup_dve"], 4)
            v.tensor_scalar(base[E0][:], iota_f[:, 0:E0], float(CAP), None, ALU.mult).then_inc(s["setup_dve"], 1)
            v.tensor_scalar(base[E1][:], iota_f[:, 0:E1], float(CAP), None, ALU.mult).then_inc(s["setup_dve"], 1)
            dve.wait_ge(s["setup_dve"], 6)
            v.tensor_copy(cnt[:], base[E0][:]).then_inc(s["setup_dve"], 1)
            dve.wait_ge(s["gb_t_ready"], 1)
            v.tensor_copy(gbT[:], ps[:, 7, 0:4 * LAT].rearrange("p (a c l) -> p a c l", a=2, c=KD)).then_inc(s["setup_dve"], 1)
            dve.wait_ge(s["tanh_done"], 1)
            v.tensor_tensor(tgg[:], tg[:, 1:2], gates[:, 4:5], ALU.mult).then_inc(s["setup_dve"], 1)
            v.memset(mask[:], 0.0).then_inc(s["setup_dve"], 1)
            dve.wait_ge(s["setup_dve"], 10)
            dve.sem_inc(s["x1_used"], 1)
            dve.sem_inc(s["x2_ready"], 1)
            lk = Steps(dve, s["vector_steps"])
            A_STEPS = 28
            with dve.Fori(0, NGA) as g:
                t1 = dve.snap(g + 1)
                lk.turn(g, A_STEPS)
                X = xs[:, bass.ds(g * GA, GA), :]
                dve.wait_ge(s["x_loaded"], dve.snap((g + 1) * 32))
                layernorm(lk, X, xl, GA, 3 * g + 1).then_inc(s["xl_ready"], 1)
                dve.wait_ge(s["phi_ready"], t1)
                v.tensor_scalar(phS[:], ps[0:LAT, 2:4, :].rearrange("p n (j d) -> p (n j) d", d=D), phb[:, 0:1], None, ALU.add).then_inc(s["phi_copied"], 1)
                dve.wait_ge(s["gt_ready"], t1)
                v.tensor_tensor(gS[:].rearrange("p j c l -> p (j c) l"), ps[:, 4, :].rearrange("p (n l) -> p n l", l=LAT),
                                gb_bc[:].unsqueeze(1).to_broadcast((P, GA * 2, LAT)), ALU.add).then_inc(s["gt_copied"], 1)
                for j in range(GA):
                    dve.wait_ge(s["scores_ready"], g * GA + (j + 1))
                    v.tensor_reduce(nm[:, j, :], ps[:, j, :].rearrange("p (c s) -> p c s", c=2), AX, ALU.max, negate=True).then_inc(s["max_ready"], 1)
                for j in range(0, GA, 2):
                    dve.wait_ge(s["pt_ready"], g * GA + (j + 1))
                    v.tensor_copy(Q2[:, j * 2 * D:(j + 1) * 2 * D], ps[:, j, :]).then_inc(s["pt_copied_v"], 1)
                dve.wait_ge(s["p_ready"], (g + 1) * GA * 2)
                lk.then(v.reciprocal(rrec[:], rsum[:]))
                dve.wait_ge(s["pv_ready"], t1)
                lk.then(v.tensor_tensor(tx[:], ps[:, 4, :].rearrange("p (j c l) -> p j c l", j=GA, c=2),
                                        rrec[:].unsqueeze(3).to_broadcast((P, GA, 2, LAT)), ALU.mult))
                v.tensor_reduce(sums[:, 0, :], tx[:].rearrange("p j c l -> p j (c l)"), AX, ALU.add)
                lk.then(v.tensor_tensor(txq[:], tx[:], tx[:], ALU.mult))
                v.tensor_reduce(sums[:, 1, :], txq[:].rearrange("p j c l -> p j (c l)"), AX, ALU.add).then_inc(s["sums_ready"], 1)
                dve.wait_ge(s["tot_ready"], t1)
                inv = 1.0 / (LAT * D)
                lk.then(v.tensor_scalar(mom[:, 0:2, :], ps[:, 5, 0:2 * GA].rearrange("p (a j) -> p a j", a=2), inv, None, ALU.mult))
                lk.then(v.tensor_tensor(mom[:, 2, :], mom[:, 0, :], mom[:, 0, :], ALU.mult))
                v.tensor_tensor(mom[:, 3, :], mom[:, 1, :], mom[:, 2, :], ALU.subtract).then_inc(s["var_ready"], 1)
                dve.wait_ge(s["rstd_ready"], 3 * g + 2)
                for j in range(GA):
                    i = v.tensor_scalar(tx[:, j, :, :], tx[:, j, :, :], mom[:, 0, j:j + 1], mom[:, 2, j:j + 1], ALU.subtract, ALU.mult)
                lk.then(i)
                lk.then(v.tensor_tensor(tx[:], tx[:], gbT[:, 0, :, :].unsqueeze(1).to_broadcast((P, GA, KD, LAT)), ALU.mult))
                v.tensor_tensor(tx[:], tx[:], gbT[:, 1, :, :].unsqueeze(1).to_broadcast((P, GA, KD, LAT)), ALU.add).then_inc(s["h_ready"], 1)
                dve.wait_ge(s["proj_ready"], t1)
                lk.then(v.scalar_tensor_tensor(tmp[:], ps[:, 0:2, :].rearrange("p n (j d) -> p (n j) d", d=D), ob[:, 0:1], cx[:], ALU.add, ALU.add))
                lk.then(v.scalar_tensor_tensor(X, tmp[:], tg[:, 0:1], X, ALU.mult, ALU.add))
                dve.sem_inc(s["x1_used"], 1)
                dve.wait_ge(s["xn_free"], t1)
                layernorm(lk, X, xn, GA, 3 * g + 3).then_inc(s["xn_ready"], 1)
                route(lk, g, GA, E0, t1, t1, ps[:, 4, 0:GA * E0].rearrange("p (j e) -> p j e", e=E0),
                      ps[:, 5, 0:(GA + 1) * E0].rearrange("p (j e) -> p j e", e=E0))
                for f in range(2):
                    dve.wait_ge(s["silu_ready"], 2 * g + (f + 1))
                    v.tensor_tensor(hs[:, f, :], hs[:, f, :], ps[:, 6 + f, :], ALU.mult).then_inc(s["hs_ready"], 1)
                dve.wait_ge(s["y_ready"], t1)
                lk.then(v.scalar_tensor_tensor(X, ps[:, 2:4, :].rearrange("p n (j d) -> p (n j) d", d=D), tg[:, 2:3], X, ALU.mult, ALU.add))
                dve.sem_inc(s["x2_ready"], 1)
            lk.end(NGA)
            lk.turn(0, 0)
            tables(lk, E0, NT0)
            lk.end(1)

            def b_copy(t, b):
                dve.wait_ge(s["tile_turned"], t + 1)
                v.tensor_copy(XTt[:, b, :], ps[:, b, 0:D]).then_inc(s["tile_copied"], 1)

            def b_h(t, b):
                dve.wait_ge(s["tile_silu"], t + 1)
                v.tensor_tensor(h0_t[:, b, :], su_t[:, b, :], ps[:, 2 + b, P:2 * P], ALU.mult).then_inc(s["tile_h"], 1)

            b_copy(0, 0)
            b_copy(1, 1)
            b_h(0, 0)
            with dve.Fori(0, (NT0 - 2) // 2) as i:
                for k in range(2):
                    b_copy(2 * i + (k + 2), k)
                    b_h(2 * i + (k + 1), 1 - k)
            b_h(NT0 - 1, 1)

            dve.wait_ge(s["tile_y"], NT0)
            v.tensor_copy(cnt[:, 0:E1], base[E1][:]).then_inc(s["setup_dve"], 1)
            v.memset(mask[:], 0.0).then_inc(s["setup_dve"], 1)
            v.memset(VT, 1.0).then_inc(s["setup_dve"], 1)
            v.memset(QK[:, 1, :].bitcast(F32), 1.0).then_inc(s["setup_dve"], 1)
            dve.wait_ge(s["setup_dve"], 14)
            dve.sem_inc(s["phase_done"], 1)
            PAIR = 16
            GATE = 2

            def item_rows(t):
                return xs[:, bass.ds(t, 1), :].rearrange("p a d -> p (a d)")

            def add_expert(t, b, x):
                return v.scalar_tensor_tensor(item_rows(t), gC[:, b, x, :], wts[:, bass.ds(t, 1), x:x + 1].rearrange("p a d -> p (a d)"),
                                              item_rows(t), ALU.mult, ALU.add)

            def c_turn(t, k):
                b = k % 2
                pair = k // 2 * 2
                gate = k % 2 == 1 and item(t - 3)
                choice = k % 2 == 0 and item(t - 4)
                E = E1
                if gate:
                    lk.turn((t - 3) // 2, PAIR)
                if choice:
                    lk.turn((t - 4) // 2, PAIR, GATE)
                l_, k_, e_, d_ = lb[:, 0:2, 0:E], key[:, 0:2, 0:E], ex[:, 0:2, 0:E], den[:, 0:2]
                o_, ox, c_, rk_ = oh[:, 0:2, :, 0:E], ohx[:, 0:2, :, 0:E], cnt[:, 0:E], rk[:, 0:2, 0:E]

                def head(h):
                    if item(t + 2):
                        dve.wait_ge(s["s_ready"], t * NH + (2 * NH + h + 1))
                        v.tensor_reduce(mraw[:, b, h, :], ps[:, h % 2, :].rearrange("p (c l) -> p c l", c=2), AX, ALU.max).then_inc(s["s_max"], 1)

                if item(t + 1):
                    dve.wait_ge(s["s_max"], t * NH + 2 * NH)
                    mr = mraw[:, 1 - b].rearrange("p a c -> p (a c)")
                    v.tensor_scalar(nmr[:, 0, :], mr, -1.0, None, ALU.mult).then_inc(s["m_high"], 1)
                if choice:
                    dve.wait_ge(s["ex_ready"], (t - 4) // 2 + (NGA + 1))
                    m_sum = lk.mark(v.tensor_reduce(d_, e_, AX, ALU.add))
                if item(t + 4):
                    dve.wait_ge(s[f"gathered{b}"], (t + 4) // 2 * 32 + 32)
                    add_expert(t + 4, b, 0).then_inc(s["row_sum0"], 1)
                head(0)
                if item(t + 1):
                    dve.wait_ge(s["m_high"], t + 2)
                    v.scalar_tensor_tensor(nmr[:, 1, :], mr, -1.0, nmr[:, 0, :].bitcast(F32), ALU.mult, ALU.subtract).then_inc(s["m_ready"], 1)
                if item(t + 4):
                    dve.wait_ge(s["row_sum0"], t + 5)
                    add_expert(t + 4, b, 1).then_inc(s["row_sum1"], 1)
                if choice:
                    dve.wait_ge(lk.sem, m_sum)
                    m_inverse = lk.mark(v.reciprocal(d_, d_))
                head(1)
                if item(t + 4):
                    dve.wait_ge(s["row_sum1"], t + 5)
                    dve.sem_inc(s["gather_used"], 1)
                    v.bn_stats(st6[:, 0, :], item_rows(t + 4)).then_inc(s["row_stats"], 1)
                if choice:
                    dve.wait_ge(lk.sem, m_inverse)
                    m_key = lk.mark(v.tensor_tensor(k_, e_, d_.unsqueeze(2).to_broadcast((P, 2, E)), ALU.mult))
                    dve.wait_ge(lk.sem, m_key)
                    alone(dve)
                    for j in range(2):
                        i = v.max(v8[:, j, :], key[:, j, 0:E])
                    m_max = lk.mark(i)
                head(2)
                if item(t + 4):
                    dve.wait_ge(s["row_stats"], t + 5)
                    alone(dve)
                    v.bn_aggr(st2[:, 0, :], st6[:, 0, :]).then_inc(s["var_ready"], 1)
                if item(t - 1):
                    dve.wait_ge(s["o_turned"], t)
                    o6 = ps[:, 6, :].rearrange("p (c h e) -> p c h e", c=2, h=NH)
                    v.reciprocal(orec, o6[:, :, :, DH]).then_inc(s["o_inverse"], 1)
                    dve.wait_ge(s["o_inverse"], t)
                    v.tensor_tensor(oN.rearrange("p (c h d) -> p c h d", c=2, h=NH), o6[:, :, :, 0:DH],
                                    orec.unsqueeze(3).to_broadcast((P, 2, NH, DH)), ALU.mult).then_inc(s["o_norm"], 1)
                if choice:
                    dve.wait_ge(lk.sem, m_max)
                    alone(dve)
                    for j in range(2):
                        i = v.max_index(i8[:, j, :], v8[:, j, :], key[:, j, 0:E])
                    m_index = lk.mark(i)
                head(3)
                if choice:
                    dve.wait_ge(lk.sem, m_index)
                    alone(dve)
                    ig = idxf[:, bass.ds(t - 4, 2), :]
                    m_choice = lk.mark(v.tensor_copy(ig, i8[:, 0:2, 0:2]))
                head(4)
                if item(t - 1):
                    dve.wait_ge(s["ot_ready"], t)
                    v.scalar_tensor_tensor(item_rows(t - 1), ps[:, 6, 0:D], tgg[:, 0:1], item_rows(t - 1), ALU.mult, ALU.add).then_inc(s["x_sum"], 1)
                if choice:
                    dve.wait_ge(lk.sem, m_choice)
                    m_hot = lk.mark(v.tensor_tensor(o_, iota_f[:, 0:E].unsqueeze(1).unsqueeze(1).to_broadcast((P, 2, 2, E)),
                                                    ig.unsqueeze(3).to_broadcast((P, 2, 2, E)), ALU.is_equal))
                if item(t + 4):
                    dve.wait_ge(s["rstd_ready"], t + (3 * NGA + 5))
                    v.tensor_scalar(xl[:, b, :], item_rows(t + 4), st2[:, 0, 0:1], rstd[:, 0:1], ALU.subtract, ALU.mult).then_inc(s["xl_ready"], 1)
                head(5)
                if item(t - 1):
                    dve.wait_ge(s["x_sum"], t)
                    alone(dve)
                    v.bn_stats(st6[:, 1, :], item_rows(t - 1)).then_inc(s["x_stats"], 1)
                if choice:
                    dve.wait_ge(lk.sem, m_hot)
                    v.tensor_tensor(mask[:, 0:2, 0:E], o_[:, :, 0, :], o_[:, :, 1, :], ALU.add).then_inc(s["mask_ready"], 1)
                    m_weighed = lk.mark(v.tensor_tensor(ox, o_, k_.unsqueeze(2).to_broadcast((P, 2, 2, E)), ALU.mult))
                if gate:
                    dve.wait_ge(s["logits_ready"], (t - 3) // 2 + (NGA + 1))
                    m_logits = lk.mark(v.tensor_tensor(l_, ps[:, 7, 0:2 * E].rearrange("p (j e) -> p j e", e=E),
                                                       gbs[:, 0:E].unsqueeze(1).to_broadcast((P, 2, E)), ALU.add))
                head(6)
                if item(t - 1):
                    dve.wait_ge(s["x_stats"], t)
                    alone(dve)
                    v.bn_aggr(st2[:, 1, :], st6[:, 1, :]).then_inc(s["x_var"], 1)
                if gate:
                    dve.wait_ge(lk.sem, m_logits)
                    m_largest = lk.mark(v.tensor_reduce(lmx[:, 0:2], l_, AX, ALU.max))
                if item(t + 4):
                    dve.wait_ge(s["q_high"], t + 5)
                    v.tensor_tensor(split[:, b, 1, :], xl[:, b, :], split[:, b, 0, :].bitcast(F32), ALU.subtract).then_inc(s["q_ready"], 1)
                if choice:
                    dve.wait_ge(lk.sem, m_weighed)
                    m_sel = lk.mark(v.tensor_reduce(sel[:, 0:2, :], ox, AX, ALU.add))
                head(7)
                if gate:
                    dve.wait_ge(lk.sem, m_largest)
                    v.tensor_tensor(e_, l_, lmx[:, 0:2].unsqueeze(2).to_broadcast((P, 2, E)), ALU.subtract).then_inc(s["dif_ready"], 1)
                    assert lk.k == GATE
                if choice:
                    dve.wait_ge(s["rank_ready"], (t - 4) // 2 + (NGA + 1))
                    psK = ps[:, 7, 0:3 * E].rearrange("p (j e) -> p j e", e=E)
                    m_rank = lk.mark(v.tensor_tensor(rk_, psK[:, 0:2, :], c_.unsqueeze(1).to_broadcast((P, 2, E)), ALU.add))
                    dve.wait_ge(lk.sem, m_sel)
                    m_wts = lk.mark(v.tensor_scalar(wts[:, bass.ds(t - 4, 2), :], sel[:, 0:2, :], tg[:, 3:4], None, ALU.mult))
                    dve.wait_ge(lk.sem, m_rank)
                    m_count = lk.mark(v.tensor_tensor(c_, psK[:, 2, :], c_, ALU.add))
                    m_row = lk.mark(v.tensor_tensor(ox, o_, rk_.unsqueeze(2).to_broadcast((P, 2, 2, E)), ALU.mult))
                if item(t - 1):
                    r_ = t - 1
                    dve.wait_ge(s["x_rstd"], t)
                    if not isinstance(t, int) or r_ >= NC:
                        dve.wait_ge(s[f"scattered{((k - 1) % NC) // 2}"], r_ // NC * 64)
                    else:
                        dve.wait_ge(s["xn_free"], NGA + 1)
                    v.tensor_scalar(xn[:, (k - 1) % NC, :], item_rows(r_), st2[:, 1, 0:1], rstd[:, 1:2], ALU.subtract, ALU.mult).then_inc(s["xn_ready"], 1)
                if choice:
                    dve.wait_ge(lk.sem, m_row)
                    sg = slotf[:, bass.ds(t - 4, 2), :]
                    m_slot = lk.mark(v.tensor_reduce(sg, ox, AX, ALU.add))
                    dve.wait_ge(lk.sem, m_slot)
                    alone(dve)
                    v.tensor_copy(slotu[:, k:k + 2, :], sg).then_inc(s["slots_ready"], 1)
                if choice:
                    assert lk.k == PAIR

            item_turns(dve, c_turn)
            lk.before += B // 2 * PAIR
            lk.turn(0, 0)
            tables(lk, E1, NT1)

            def d_split(src, parts, ready, copied, done, value):
                dve.wait_ge(s[ready], value[0])
                v.tensor_copy(parts[0], src).then_inc(s[copied], 1)
                dve.wait_ge(s[copied], value[1])
                v.tensor_tensor(parts[1], src, parts[0].bitcast(F32), ALU.subtract).then_inc(s[done], 1)

            def d_turn(t, k):
                if is_tile(t + 1):
                    d_split(Ha, (Hap[:, 0], Hap[:, 1]), "l1_h1_gelu", "h1_high", "l1_h1_split", (KH * (t + 2), t + 2))
                if is_tile(t):
                    if is_tile(t - 1):
                        dve.wait_ge(s["tile_y"], NT0 + t)
                    d_split(Hb, (Hbp[:, 0], Hbp[:, 1]), "l1_h2_gelu", "h2_high", "l1_h2_split", (KH * (t + 1), t + 1))
                if is_tile(t + 3):
                    d_split(ps[:, (k + 1) % 2, 0:D], (XTp[:, 0], XTp[:, 1]), "tile_turned", "x_high", "tile_copied",
                            (NT0 + t + 4, t + 4))
                if is_tile(t - 1):
                    b = (k + 1) % 2
                    e = dve.value_load(tab[0:1, t - 1, 0:1], min_val=0, max_val=E1 - 1)
                    dve.wait_ge(s["tile_y"], NT0 + t)
                    if is_tile(t - 3):
                        dve.wait_ge(s[f"output_stored{b}"], ((t - 1) // 2) * 16)
                    v.tensor_tensor(Yt[:, b, :], ps[:, 6 + b, 0:D], b3bc[:, bass.ds(e, 1), :].rearrange("p a d -> p (a d)"),
                                    ALU.add).then_inc(s["tile_out"], 1)

            dve.wait_ge(s["w1_loaded"], 16 * 3)
            tile_turns(dve, d_turn)

            with dve.Fori(0, NGE // 2) as g2:
                for m in range(2):
                    g = 2 * g2 + m
                    dve.wait_ge(s[f"gathered{m}"], g2 * (GE * 2 * 16) + (B // 2 * 32 + GE * 2 * 16))
                    for k in range(2):
                        for j in range(GE):
                            xj = xs[:, bass.ds(g * GE + j, 1), :].rearrange("p a d -> p (a d)")
                            i = v.scalar_tensor_tensor(xj, gE[:, m, j, k, :], wts[:, bass.ds(g * GE + j, 1), k:k + 1].rearrange("p a d -> p (a d)"),
                                                       xj, ALU.mult, ALU.add)
                        i.then_inc(s["out_summed"], 1)
                        dve.wait_ge(s["out_summed"], 2 * g + (k + 1))
                    dve.sem_inc(s["gather_used"], 1)
                    dve.sem_inc(s["out_ready"], 1)

        @blk.scalar
        def _(act):
            a = nc.scalar
            act.wait_ge(s["consts_loaded"], 16 * N_CONST)
            a.activation(tg[:], gates[:, 0:4], ACT.Tanh).then_inc(s["tanh_done"], 1)

            def routing_side(n, E, turn):
                act.wait_ge(s["xnt_ready"], turn)
                if E == E0:
                    a.copy(xT[:], ps[:, 2:4, :]).then_inc(s["xnt_copied"], 1)
                else:
                    a.copy(xT[:, :, 0:n * P], ps[:, 6, :].rearrange("p (k t) -> p k t", k=KD)).then_inc(s["xnt_copied"], 1)
                act.wait_ge(s["dif_ready"], turn)
                a.activation(ex[:, 0:n, 0:E], ex[:, 0:n, 0:E], ACT.Exp).then_inc(s["ex_ready"], 1)

            with act.Fori(0, NGA) as g:
                t1 = act.snap(g + 1)
                act.wait_ge(s["theta_ready"], t1)
                a.activation(thS[:], ps[0:LAT, 0:2, :].rearrange("p n (j d) -> p (n j) d", d=D), ACT.Identity, bias=thb[:, 0:1]).then_inc(s["theta_copied"], 1)
                for j in range(GA):
                    act.wait_ge(s["max_ready"], g * GA + (j + 1))
                    for c in range(2):
                        a.activation(Pm[:, j, c, :], ps[:, j, c * D:(c + 1) * D], ACT.Exp, bias=nm[:, j, c:c + 1],
                                     accum_out=rsum[:, j, c:c + 1]).then_inc(s["p_ready"], 1)
                for j in range(1, GA, 2):
                    act.wait_ge(s["pt_ready"], g * GA + (j + 1))
                    a.copy(PTm[:, j].rearrange("p c t -> p (c t)"), ps[:, j, :]).then_inc(s["pt_copied_a"], 1)
                act.wait_ge(s["ht_ready"], t1)
                a.activation(hS[:], ps[0:LAT, 6:8, :].rearrange("p n (j d) -> p (n j) d", d=D), ACT.Relu).then_inc(s["ht_copied"], 1)
                routing_side(GA, E0, t1)
                for f in range(2):
                    act.wait_ge(s["u_ready"], 2 * g + (f + 1))
                    a.activation(hs[:, f, :], ps[:, f, :], ACT.Silu).then_inc(s["silu_ready"], 1)

            def silu(t, b):
                act.wait_ge(s["ug_ready"], t + 1)
                a.activation(su_t[:, b, :], ps[:, 2 + b, 0:P], ACT.Silu).then_inc(s["tile_silu"], 1)

            def tile_out(t, b, i):
                act.wait_ge(s["tile_y"], t + 1)
                if i is not None:
                    act.wait_ge(s[f"tile_stored{b}"], i * 16)
                a.copy(Yt[:, b, :], ps[:, 4 + b, 0:D]).then_inc(s["tile_out"], 1)

            def hidden_out(t, b):
                act.wait_ge(s["tile_ht"], t + 1)
                a.copy(h0T[:, b, :], ps[:, 6 + b, 0:P]).then_inc(s["tile_ht_copied"], 1)

            silu(0, 0)
            for k in range(2):
                hidden_out(k, k)
                silu(k + 1, 1 - k)
                tile_out(k, k, None)
            with act.Fori(1, (NT0 - 2) // 2) as i:
                for k in range(2):
                    hidden_out(2 * i + k, k)
                    silu(2 * i + (k + 1), 1 - k)
                    tile_out(2 * i + k, k, i)
            hidden_out(NT0 - 2, 0)
            silu(NT0 - 1, 1)
            tile_out(NT0 - 2, 0, NT0 // 2 - 1)
            hidden_out(NT0 - 1, 1)
            tile_out(NT0 - 1, 1, NT0 // 2 - 1)

            def c_act_turn(t, k):
                b = k % 2
                if item(t - 1):
                    act.wait_ge(s["o_ready"], t)
                    a.copy(oU, ps[:, 4 + (1 - b), :]).then_inc(s["o_copied"], 1)
                for h in range(NH):
                    if item(t):
                        act.wait_ge(s["st_ready"], t * NH + (h + 1))
                        a.activation(PTb[:, h % 4].rearrange("p c q -> p (c q)"), ps[:, 2 + h % 2, :], ACT.Exp,
                                     scale=DH ** -0.5).then_inc(s["st_exp"], 1)
                    if h == 0 and item(t - 2):
                        n = (k + 2) % NC
                        act.wait_ge(s["xnt_ready"], t + (NGA - 1))
                        a.copy(xT[:, :, n * P:(n + 1) * P], ps[:, 7, 0:D].rearrange("p (k t) -> p k t", k=KD)).then_inc(s["xnt_copied"], 1)
                    if h == 3 and item(t + 1):
                        if item(t):
                            act.wait_ge(s["m_stacked"], t * 32 + 32)
                        act.wait_ge(s["vt_ready"], t + 2)
                        a.copy(mT[:], ps[0:2 * 2 * NH, 7, D:D + P]).then_inc(s["mt_copied"], 1)
                        a.copy(VT[:, 1 - b, :, :, 0:DH], ps[:, 7, 0:D].rearrange("p (c h d) -> p c h d", c=2, h=NH)).then_inc(s["vt_copied"], 1)
                    if h == 5 and item(t + 4):
                        if item(t + 2):
                            act.wait_ge(s[f"q_stored{b}"], (t + 4) // 2 * 32)
                        act.wait_ge(s["xl_ready"], t + (NGA + 5))
                        a.copy(split[:, b, 0, :], xl[:, b, :]).then_inc(s["q_high"], 1)
                    if h == NH - 1 and k % 2 == 1 and item(t - 3):
                        act.wait_ge(s["dif_ready"], (t - 3) // 2 + (NGA + 1))
                        a.activation(ex[:, 0:2, 0:E1], ex[:, 0:2, 0:E1], ACT.Exp).then_inc(s["ex_ready"], 1)

            item_turns(act, c_act_turn)

            def gelu(t, which):
                e = act.value_load(tab[0:1, t, 0:1], min_val=0, max_val=E1 - 1)
                bank, dst, bias = (3, Ha, b1T) if which == 1 else (5, Hb, b2T)
                if which == 2 and is_tile(t - 1):
                    act.wait_ge(s["l1_h2_split"], t)
                act.wait_ge(s[f"l1_h{which}_turned"], t + 1)
                for f in range(KH):
                    a.activation(dst[:, f, :], ps[:, bank, f * P:(f + 1) * P], ACT.Gelu,
                                 bias=bias[:, bass.ds(e, 1), f:f + 1].rearrange("p a b -> p (a b)")).then_inc(s[f"l1_h{which}_gelu"], 1)

            def copy(t, which):
                pre, bank = (pre1, 2) if which == 1 else (pre2, 4)
                act.wait_ge(s[f"l1_h{which}_ready"], t + 1)
                a.copy(pre, ps[:, bank, :]).then_inc(s[f"l1_h{which}_copied"], 1)

            def a_turn(t, k):
                if is_tile(t - 2):
                    act.wait_ge(s["tile_out"], NT0 + t - 1)
                    alone(act)
                    act.dma_start(yg1[bass.ds((t - 2) * P, P), :], Yt[:, k % 2, :]).then_inc(s[f"output_stored{k % 2}"], 16)
                if is_tile(t + 1):
                    gelu(t + 1, 1)
                if is_tile(t + 2):
                    copy(t + 2, 1)
                if is_tile(t):
                    gelu(t, 2)
                if is_tile(t + 1):
                    copy(t + 1, 2)

            act.wait_ge(s["w1_loaded"], 16 * 3)
            act.wait_ge(s["table_ready"], 2)
            tile_turns(act, a_turn)

        @blk.tensor
        def _(pe):
            mm, tr = nc.tensor.matmul, nc.tensor.transpose
            pe.wait_ge(s["setup_pool"], 2)
            pe.wait_ge(s["consts_loaded"], 16 * N_CONST)
            for q in range(2):
                for c in range(KD):
                    o = (q * 2 + c) * LAT
                    i = tr(ps[:, 7, o:o + LAT], gam_n[:, q, c * P:(c + 1) * P], ident[0:LAT, 0:LAT])
            i.then_inc(s["gb_t_ready"], 1)
            pe.wait_ge(s["setup_dve"], 10)

            def ranks(n, E, turn):
                pe.wait_ge(s["xnt_copied"], turn)
                bank, w = (4, rw) if E == E0 else (7, gwt)
                for j in range(n):
                    for k in range(KD):
                        i = mm(ps[:, bank, j * E:(j + 1) * E], xT[:, k, j * P:(j + 1) * P], w[:, k, :], start=(k == 0), stop=(k == KD - 1))
                i.then_inc(s["logits_ready"], 1)
                count_ranks(n, E, 5, turn)

            def count_ranks(n, E, bank, turn):
                pe.wait_ge(s["mask_ready"], turn)
                r = ps[:, bank, 0:(n + 1) * E].rearrange("p (j e) -> p j e", e=E)
                mm(r, tri[:], mask[:, 0:n + 1, 0:E], start=True, stop=False)
                for j in range(n):
                    i = mm(r[:, j + 1:n + 1, :], ones_b[:], mask[:, j, 0:E].unsqueeze(1).to_broadcast((P, n - j, E)),
                           start=False, stop=(j == n - 1))
                i.then_inc(s["rank_ready"], 1)

            with pe.Fori(0, NGA) as g:
                t1 = pe.snap(g + 1)
                pe.wait_ge(s["x_loaded"], (g + 1) * 32)
                pe.wait_ge(s["x2_ready"], t1)
                for q in range(2):
                    i = mm(ps[0:LAT, q, :], thw[:], cx[:, 2 * q:2 * q + 2, :], start=True, stop=True)
                i.then_inc(s["theta_ready"], 1)
                pe.wait_ge(s["xl_ready"], t1)
                for q in range(2):
                    i = mm(ps[0:LAT, 2 + q, :], phw[:], xl[:, 2 * q:2 * q + 2, :], start=True, stop=True)
                i.then_inc(s["phi_ready"], 1)
                for j in range(GA):
                    for c in range(2):
                        o = (j * 2 + c) * LAT
                        i = mm(ps[:, 4, o:o + LAT], xl[:, j, c * P:(c + 1) * P], gw[:], start=True, stop=True)
                i.then_inc(s["gt_ready"], 1)
                pe.wait_ge(s["theta_copied"], t1)
                pe.wait_ge(s["phi_copied"], t1)
                for j in range(GA):
                    for c in range(2):
                        i = mm(ps[:, j, c * D:(c + 1) * D], thS[:, j, c * P:(c + 1) * P], phS[:, j, :], start=True, stop=True)
                    i.then_inc(s["scores_ready"], 1)
                for j in range(GA):
                    pe.wait_ge(s["p_ready"], g * (GA * 2) + (2 * j + 2))
                    for sc in range(2):
                        for c in range(2):
                            o = sc * D + c * P
                            i = tr(ps[:, j, o:o + P], Pm[:, j, c, sc * P:(sc + 1) * P], ident[:])
                    i.then_inc(s["pt_ready"], 1)
                pe.wait_ge(s["pt_copied_v"], (g + 1) * 2)
                pe.wait_ge(s["pt_copied_a"], (g + 1) * 2)
                pe.wait_ge(s["gt_copied"], t1)
                for j in range(GA):
                    for c in range(2):
                        o = (j * 2 + c) * LAT
                        for sc in range(2):
                            i = mm(ps[:, 4, o:o + LAT], PTm[:, j, sc, c * P:(c + 1) * P], gS[:, j, sc, :], start=(sc == 0), stop=(sc == 1))
                i.then_inc(s["pv_ready"], 1)
                pe.wait_ge(s["sums_ready"], t1)
                mm(ps[:, 5, 0:2 * GA], ones[:], sums[:].rearrange("p a j -> p (a j)"), start=True, stop=True).then_inc(s["tot_ready"], 1)
                pe.wait_ge(s["h_ready"], t1)
                alone(pe)
                for j in range(GA):
                    for c in range(2):
                        o = (j % 2) * D + c * P
                        i = tr(ps[0:LAT, 6 + j // 2, o:o + P], tx[:, j, c, :], ident[:])
                i.then_inc(s["ht_ready"], 1)
                pe.wait_ge(s["ht_copied"], t1)
                for q in range(2):
                    i = mm(ps[:, q, :], ow[:], hS[:, 2 * q:2 * q + 2, :], start=True, stop=True)
                i.then_inc(s["proj_ready"], 1)
                pe.wait_ge(s["xn_ready"], t1)
                for k in range(KD):
                    for j in range(GA):
                        i = tr(ps[:, 2 + k, j * P:(j + 1) * P], xn[:, j, k * P:(k + 1) * P], ident[:])
                i.then_inc(s["xnt_ready"], 1)
                ranks(GA, E0, t1)
                pe.wait_ge(s["w0_loaded"], 8 * 16)
                for f in range(2):
                    for w, bank in ((Sus, f), (Sgs, 6 + f)):
                        for k in range(KD):
                            i = mm(ps[:, bank, :], w[:, k, f * P:(f + 1) * P], xT[:, k, :], start=(k == 0), stop=(k == KD - 1))
                    i.then_inc(s["u_ready"], 1)
                pe.wait_ge(s["hs_ready"], 2 * (g + 1))
                for j in range(GA):
                    for f in range(2):
                        o = (j % 2) * D
                        i = mm(ps[:, 2 + j // 2, o:o + D], hs[:, f, j * P:(j + 1) * P], Sds[:, f, :], start=(f == 0), stop=(f == 1))
                i.then_inc(s["y_ready"], 1)

            def turn_tile(t, x, b, before, loads):
                pe.wait_ge(s[f"tile_loaded{x}"], loads * 16)
                for k in range(KD):
                    i = tr(ps[:, b, k * P:(k + 1) * P], Xin[:, x, k * P:(k + 1) * P], ident[:])
                i.then_inc(s["tile_turned"], 1)

            def expert0(t):
                return pe.value_load(tab[0:1, t, 0:1], min_val=0, max_val=E0 - 1)

            def up_gate(t, b):
                e = expert0(t)
                pe.wait_ge(s["tile_copied"], t + 1)
                for k in range(KD):
                    i = mm(ps[:, 2 + b, 0:2 * F0], XTt[:, b, k * P:(k + 1) * P],
                           Wug[:, bass.ds(e, 1), k, :, :].rearrange("p x a f -> p (x a f)"), start=(k == 0), stop=(k == KD - 1))
                i.then_inc(s["ug_ready"], 1)

            def turn_hidden(t, b):
                pe.wait_ge(s["tile_h"], t + 1)
                tr(ps[:, 6 + b, 0:P], h0_t[:, b, :], ident[:]).then_inc(s["tile_ht"], 1)

            def down(t, b):
                e = expert0(t)
                pe.wait_ge(s["tile_ht_copied"], t + 1)
                mm(ps[:, 4 + b, 0:D], h0T[:, b, :], Wds[:, bass.ds(e, 1), :].rearrange("p a d -> p (a d)"),
                   start=True, stop=True).then_inc(s["tile_y"], 1)

            pe.wait_ge(s["table_ready"], 1)
            turn_tile(0, 0, 0, 0, 1)
            turn_tile(1, 1, 1, 0, 1)
            up_gate(0, 0)

            def b_turn(t, k, loads):
                turn_hidden(t, k % 2)
                if loads is not None:
                    turn_tile(t + 2, (k + 2) % NX, k % 2, 0, loads)
                up_gate(t + 1, (k + 1) % 2)
                down(t, k % 2)

            with pe.Fori(0, NT0 // NX - 1) as i4:
                for k in range(NX):
                    b_turn(NX * i4 + k, k, i4 + (1 if k < 2 else 2))
            for t in range(NT0 - NX, NT0 - 1):
                b_turn(t, t % NX, NT0 // NX if t < NT0 - 2 else None)
            turn_hidden(NT0 - 1, 1)
            down(NT0 - 1, 1)

            pe.wait_ge(s["phase_done"], 1)

            def c_pe_turn(t, k):
                b = k % 2
                if item(t - 2):
                    n = (k + 2) % NC
                    pe.wait_ge(s["xn_ready"], t + (NGA - 1))
                    for x in range(KD):
                        i = tr(ps[:, 7, x * P:(x + 1) * P], xn[:, n, x * P:(x + 1) * P], ident[:])
                    i.then_inc(s["xnt_ready"], 1)
                for h in range(NH + 1):
                    if h < NH and item(t + 2):
                        n = (k + 2) % NC
                        if h == 0:
                            pe.wait_ge(s[f"k_stacked{b}"], (t + 2) // 2 * 48 + 48)
                            pe.wait_ge(s[f"q_stacked{b}"], (t + 2) // 2 * 48 + 48)
                        if h >= 2 or item(t + 1):
                            pe.wait_ge(s["s_max"], t * NH + (2 * NH + h - 1))
                        for c in range(2):
                            i = mm(ps[:, h % 2, c * D:(c + 1) * D], QS[0:NK, n, h, c * P:(c + 1) * P], KS[0:NK, n, h, :], start=True, stop=True)
                        i.then_inc(s["s_ready"], 1)
                    if h < NH and item(t):
                        if h == 0:
                            pe.wait_ge(s["m_stacked"], t * 32 + 32)
                        if h >= 2 or item(t - 1):
                            pe.wait_ge(s["st_exp"], t * NH + (h - 1))
                        for c in range(2):
                            i = mm(ps[:, 2 + h % 2, c * D:(c + 1) * D], KS[0:NK + 2, k, h, c * P:(c + 1) * P], QS[0:NK + 2, k, h, :], start=True, stop=True)
                        i.then_inc(s["st_ready"], 1)
                    if h > 0 and h % 2 == 0 and item(t):
                        if h == 2:
                            pe.wait_ge(s["vt_copied"], t + 1)
                            if item(t - 2):
                                pe.wait_ge(s["o_copied"], t - 1)
                        pe.wait_ge(s["st_exp"], t * NH + h)
                        for lc in range(2):
                            for v_h in (h - 2, h - 1):
                                p_, o = v_h % 4 * VE, v_h // 4 * D
                                i = mm(ps[p_:p_ + VE, 4 + b, o:o + D], VT[:, b, lc, v_h, :], PTb[:, v_h % 4, lc, :],
                                       start=(lc == 0), stop=(lc == 1))
                        if h == NH:
                            i.then_inc(s["o_ready"], 1)
                    if h == 1 and item(t - 1):
                        pe.wait_ge(s["o_copied"], t)
                        if item(t - 2):
                            pe.wait_ge(s["x_sum"], t - 1)
                        for c in range(2):
                            for q in range(2):
                                o = (c * 2 + q) * P
                                i = tr(ps[:, 6, o:o + P], oU[:, q * D + c * P:q * D + (c + 1) * P], ident[:])
                        i.then_inc(s["o_turned"], 1)
                    if h == 2 and item(t + 1):
                        if item(t - 2):
                            pe.wait_ge(s["xnt_copied"], t + (NGA - 1))
                        elif item(t):
                            pe.wait_ge(s["vt_copied"], t + 1)
                        pe.wait_ge(s["m_ready"], t + 2)
                        alone(pe)
                        tr(ps[0:2 * 2 * NH, 7, D:D + P], nmr[:].bitcast(F32).rearrange("p t a -> p (t a)"), ident[:])
                        n = (k + 1) % NC
                        pe.wait_ge(s[f"v_loaded{1 - b}"], (t + 1) // 2 * 16 + 16)
                        for c in range(2):
                            i = tr(ps[:, 7, c * P:(c + 1) * P], cx[:, n, c * P:(c + 1) * P], ident[:])
                        i.then_inc(s["vt_ready"], 1)
                    if h == 4 and k % 2 == 1 and item(t - 3):
                        pe.wait_ge(s["xnt_copied"], t + (NGA - 1))
                        if item(t + 1):
                            pe.wait_ge(s["vt_copied"], t + 2)
                        pe.wait_ge(s["slots_ready"], (t - 3) // 2 + NGA)
                        for j in range(2):
                            n = ((k + 1) % NC + j) * P
                            for x in range(KD):
                                i = mm(ps[:, 7, j * E1:(j + 1) * E1], xT[:, x, n:n + P], gwt[:, x, :], start=(x == 0), stop=(x == KD - 1))
                        i.then_inc(s["logits_ready"], 1)
                    if h == 3 and item(t - 1):
                        pe.wait_ge(s["o_norm"], t)
                        for c in range(2):
                            i = tr(ps[:, 6, c * P:(c + 1) * P], oN[:, c * P:(c + 1) * P], ident[:])
                        i.then_inc(s["ot_ready"], 1)
                    if h == 7 and k % 2 == 0 and item(t - 4):
                        if item(t + 1):
                            pe.wait_ge(s["vt_copied"], t + 2)
                        elif item(t - 2):
                            pe.wait_ge(s["xnt_copied"], t + (NGA - 1))
                        count_ranks(2, E1, 7, (t - 4) // 2 + (NGA + 1))

            item_turns(pe, c_pe_turn)

            def product(out, parts, n_k, place, at, width):
                i = None
                for k in range(n_k):
                    for x_part, w_part in ((0, 0), (1, 0), (0, 1)):
                        i = mm(out, parts(x_part, k), WR[:, bass.ds(place * (2 * WX) + (w_part * WX + at + k * width), width)],
                               start=(k == 0 and x_part == 0 and w_part == 0), stop=(k == n_k - 1 and w_part == 1))
                return i

            def weights(t):
                e = pe.value_load(tab[0:1, t, 0:1], min_val=0, max_val=E1 - 1)
                place = pe.value_load(tab[0:1, t, 2:3], min_val=0, max_val=RING - 1)
                pe.wait_ge(s["w_split"], e + 1)
                return place

            def hidden1(t):
                place = weights(t)
                pe.wait_ge(s["tile_copied"], NT0 + t + 1)
                product(ps[:, 2, :], lambda part, k: XTp[:, part, k * P:(k + 1) * P], KD, place, 0, H1).then_inc(s["l1_h1_ready"], 1)

            def hidden2(t):
                place = weights(t)
                pe.wait_ge(s["l1_h1_split"], t + 1)
                product(ps[:, 4, :], lambda part, k: Hap[:, part, k, :], KH, place, KD * H1, H1).then_inc(s["l1_h2_ready"], 1)

            def hidden3(t, b):
                place = weights(t)
                pe.wait_ge(s["l1_h2_split"], t + 1)
                product(ps[:, 6 + b, 0:D], lambda part, k: Hbp[:, part, k, :], KH, place, (KD + KH) * H1, D).then_inc(s["tile_y"], 1)

            def turn_pre(t, which):
                pre, bank = (pre1, 3) if which == 1 else (pre2, 5)
                pe.wait_ge(s[f"l1_h{which}_copied"], t + 1)
                for f in range(KH):
                    i = tr(ps[:, bank, f * P:(f + 1) * P], pre[:, f * P:(f + 1) * P], ident[:])
                i.then_inc(s[f"l1_h{which}_turned"], 1)

            def p_turn(t, k):
                if is_tile(t + 1):
                    turn_pre(t + 1, 1)
                if is_tile(t + 2):
                    hidden1(t + 2)
                if is_tile(t + 3):
                    turn_tile(t + 3, (k + 3) % NX, (k + 1) % 2, NT0, loads1(t + 3, k))
                if is_tile(t):
                    turn_pre(t, 2)
                if is_tile(t - 1):
                    hidden3(t - 1, (k + 1) % 2)
                if is_tile(t + 1):
                    hidden2(t + 1)

            def loads1(t, k):
                return NT0 // NX + t // NX + 1

            pe.wait_ge(s["table_ready"], 2)
            tile_turns(pe, p_turn)




def kernel(**inputs):
    import numpy as _np
    import concourse.bacc as _bacc
    from concourse import mybir as _mybir
    from concourse.bass_utils import run_bass_kernel_spmd as _run

    i = {k: _np.asarray(v) for k, v in inputs.items()}

    def by_feature(b):
        return b.reshape(b.shape[0], -1, P).transpose(2, 0, 1)

    arrays = {
        "x": i["x"], "ctx": i["ctx_2048"], "g_xattn": i["g_xattn"], "g_ffn": i["g_ffn"],
        "theta_wT": i["L0_xattn_theta_w"].T, "theta_b": i["L0_xattn_theta_b"],
        "phi_wT": i["L0_xattn_phi_w"].T, "phi_b": i["L0_xattn_phi_b"],
        "g_wT": i["L0_xattn_g_w"].T, "g_b": i["L0_xattn_g_b"],
        "ln_gamma": i["L0_xattn_ln_gamma"], "ln_beta": i["L0_xattn_ln_beta"],
        "out_wT": i["L0_xattn_out_w"].T, "out_b": i["L0_xattn_out_b"],
        "router_wT": i["L0_ffn_router_w"].T, "router_bias": i["L0_ffn_router_bias"],
        "Wu0": i["L0_ffn_Wu"], "Wg0": i["L0_ffn_Wg"], "Wd0": i["L0_ffn_Wd"],
        "Su": i["L0_ffn_Su"], "Sg": i["L0_ffn_Sg"], "Sd": i["L0_ffn_Sd"],
        "gamma1": i["L1_xattn_gamma"].reshape(1, 1),
        "W1": i["L1_ffn_W1"], "b1": by_feature(i["L1_ffn_b1"]), "W2": i["L1_ffn_W2"], "b2": by_feature(i["L1_ffn_b2"]),
        "W3": i["L1_ffn_W3"], "b3": i["L1_ffn_b3"], "gate_w": i["L1_ffn_Wg"], "gate_b": i["L1_ffn_bg"],
    }
    arrays = {k: _np.ascontiguousarray(v) for k, v in arrays.items()}
    nc = _bacc.Bacc("TRN2", target_bir_lowering=False, num_devices=1)
    args = {k: nc.dram_tensor(f"in_{k}", v.shape, _mybir.dt.from_np(v.dtype), kind="ExternalInput").ap()
            for k, v in arrays.items()}
    out = nc.dram_tensor("out", i["x"].shape, _mybir.dt.float32, kind="ExternalOutput").ap()
    flamingo_kernel(nc, **args, out=out)
    r = _run(nc, [{f"in_{k}": v for k, v in arrays.items()}], core_ids=[0])
    return r.results[0]["out"]
```

```python
from contextlib import ExitStack

import numpy as np

import concourse.bass as bass
from concourse import mybir

P = 128
ALU = mybir.AluOpType
ACT = mybir.ActivationFunctionType
AX = mybir.AxisListType.X
F32 = mybir.dt.float32
F32R = mybir.dt.float32r
BF16 = mybir.dt.bfloat16
I32 = mybir.dt.int32
U32 = mybir.dt.uint32
LN_EPS = 1e-5
GA = 4
NC = 4
GE = 2
NX = 4


class Steps:

    def __init__(self, eng, sem):
        self.eng, self.sem, self.before = eng, sem, 0

    def turn(self, g, per_turn, k=0):
        self.g, self.per_turn, self.k = g, per_turn, k

    def step(self, k):
        return self.g * self.per_turn + (self.before + k)

    def mark(self, ins):
        self.k += 1
        ins.then_inc(self.sem, 1)
        return self.step(self.k)

    def then(self, ins):
        self.eng.wait_ge(self.sem, self.mark(ins))

    def end(self, turns):
        assert self.per_turn in (self.k, 0), self.k
        self.before += turns * self.k


def flamingo_kernel(nc, x, ctx, g_xattn, g_ffn, theta_wT, theta_b, phi_wT, phi_b, g_wT, g_b, ln_gamma, ln_beta,
                    out_wT, out_b, router_wT, router_bias, Wu0, Wg0, Wd0, Su, Sg, Sd, gamma1,
                    W1, b1, W2, b2, W3, b3, gate_w, gate_b, out):
    B, S, D = x.shape
    LAT = theta_wT.shape[1]
    E0, _, F0 = Wu0.shape
    E1, _, H1 = W1.shape
    KD = D // P
    KH = H1 // P
    TOK = B * S
    CAP = TOK + P
    NT0 = (2 * TOK + E0 * (P - 1)) // P
    NT1 = (2 * TOK + E1 * (P - 1)) // P
    NT0 += -NT0 % NX
    NT1 += -NT1 % NX
    NGA, NGE = B // GA, B // GE
    NH, DH = 8, S // 8

    x_v = x.rearrange("b p d -> p b d")
    ctx_v = ctx.rearrange("b p d -> p b d")
    out_v = out.rearrange("b p d -> p b d")
    xg0 = nc.dram_tensor("xg0", [E0 * CAP, D], F32, kind="Internal").ap()
    yg0 = nc.dram_tensor("yg0", [NT0 * P, D], F32, kind="Internal").ap()
    xg1 = nc.dram_tensor("xg1", [E1 * CAP, D], F32, kind="Internal").ap()
    yg1 = nc.dram_tensor("yg1", [NT1 * P, D], F32, kind="Internal").ap()
    kscr = nc.dram_tensor("kscr", [2, TOK, D], F32, kind="Internal").ap()
    qscr = nc.dram_tensor("qscr", [2, TOK, D], F32, kind="Internal").ap()

    with ExitStack() as es:
        def sb(name, shape, dt=F32):
            return es.enter_context(nc.sbuf_tensor(name, shape, dt))

        def sem(name):
            return es.enter_context(nc.semaphore(name))

        xs = sb("xs", [P, B, D])
        WX = KD * H1 + KH * H1 + KH * D
        RING = 3
        with nc.sbuf_tensor("QK", [P, 2, NC * 8 * D], F32R) as QK:
            pass
        with nc.sbuf_tensor("WR", [P, RING * 2 * WX], F32R) as WR:
            with nc.sbuf_tensor("wraw", [P, WX], F32) as wraw:
                pass
        R2 = sb("R2", [P, 2 * RING * WX + WX])
        n = E0 * KD * F0
        Wug = R2[:, 0:2 * n].rearrange("p (e k a f) -> p e k a f", e=E0, k=KD, a=2)
        Wds = R2[:, 2 * n:3 * n].rearrange("p (e d) -> p e d", e=E0)
        F2 = Su.shape[2]
        m = 3 * n
        Sus = R2[:, m:m + KD * F2].rearrange("p (k f) -> p k f", k=KD)
        Sgs = R2[:, m + KD * F2:m + 2 * KD * F2].rearrange("p (k f) -> p k f", k=KD)
        Sds = R2[:, m + 2 * KD * F2:m + 3 * KD * F2].rearrange("p (k d) -> p k d", k=KD)
        m += 3 * KD * F2
        hs = R2[:, m:m + 2 * GA * P].rearrange("p (f t) -> p f t", f=2)
        m += 2 * GA * P
        gS, tx = (R2[:, m + k * GA * 2 * LAT:m + (k + 1) * GA * 2 * LAT].rearrange("p (j c l) -> p j c l", j=GA, c=2) for k in range(2))
        assert 2 * NC * 8 * D <= 2 * (RING - 1) * WX and m + 2 * GA * 2 * LAT <= 2 * RING * WX + WX
        ident = sb("ident", [P, P])
        ones = sb("ones", [P, P])
        tri_f = sb("tri_f", [P, P])
        tri = sb("tri", [P, P], BF16)
        ones_b = sb("ones_b", [P, P], BF16)
        iota_i = sb("iota_i", [P, 64], I32)
        iota_f = sb("iota_f", [P, 64])
        zeros = sb("zeros", [P, D])
        gates = sb("gates", [P, 5])
        tg = sb("tg", [P, 4])
        tgg = sb("tgg", [P, 1])
        thw = sb("thw", [P, LAT])
        phw = sb("phw", [P, LAT])
        gw = sb("gw", [P, LAT])
        thb = sb("thb", [LAT, 1])
        phb = sb("phb", [LAT, 1])
        gb_bc = sb("gb_bc", [P, LAT])
        gbT = sb("gbT", [P, 2, KD, LAT])
        ow = sb("ow", [LAT, P])
        ob = sb("ob", [P, 1])
        rw = sb("rw", [P, KD, E0])
        rb_bc = sb("rb_bc", [P, E0])
        gwt = sb("gwt", [P, KD, E1])
        gbs = sb("gbs", [P, E1])
        b1T = sb("b1T", [P, E1, KH])
        b2T = sb("b2T", [P, E1, KH])
        b3bc = sb("b3bc", [P, E1, D])
        wts = sb("wts", [P, B, 2])
        idxf = sb("idxf", [P, B, 2])
        slotf = sb("slotf", [P, B, 2])
        yslot = sb("yslot", [P, B, 2], U32)
        base = {E0: sb("base0", [P, E0]), E1: sb("base1", [P, E1])}
        cnt = sb("cnt", [P, E0])
        meta = sb("meta", [P, 9, E0])
        tabf = sb("tabf", [P, NT0, 4])
        tab = sb("tab", [1, NT0, 3], I32)
        endi = sb("endi", [1, E0], I32)
        tail = sb("tail", [1, E0], I32)

        R3 = sb("R3", [P, WX])
        assert WX >= 4 * GA * D
        cx, xl, xn = (R3[:, q * GA * D:(q + 1) * GA * D].rearrange("p (j d) -> p j d", j=GA) for q in range(3))
        xT = R3[:, 3 * GA * D:4 * GA * D].rearrange("p (k t) -> p k t", k=KD)
        raw = (wraw[:, :], R3[:, :])
        st6 = sb("st6", [P, 2 * GA, 6])
        st2 = sb("st2", [P, 2 * GA, 2])
        rstd = sb("rstd", [P, 2 * GA])
        veps = sb("veps", [P, 2 * GA])
        nhalf = sb("nhalf", [P, GA])
        Q1 = sb("Q1", [P, GA * 2 * D])
        Q2 = sb("Q2", [P, GA * 2 * D])
        thS = sb("thS", [LAT, GA, D])
        nm = sb("nm", [P, GA, 2])
        rsum = sb("rsum", [P, GA, 2])
        rrec = sb("rrec", [P, GA, 2])
        sums = sb("sums", [P, 2, GA])
        mom = sb("mom", [P, 4, GA])
        lb = sb("lb", [P, GA, E0])
        lmx = sb("lmx", [P, GA])
        ex = sb("ex", [P, GA, E0])
        key = sb("key", [P, GA, E0])
        v8 = sb("v8", [P, GA, 8])
        i8 = sb("i8", [P, GA, 8], U32)
        oh = sb("oh", [P, GA, 2, E0])
        ohx = sb("ohx", [P, GA, 2, E0])
        mask = sb("mask", [P, GA + 1, E0], BF16)
        rk = sb("rk", [P, GA, E0])
        sel = sb("sel", [P, GA, 2])
        den = sb("den", [P, GA])
        slotu = sb("slotu", [P, GA, 2], U32)
        ps = es.enter_context(nc.psum_tensor("ps", [P, 8, 512], F32))

        gam_n = Q1[0:LAT, 0:2 * D].rearrange("p (a d) -> p a d", a=2)
        phS = Q2[0:LAT, 0:GA * D].rearrange("p (j d) -> p j d", j=GA)
        big1 = Q2[:, 2 * GA * P:2 * GA * P + NT0 * E0]
        hS = thS
        txq = gS
        tmp = Q1[:, 0:GA * D].rearrange("p (j d) -> p j d", j=GA)
        Pm = Q1[:, :].rearrange("p (j c s) -> p j c s", j=GA, c=2)
        PTm = Q2[:, :].rearrange("p (j c t) -> p j c t", j=GA, c=2)
        Xin = Q1[:, 0:NX * D].rearrange("p (n d) -> p n d", n=NX)
        Yt = Q1[:, 4 * D:6 * D].rearrange("p (n d) -> p n d", n=2)
        XTt = Q2[:, 0:2 * D].rearrange("p (n d) -> p n d", n=2)
        su_t = Q2[:, 2 * D:3 * D].rearrange("p (n d) -> p n d", n=2)
        h0_t = Q2[:, 3 * D:4 * D].rearrange("p (n d) -> p n d", n=2)
        h0T = Q2[:, 4 * D:5 * D].rearrange("p (n d) -> p n d", n=2)
        pre1, pre2 = Q1[:, 6 * D:8 * D], Q2[:, 0:2 * D]
        Ha = Q2[:, 2 * D:4 * D].rearrange("p (k t) -> p k t", k=KH)
        Hb = Q2[:, 4 * D:6 * D].rearrange("p (k t) -> p k t", k=KH)
        XTp = sb("XTp", [P, 2, D], F32R)
        Hap = sb("Hap", [P, 2, KH, P], F32R)
        Hbp = sb("Hbp", [P, 2, KH, P], F32R)
        NK = 3 * DH
        QS = QK[:, 0, :].rearrange("p (n a t) -> p n a t", n=NC, a=NH)
        KS = QK[:, 1, :].rearrange("p (n a t) -> p n a t", n=NC, a=NH)
        split = sb("split", [P, 2, 2, D], F32R)
        csplit = [split[:], Hap[:].rearrange("p a k t -> p a (k t)").rearrange("p a (j d) -> p a j d", j=2)]
        mraw = sb("mraw", [P, 2, NH, 2])
        nmr = sb("nmr", [P, 2, NH * 2], F32R)
        mT = sb("mT", [2 * NH * 2, P], F32R)
        PTb = Q1[:, :].rearrange("p (n c q) -> p n c q", n=4, c=2)
        gC = sb("gC", [P, 2, 2, D])
        VE = 32
        VT = Q2[:, 0:2 * 2 * NH * VE].rearrange("p (n c h e) -> p n c h e", n=2, c=2, h=NH)
        q2 = 2 * 2 * NH * VE
        oU = Q2[:, q2:q2 + 2 * D]
        q2 += 2 * D
        oN = Q2[:, q2:q2 + D]
        q2 += D
        orec = Q2[:, q2:q2 + 2 * NH].rearrange("p (c h) -> p c h", c=2)
        gE = Q1[:, :].rearrange("p (n j k d) -> p n j k d", n=2, j=GE, k=2)
        idxg = sb("idxg", [P, 2, GE, 2], U32)

        names = ("vector_steps routing_steps x_loaded ctx_loaded ctx_high ctx_split ctx_split_stored0 ctx_split_stored1 setup_pool setup_dve tanh_done gb_t_ready w0_loaded w1_loaded raw_loaded0 raw_loaded1 w_high w_split l1_h1_split l1_h2_split h1_high h2_high x_high "
                 "xl_ready theta_ready theta_copied phi_ready phi_copied gt_ready gt_copied "
                 "scores_ready max_ready p_ready pt_ready pt_copied_v pt_copied_a pv_ready sums_ready tot_ready "
                 "h_ready ht_ready ht_copied proj_ready xn_ready xnt_ready xnt_copied logits_ready "
                 "dif_ready ex_ready mask_ready rank_ready slots_ready scattered scattered0 scattered1 u_ready silu_ready "
                 "hs_ready y_ready x2_ready tails_ready tails_zeroed table_ready yslots_ready "
                 "tile_loaded0 tile_loaded1 tile_loaded2 tile_loaded3 tile_turned tile_copied ug_ready tile_silu tile_h tile_y tile_out tile_stored0 tile_stored1 output_stored0 output_stored1 "
                 "l1_h1_ready l1_h1_copied l1_h1_turned l1_h1_gelu l1_h2_ready l1_h2_copied l1_h2_turned l1_h2_gelu "
                 "tile_ht tile_ht_copied var_ready var_eps rstd_ready alone "
                 "idx_copied gathered0 gathered1 gather_used q_ready q_stored0 q_stored1 q_stacked0 q_stacked1 k_stacked0 k_stacked1 v_loaded0 v_loaded1 vt_ready vt_copied "
                 "s_ready s_max m_high m_ready mt_copied m_stacked st_ready st_exp o_ready o_copied o_turned o_inverse o_norm ot_ready row_sum0 row_sum1 row_stats q_high x_sum x_stats x_var x_eps x_rstd "
                 "consts_loaded out_summed xn_free pool_a phase_done out_ready out_stored x1_used").split()
        s = {nm_: sem(nm_) for nm_ in names}

        def alone(eng):
            eng.sem_inc(s["alone"], 1)

        def is_tile(t):
            return not isinstance(t, int) or 0 <= t < NT1

        def group_turns(eng, turn):
            turn(0, True, False)
            with eng.Fori(1, NGA) as g:
                turn(g, True, True)
            turn(NGA, False, True)

        def item(t):
            return not isinstance(t, int) or 0 <= t < B

        def item_turns(eng, turn):
            for t in range(-4, 3):
                turn(t, t % NC)
            full = (B - 8) // NC
            with eng.Fori(0, full) as i:
                for k in range(3, NC + 3):
                    turn(NC * i + k, k % NC)
            for t in range(NC * full + 3, B + 3):
                turn(t, t % NC)

        def tile_turns(eng, turn):
            for t in range(-3, 3):
                turn(t, t % NX)
            full = (NT1 - 6) // NX
            with eng.Fori(0, full) as i:
                for k in range(3, NX + 3):
                    turn(NX * i + k, k % NX)
            for t in range(NX * full + 3, NT1 + 2):
                turn(t, t % NX)

        blk = es.enter_context(nc.Block())

        def load_tile(sp, t, b, xg):
            row = sp.value_load(tab[0:1, t, 1:2], min_val=0, max_val=xg.shape[0] - P)
            sp.dma_start(Xin[:, b, :], xg[bass.ds(row, P), :]).then_inc(s[f"tile_loaded{b}"], 16)

        def load_next(sp, t, b, xg, before):
            sp.wait_ge(s["tile_turned"], t + (before - NX + 1))
            alone(sp)
            load_tile(sp, t, b, xg)

        def store_tiles(pool, nt, yg, before):
            with pool.Fori(0, nt // 2) as i:
                for b in range(2):
                    pool.wait_ge(s["tile_out"], 2 * i + (before + b + 1))
                    alone(pool)
                    pool.dma_start(yg[bass.ds((2 * i + b) * P, P), :], Yt[:, b, :]).then_inc(s[f"tile_stored{b}"], 16)

        constants = (
            (gates[:, 0:2], g_xattn.unsqueeze(0).to_broadcast((P, 2))),
            (gates[:, 2:4], g_ffn.unsqueeze(0).to_broadcast((P, 2))),
            (gates[:, 4:5], gamma1.to_broadcast((P, 1))),
            (phw[:], phi_wT),
            (gw[:], g_wT),
            (thw[:], theta_wT),
            (gam_n[:, 0, :], ln_gamma),
            (gam_n[:, 1, :], ln_beta),
            (phb[:], phi_b.unsqueeze(1)),
            (thb[:], theta_b.unsqueeze(1)),
            (gb_bc[:], g_b.unsqueeze(0).to_broadcast((P, LAT))),
            (ow[:], out_wT),
            (ob[:], out_b.unsqueeze(1)),
            (rw[:], router_wT.rearrange("(k p) e -> p k e", p=P)),
            (rb_bc[:], router_bias.unsqueeze(0).to_broadcast((P, E0))),
            (gwt[:], gate_w.rearrange("(k p) e -> p k e", p=P)),
            (gbs[:], gate_b.unsqueeze(0).to_broadcast((P, E1))))
        N_CONST = len(constants)
        @blk.sync
        def _(sp):
            for dst, src in constants[:len(constants) // 2]:
                sp.dma_start(dst, src).then_inc(s["consts_loaded"], 16)
            def sp_group(g, more):
                sp.wait_ge(s["x1_used"], g + 1)
                sp.dma_start(cx, ctx_v[:, bass.ds(g * GA, GA), :]).then_inc(s["ctx_loaded"], 16)
                for c in range(2):
                    sp.wait_ge(s["ctx_split"], 2 * g + (c + 1))
                    for p in range(2):
                        sp.dma_start(kscr[p, bass.ds((2 * g + c) * 2 * P, 2 * P), :].rearrange("(j p) d -> p j d", p=P),
                                     csplit[c][:, p].bitcast(F32)).then_inc(s[f"ctx_split_stored{c}"], 16)
                if more:
                    sp.dma_start(xs[:, bass.ds((g + 1) * GA, GA), :], x_v[:, bass.ds((g + 1) * GA, GA), :]).then_inc(s["x_loaded"], 16)

            with sp.Fori(0, NGA - 1) as g:
                sp_group(g, True)
            sp_group(NGA - 1, False)

            def zero_tails(turn, E, xg):
                sp.wait_ge(s["tails_ready"], turn)
                with sp.Fori(0, E) as e:
                    row = sp.value_load(tail[0:1, bass.ds(e, 1)], min_val=0, max_val=xg.shape[0] - P)
                    sp.dma_start(xg[bass.ds(row, P), :], zeros[:, :]).then_inc(s["tails_zeroed"], 16)

            zero_tails(1, E0, xg0)
            sp.wait_ge(s["table_ready"], 1)
            sp.wait_ge(s["tails_zeroed"], 16 * E0)
            sp.wait_ge(s["scattered"], 16 * 2 * B)
            for b in range(NX):
                load_tile(sp, b, b, xg0)
            with sp.Fori(1, NT0 // NX) as i:
                for b in range(NX):
                    load_next(sp, NX * i + b, b, xg0, 0)
            for c in range(2):
                sp.wait_ge(s[f"ctx_split_stored{c}"], NGA * 32)

            def stack(S_, scratch, t, n, parts, done):
                for i, part in enumerate(parts):
                    sp.dma_start(S_[i * DH:(i + 1) * DH, n].bitcast(F32),
                                 scratch[part, bass.ds(t * P, P), :].rearrange("(a d) t -> d a t", d=DH)).then_inc(s[done], 16)

            def sp_turn(t, k):
                if item(t + 2):
                    sp.wait_ge(s["vt_ready"], t - 1) if item(t - 2) else None
                    n, b = (k + 2) % NC, k % 2
                    sp.dma_start(cx[:, n, :], ctx_v[:, bass.ds(t + 2, 1), :].rearrange("p a d -> p (a d)")).then_inc(s[f"v_loaded{b}"], 16)
                if item(t + 3):
                    n, b = (k + 3) % NC, (k + 1) % 2
                    sp.wait_ge(s["o_ready"], t) if item(t - 1) else sp.wait_ge(s["phase_done"], 1)
                    alone(sp)
                    stack(KS, kscr, t + 3, n, (0, 1, 0), f"k_stacked{b}")
                    sp.wait_ge(s[f"q_stored{b}"], (t + 3) // 2 * 32 + 32)
                    alone(sp)
                    stack(QS, qscr, t + 3, n, (0, 0, 1), f"q_stacked{b}")
                if item(t + 1):
                    n = (k + 1) % NC
                    sp.wait_ge(s["mt_copied"], t + 2)
                    for p in range(2):
                        sp.dma_start(QS[NK + p:NK + p + 1, n].rearrange("o a (c q) -> o (a c) q", c=2).bitcast(F32),
                                     mT[p * 2 * NH:(p + 1) * 2 * NH, :].bitcast(F32)).then_inc(s["m_stacked"], 16)
                if item(t + 4):
                    sp.wait_ge(s["q_ready"], t + 5)
                    alone(sp)
                    for p in range(2):
                        sp.dma_start(qscr[p, bass.ds((t + 4) * P, P), :], split[:, k % 2, p, :].bitcast(F32)).then_inc(s[f"q_stored{k % 2}"], 16)

            item_turns(sp, sp_turn)
            zero_tails(2, E1, xg1)
            sp.wait_ge(s["table_ready"], 2)
            sp.wait_ge(s["tails_zeroed"], 16 * (E0 + E1))
            for b in range(2):
                sp.wait_ge(s[f"scattered{b}"], 16 * B)
            for t in range(2 * NX):
                load_tile(sp, t, t % NX, xg1) if t < NX else load_next(sp, t, t % NX, xg1, NT0)

            def store_output(t, b):
                sp.wait_ge(s["tile_out"], t + (NT0 + 1))
                alone(sp)
                sp.dma_start(yg1[bass.ds(t * P, P), :], Yt[:, b, :]).then_inc(s[f"output_stored{b}"], 16)

            with sp.Fori(0, NT1 // NX - 2) as i:
                for b in range(NX):
                    load_next(sp, NX * i + (b + 2 * NX), b, xg1, NT0)
                    store_output(NX * i + b, b % 2)
            for t in range(NT1 - 2 * NX, NT1):
                store_output(t, t % 2)
            with sp.Fori(0, NGE) as g:
                sp.wait_ge(s["out_ready"], g + 1)
                sp.dma_start(out_v[:, bass.ds(g * GE, GE), :], xs[:, bass.ds(g * GE, GE), :]).then_inc(s["out_stored"], 16)
            sp.wait_ge(s["out_stored"], NGE * 16)

        @blk.gpsimd
        def _(pool):
            nc.gpsimd.memset(ones[:], 1.0).then_inc(s["pool_a"], 1)
            nc.gpsimd.memset(ident[:], 0.0).then_inc(s["pool_a"], 1)
            nc.gpsimd.memset(zeros[:], 0.0).then_inc(s["pool_a"], 1)
            nc.gpsimd.memset(nhalf[:], -0.5).then_inc(s["pool_a"], 1)
            nc.gpsimd.iota(iota_i[:], pattern=[[1, 64]], base=0, channel_multiplier=0).then_inc(s["pool_a"], 1)
            pool.wait_ge(s["pool_a"], 5)
            nc.gpsimd.affine_select(out=ident[:], in_=ident[:], compare_op=ALU.not_equal, fill=1.0, base=0,
                                    pattern=[[-1, P]], channel_multiplier=1).then_inc(s["setup_pool"], 1)
            nc.gpsimd.affine_select(out=tri_f[:], in_=ones[:], compare_op=ALU.is_gt, fill=0.0, base=0,
                                    pattern=[[1, P]], channel_multiplier=-1).then_inc(s["setup_pool"], 1)
            def root(n, src, eps, dst, names, turn):
                ready, added, done = names
                pool.wait_ge(s[ready], turn)
                alone(pool)
                nc.gpsimd.tensor_scalar(eps, src, LN_EPS, None, ALU.add).then_inc(s[added], 1)
                pool.wait_ge(s[added], turn)
                nc.gpsimd.tensor_tensor(dst, eps, nhalf[:, 0:n], ALU.pow).then_inc(s[done], 1)

            def raw_buffer(e):
                return 1 if e % 2 == 0 and e > 0 else 0

            def load_weights(e):
                at, b = 0, raw_buffer(e)
                for W, k_ in ((W1, KD), (W2, KH), (W3, KH)):
                    size = k_ * W.shape[2]
                    pool.dma_start(raw[b][:, at:at + size].rearrange("p (k n) -> p k n", k=k_),
                                   W[e].rearrange("(k p) n -> p k n", p=P)).then_inc(s[f"raw_loaded{b}"], 16)
                    at += size

            def split_part(e, part, parts):
                n, place = WX // parts, (e + 2) % RING
                share = slice(0, n) if parts == 1 else bass.ds(part * n, n)
                high, low = (WR[:, (2 * place + h) * WX:(2 * place + h + 1) * WX][:, share] for h in range(2))
                src = raw[raw_buffer(e)][:, share]
                count = e + NGA if parts == 1 else part + 1
                alone(pool)
                nc.gpsimd.tensor_copy(high, src).then_inc(s["w_high"], 1)
                pool.wait_ge(s["w_high"], count)
                alone(pool)
                nc.gpsimd.tensor_tensor(low, src, high.bitcast(F32), ALU.subtract).then_inc(s["w_split"], 1)
                pool.wait_ge(s["w_split"], count)
                alone(pool)

            def split_weights(e):
                if e >= RING:
                    done = pool.value_load(endi[0:1, e - RING:e - RING + 1], min_val=0, max_val=NT1)
                    pool.wait_ge(s["tile_y"], done + NT0)
                b = raw_buffer(e)
                pool.wait_ge(s[f"raw_loaded{b}"], (e // 2 + (2 if b == 0 else 0)) * 48)
                split_part(e, 0, 1)

            def scatter(turn, n, xg, total):
                pool.wait_ge(s["slots_ready"], turn)
                alone(pool)
                for j in range(n):
                    for k in range(2):
                        pool.indirect_dma_start(xg[:, :], bass.IndirectOffsetOnAxis(ap=slotu[:, j, k:k + 1], axis=0),
                                                xn[:, j, :], None).then_inc(s["scattered"], 16)
                pool.wait_ge(s["scattered"], total)
                pool.sem_inc(s["xn_free"], 1)

            def gather(items, n, yg, turn, buf, ix, done):
                nc.gpsimd.tensor_copy(idxg[:, ix, 0:n], yslot[:, items, :]).then_inc(s["idx_copied"], 1)
                pool.wait_ge(s["idx_copied"], turn)
                alone(pool)
                for j in range(n):
                    for k in range(2):
                        pool.indirect_dma_start(buf[:, 2 * j + k, :], None, yg[:, :],
                                                bass.IndirectOffsetOnAxis(ap=idxg[:, ix, j, k:k + 1], axis=0)).then_inc(s[done], 16)

            pool.sem_inc(s["xn_free"], 1)

            def load_layers():
                for dst, src in ((Sus, Su[0].rearrange("(k p) f -> p k f", p=P)), (Sgs, Sg[0].rearrange("(k p) f -> p k f", p=P)),
                                 (Sds, Sd[0].rearrange("(k p) d -> p k d", p=P)),
                                 (Wug[:, :, 0, 0, :], Wu0[:, 0:P, :].rearrange("e p f -> p e f")),
                                 (Wug[:, :, 1, 0, :], Wu0[:, P:2 * P, :].rearrange("e p f -> p e f")),
                                 (Wug[:, :, 0, 1, :], Wg0[:, 0:P, :].rearrange("e p f -> p e f")),
                                 (Wug[:, :, 1, 1, :], Wg0[:, P:2 * P, :].rearrange("e p f -> p e f")),
                                 (Wds, Wd0.rearrange("e f d -> f e d"))):
                    pool.dma_start(dst, src).then_inc(s["w0_loaded"], 16)
                for dst, src in ((b1T[:], b1), (b2T[:], b2),
                                 (b3bc[:], b3.unsqueeze(0).to_broadcast((P, E1, D)))):
                    pool.dma_start(dst, src).then_inc(s["w1_loaded"], 16)
                load_weights(0)

            def pool_turn(g, front, back):
                if front:
                    root(GA, st2[:, 0:GA, 1], veps[:, 0:GA], rstd[:, 0:GA], ("var_ready", "var_eps", "rstd_ready"), 2 * g + 1)
                if not back:
                    load_layers()
                if back:
                    root(GA, st2[:, GA:2 * GA, 1], veps[:, GA:2 * GA], rstd[:, GA:2 * GA], ("x_var", "x_eps", "x_rstd"), g)
                if front:
                    pool.wait_ge(s["ctx_loaded"], (g + 1) * 16)
                    for c in range(2):
                        pool.wait_ge(s[f"ctx_split_stored{c}"], g * 32)
                        alone(pool)
                        src = cx[:, 2 * c:2 * c + 2, :]
                        nc.gpsimd.tensor_copy(csplit[c][:, 0], src).then_inc(s["ctx_high"], 1)
                        pool.wait_ge(s["ctx_high"], 2 * g + (c + 1))
                        nc.gpsimd.tensor_tensor(csplit[c][:, 1], src, csplit[c][:, 0].bitcast(F32), ALU.subtract).then_inc(s["ctx_split"], 1)
                if back:
                    scatter(g, GA, xg0, g * (GA * 2 * 16))
                if front:
                    root(GA, mom[:, 3, :], veps[:, 0:GA], mom[:, 2, :], ("var_ready", "var_eps", "rstd_ready"), 2 * g + 2)
                    pool.wait_ge(s["raw_loaded0"], 48)
                    split_part(0, g, NGA)

            group_turns(pool, pool_turn)
            load_weights(1)
            store_tiles(pool, NT0, yg0, 0)
            for b in range(2):
                pool.wait_ge(s[f"tile_stored{b}"], NT0 // 2 * 16)
            pool.wait_ge(s["yslots_ready"], 1)

            def c_gather(t, b):
                pool.wait_ge(s["gather_used"], t - 1) if item(t - 2) else None
                gather(bass.ds(t, 1), 1, yg0, t + 1, gC[:, b], b, f"gathered{b}")

            def c_pool_turn(t, k):
                if item(t + 4):
                    root(1, st2[:, 0, 1:2], veps[:, 0:1], rstd[:, 0:1], ("var_ready", "var_eps", "rstd_ready"), t + (2 * NGA + 5))
                if item(t + 5):
                    c_gather(t + 5, (k + 1) % 2)
                if item(t - 1):
                    root(1, st2[:, 1, 1:2], veps[:, 1:2], rstd[:, 1:2], ("x_var", "x_eps", "x_rstd"), t + NGA)
                if k % 2 == 0 and item(t - 3):
                    pair = (t - 4) // 2
                    pool.wait_ge(s["slots_ready"], pair + (NGA + 1))
                    alone(pool)
                    for j in range(k, k + 2):
                        for x in range(2):
                            pool.indirect_dma_start(xg1[:, :], bass.IndirectOffsetOnAxis(ap=slotu[:, j, x:x + 1], axis=0),
                                                    xn[:, j, :], None).then_inc(s[f"scattered{(k // 2) % 2}"], 16)

            c_gather(0, 0)
            item_turns(pool, c_pool_turn)
            pool.wait_ge(s["ot_ready"], B)
            for b in range(2):
                pool.wait_ge(s[f"scattered{b}"], 16 * B)
            load_weights(2)
            for e in range(1, E1):
                if e == RING:
                    pool.wait_ge(s["table_ready"], 2)
                split_weights(e)
                if e + 2 < E1:
                    load_weights(e + 2)
            for b in range(2):
                pool.wait_ge(s[f"output_stored{b}"], NT1 // 2 * 16)
            pool.wait_ge(s["yslots_ready"], 2)
            with pool.Fori(0, NGE // 2) as g:
                for k in range(2):
                    if k == 0:
                        pool.wait_ge(s["gather_used"], 2 * g + (B - 1))
                    else:
                        pool.wait_ge(s["gather_used"], 2 * g + B)
                    gather(bass.ds((2 * g + k) * GE, GE), GE, yg1, 2 * g + (B + k + 1), gE[:, k].rearrange("p j k d -> p (j k) d"), k, f"gathered{k}")

        @blk.vector
        def _(dve):
            v = nc.vector

            def row_moments(lk, src, n, at, ready):
                alone(dve)
                for j in range(n):
                    i = v.bn_stats(st6[:, at + j, :], src[:, j, :])
                lk.then(i)
                alone(dve)
                for j in range(n):
                    i = v.bn_aggr(st2[:, at + j, :], st6[:, at + j, :])
                i.then_inc(s[ready], 1)

            def normalise(src, dst, n, at):
                for j in range(n):
                    i = v.tensor_scalar(dst[:, j, :], src[:, j, :], st2[:, at + j, 0:1], rstd[:, at + j:at + j + 1], ALU.subtract, ALU.mult)
                return i

            def choose(lk, g):
                n, E = GA, E0
                dve.wait_ge(s["logits_ready"], g + 1)
                lg = ps[:, 5, 0:n * E].rearrange("p (j e) -> p j e", e=E)
                lk.then(v.tensor_reduce(lmx[:], lg, AX, ALU.max))
                v.tensor_tensor(ex[:], lg, lmx[:].unsqueeze(2).to_broadcast((P, n, E)), ALU.subtract).then_inc(s["dif_ready"], 1)
                lk.then(v.tensor_tensor(lb[:], lg, rb_bc[:].unsqueeze(1).to_broadcast((P, n, E)), ALU.add))
                alone(dve)
                for j in range(n):
                    i = v.max(v8[:, j, :], lb[:, j, :])
                lk.then(i)
                alone(dve)
                for j in range(n):
                    i = v.max_index(i8[:, j, :], v8[:, j, :], lb[:, j, :])
                lk.then(i)
                ig = idxf[:, bass.ds(g * n, n), :]
                alone(dve)
                lk.then(v.tensor_copy(ig, i8[:, 0:n, 0:2]))
                lk.then(v.tensor_tensor(oh[:], iota_f[:, 0:E].unsqueeze(1).unsqueeze(1).to_broadcast((P, n, 2, E)),
                                        ig.unsqueeze(3).to_broadcast((P, n, 2, E)), ALU.is_equal))
                v.tensor_tensor(mask[:, 0:n, :], oh[:, :, 0, :], oh[:, :, 1, :], ALU.add).then_inc(s["mask_ready"], 1)

            def place(lk, g):
                n, E = GA, E0
                dve.wait_ge(s["ex_ready"], g + 1)
                lk.then(v.tensor_tensor(ohx[:], oh[:], ex[:].unsqueeze(2).to_broadcast((P, n, 2, E)), ALU.mult))
                lk.then(v.tensor_reduce(sel[:], ohx[:], AX, ALU.add))
                lk.then(v.tensor_tensor(den[:], sel[:, :, 0], sel[:, :, 1], ALU.add))
                dve.wait_ge(s["rank_ready"], g + 1)
                psK = ps[:, 5, 0:(n + 1) * E].rearrange("p (j e) -> p j e", e=E)
                m_rank = lk.mark(v.tensor_tensor(rk[:], psK[:, 0:n, :], cnt[:].unsqueeze(1).to_broadcast((P, n, E)), ALU.add))
                lk.then(v.reciprocal(den[:], den[:]))
                m_count = lk.mark(v.tensor_tensor(cnt[:], psK[:, n, :], cnt[:], ALU.add))
                m_row = lk.mark(v.tensor_tensor(ohx[:], oh[:], rk[:].unsqueeze(2).to_broadcast((P, n, 2, E)), ALU.mult))
                m_share = lk.mark(v.tensor_tensor(sel[:], sel[:], den[:].unsqueeze(2).to_broadcast((P, n, 2)), ALU.mult))
                dve.wait_ge(lk.sem, m_row)
                sg = slotf[:, bass.ds(g * n, n), :]
                m_slot = lk.mark(v.tensor_reduce(sg, ohx[:], AX, ALU.add))
                dve.wait_ge(lk.sem, m_share)
                v.tensor_scalar(wts[:, bass.ds(g * n, n), :], sel[:], tg[:, 2:3], None, ALU.mult)
                dve.wait_ge(lk.sem, m_slot)
                alone(dve)
                v.tensor_copy(slotu[:], sg).then_inc(s["slots_ready"], 1)

            def tables(lk, E, NT):
                c_ = cnt[:, 0:E]
                v.tensor_copy(tail[0:1, 0:E], c_[0:1, :]).then_inc(s["tails_ready"], 1)
                n_e, nt, end, off, dlt = (meta[:, k, 0:E] for k in range(5))
                lk.then(v.tensor_tensor(n_e, c_, base[E][:], ALU.subtract))
                NJ = TOK // P
                cmp = big1[:, 0:E * NJ].rearrange("p (e j) -> p e j", e=E)
                lk.then(v.tensor_scalar(tabf[:, 0:NJ, 0], iota_f[:, 0:NJ], float(P), None, ALU.mult))
                lk.then(v.tensor_tensor(cmp, n_e.unsqueeze(2).to_broadcast((P, E, NJ)),
                                        tabf[:, 0:NJ, 0].unsqueeze(1).to_broadcast((P, E, NJ)), ALU.is_gt))
                lk.then(v.tensor_reduce(nt, cmp, AX, ALU.add))
                le = big1[:, 0:E * E].rearrange("p (e f) -> p e f", e=E)
                lk.then(v.tensor_tensor(le, iota_f[:, 0:E].unsqueeze(2).to_broadcast((P, E, E)),
                                        iota_f[:, 0:E].unsqueeze(1).to_broadcast((P, E, E)), ALU.is_ge))
                lk.then(v.tensor_tensor(le, le, nt.unsqueeze(1).to_broadcast((P, E, E)), ALU.mult))
                lk.then(v.tensor_reduce(end, le, AX, ALU.add))
                lk.then(v.tensor_tensor(off, end, nt, ALU.subtract))
                ge = big1[:, 0:NT * E].rearrange("p (t e) -> p t e", e=E)
                lk.then(v.tensor_tensor(ge, iota_f[:, 0:NT].unsqueeze(2).to_broadcast((P, NT, E)),
                                        end.unsqueeze(1).to_broadcast((P, NT, E)), ALU.is_ge))
                lk.then(v.tensor_reduce(tabf[:, 0:NT, 0], ge, AX, ALU.add))
                lk.then(v.tensor_scalar(tabf[:, 0:NT, 0], tabf[:, 0:NT, 0], float(E - 1), None, ALU.min))
                lk.then(v.tensor_tensor(ge, ge, nt.unsqueeze(1).to_broadcast((P, NT, E)), ALU.mult))
                lk.then(v.tensor_reduce(tabf[:, 0:NT, 1], ge, AX, ALU.add))
                lk.then(v.tensor_tensor(tabf[:, 0:NT, 1], iota_f[:, 0:NT], tabf[:, 0:NT, 1], ALU.subtract))
                lk.then(v.tensor_scalar(tabf[:, 0:NT, 2], iota_f[:, 0:NT], end[:, E - 1:E], float(P), ALU.is_lt, ALU.mult))
                lk.then(v.tensor_tensor(tabf[:, 0:NT, 1], tabf[:, 0:NT, 1], tabf[:, 0:NT, 2], ALU.mult))
                lk.then(v.scalar_tensor_tensor(tabf[:, 0:NT, 1], tabf[:, 0:NT, 0], float(CAP), tabf[:, 0:NT, 1], ALU.mult, ALU.add))
                lk.then(v.scalar_tensor_tensor(dlt, off, float(P), base[E][:], ALU.mult, ALU.subtract))
                if E == E1:
                    times = (E1 + 1) // RING
                    over = big1[:, 0:times * NT].rearrange("p (m t) -> p m t", m=times)
                    v.tensor_scalar(tabf[:, 0:NT, 2], tabf[:, 0:NT, 0], 2.0, None, ALU.add)
                    for m_ in range(times):
                        i = v.tensor_scalar(over[:, m_, :], tabf[:, 0:NT, 0], float(RING * (m_ + 1) - 2), -float(RING), ALU.is_ge, ALU.mult)
                    lk.then(i)
                    for m_ in range(times):
                        lk.then(v.tensor_tensor(tabf[:, 0:NT, 2], tabf[:, 0:NT, 2], over[:, m_, :], ALU.add))
                lk.then(v.tensor_copy(endi[0:1, 0:E], end[0:1, :]))
                v.tensor_copy(tab[0:1, 0:NT, :], tabf[0:1, 0:NT, 0:3]).then_inc(s["table_ready"], 1)
                bo = big1[:, 0:B * 2 * E].rearrange("p (b k e) -> p b k e", b=B, k=2)
                lk.then(v.tensor_tensor(bo, iota_f[:, 0:E].unsqueeze(1).unsqueeze(1).to_broadcast((P, B, 2, E)),
                                        idxf[:].unsqueeze(3).to_broadcast((P, B, 2, E)), ALU.is_equal))
                lk.then(v.tensor_tensor(bo, bo, dlt.unsqueeze(1).unsqueeze(1).to_broadcast((P, B, 2, E)), ALU.mult))
                lk.then(v.tensor_reduce(idxf[:], bo, AX, ALU.add))
                lk.then(v.tensor_tensor(slotf[:], slotf[:], idxf[:], ALU.add))
                v.tensor_copy(yslot[:], slotf[:]).then_inc(s["yslots_ready"], 1)

            dve.wait_ge(s["setup_pool"], 2)
            v.tensor_copy(tri[:], tri_f[:]).then_inc(s["setup_dve"], 1)
            v.tensor_copy(ones_b[:], ones[:]).then_inc(s["setup_dve"], 1)
            v.tensor_copy(iota_f[:], iota_i[:]).then_inc(s["setup_dve"], 1)
            dve.wait_ge(s["setup_dve"], 3)
            v.tensor_scalar(base[E0][:], iota_f[:, 0:E0], float(CAP), None, ALU.mult).then_inc(s["setup_dve"], 1)
            v.tensor_scalar(base[E1][:], iota_f[:, 0:E1], float(CAP), None, ALU.mult).then_inc(s["setup_dve"], 1)
            dve.wait_ge(s["setup_dve"], 5)
            v.tensor_copy(cnt[:], base[E0][:]).then_inc(s["setup_dve"], 1)
            dve.sem_inc(s["x1_used"], 1)
            dve.sem_inc(s["x2_ready"], 1)
            lk = Steps(dve, s["vector_steps"])
            lr = Steps(dve, s["routing_steps"])
            FRONT, BACK = 9, 16

            def late_constants():
                dve.wait_ge(s["gb_t_ready"], 1)
                v.tensor_copy(gbT[:], ps[:, 7, 0:4 * LAT].rearrange("p (a c l) -> p a c l", a=2, c=KD)).then_inc(s["setup_dve"], 1)
                dve.wait_ge(s["tanh_done"], 1)
                v.tensor_tensor(tgg[:], tg[:, 1:2], gates[:, 4:5], ALU.mult).then_inc(s["setup_dve"], 1)
                v.memset(mask[:], 0.0).then_inc(s["setup_dve"], 1)
                dve.wait_ge(s["setup_dve"], 9)

            def a_turn(g, front, back):
                t1 = g + 1
                if front:
                    lk.turn(g, FRONT)
                    X = xs[:, bass.ds(g * GA, GA), :]
                    dve.wait_ge(s["x_loaded"], g * 16 + 16)
                    row_moments(lk, X, GA, 0, "var_ready")
                if not back:
                    late_constants()
                if back:
                    lr.turn(g - 1, BACK)
                    Xb = xs[:, bass.ds((g - 1) * GA, GA), :]
                    row_moments(lr, Xb, GA, GA, "x_var")
                if front:
                    dve.wait_ge(s["rstd_ready"], 2 * g + 1)
                    normalise(X, xl, GA, 0).then_inc(s["xl_ready"], 1)
                if back:
                    dve.wait_ge(s["x_rstd"], g)
                    dve.wait_ge(s["xn_free"], g)
                    normalise(Xb, xn, GA, GA).then_inc(s["xn_ready"], 1)
                if front:
                    dve.wait_ge(s["phi_ready"], t1)
                    v.tensor_scalar(phS[:], ps[0:LAT, 2:4, :].rearrange("p n (j d) -> p (n j) d", d=D), phb[:, 0:1], None, ALU.add).then_inc(s["phi_copied"], 1)
                    dve.wait_ge(s["gt_ready"], t1)
                    v.tensor_tensor(gS[:].rearrange("p j c l -> p (j c) l"), ps[:, 4, :].rearrange("p (n l) -> p n l", l=LAT),
                                    gb_bc[:].unsqueeze(1).to_broadcast((P, GA * 2, LAT)), ALU.add).then_inc(s["gt_copied"], 1)
                if back:
                    choose(lr, g - 1)
                if front:
                    for j in range(GA):
                        dve.wait_ge(s["scores_ready"], g * GA + (j + 1))
                        v.tensor_reduce(nm[:, j, :], ps[:, j, :].rearrange("p (c s) -> p c s", c=2), AX, ALU.max, negate=True).then_inc(s["max_ready"], 1)
                if back:
                    place(lr, g - 1)
                if front:
                    for j in range(0, GA, 2):
                        dve.wait_ge(s["pt_ready"], g * GA + (j + 1))
                        v.tensor_copy(Q2[:, j * 2 * D:(j + 1) * 2 * D], ps[:, j, :]).then_inc(s["pt_copied_v"], 1)
                def shared_hidden(f):
                    dve.wait_ge(s["silu_ready"], 2 * g + (f - 1))
                    v.tensor_tensor(hs[:, f, :], hs[:, f, :], ps[:, 7, :], ALU.mult).then_inc(s["hs_ready"], 1)

                if back:
                    shared_hidden(0)
                if not front:
                    lk.before += NGA * FRONT
                    lk.turn(0, 0)
                    tables(lk, E0, NT0)
                    lk.end(1)
                if front:
                    dve.wait_ge(s["p_ready"], t1 * (GA * 2))
                    lk.then(v.reciprocal(rrec[:], rsum[:]))
                    dve.wait_ge(s["pv_ready"], t1)
                    lk.then(v.tensor_tensor(tx[:], ps[:, 4, :].rearrange("p (j c l) -> p j c l", j=GA, c=2),
                                            rrec[:].unsqueeze(3).to_broadcast((P, GA, 2, LAT)), ALU.mult))
                    m_squares = lk.mark(v.tensor_tensor(txq[:], tx[:], tx[:], ALU.mult))
                    v.tensor_reduce(sums[:, 0, :], tx[:].rearrange("p j c l -> p j (c l)"), AX, ALU.add)
                    dve.wait_ge(lk.sem, m_squares)
                    v.tensor_reduce(sums[:, 1, :], txq[:].rearrange("p j c l -> p j (c l)"), AX, ALU.add).then_inc(s["sums_ready"], 1)
                if back:
                    shared_hidden(1)
                if front:
                    dve.wait_ge(s["tot_ready"], t1)
                    inv = 1.0 / (LAT * D)
                    lk.then(v.tensor_scalar(mom[:, 0:2, :], ps[:, 4, 0:2 * GA].rearrange("p (a j) -> p a j", a=2), inv, None, ALU.mult))
                    lk.then(v.tensor_tensor(mom[:, 2, :], mom[:, 0, :], mom[:, 0, :], ALU.mult))
                    v.tensor_tensor(mom[:, 3, :], mom[:, 1, :], mom[:, 2, :], ALU.subtract).then_inc(s["var_ready"], 1)
                if back:
                    dve.wait_ge(s["y_ready"], g)
                    v.scalar_tensor_tensor(Xb, ps[:, 6:8, :].rearrange("p n (j d) -> p (n j) d", d=D), tg[:, 2:3], Xb, ALU.mult, ALU.add).then_inc(s["x2_ready"], 1)
                if front:
                    dve.wait_ge(s["rstd_ready"], 2 * g + 2)
                    for j in range(GA):
                        i = v.tensor_scalar(tx[:, j, :, :], tx[:, j, :, :], mom[:, 0, j:j + 1], mom[:, 2, j:j + 1], ALU.subtract, ALU.mult)
                    lk.then(i)
                    lk.then(v.tensor_tensor(tx[:], tx[:], gbT[:, 0, :, :].unsqueeze(1).to_broadcast((P, GA, KD, LAT)), ALU.mult))
                    v.tensor_tensor(tx[:], tx[:], gbT[:, 1, :, :].unsqueeze(1).to_broadcast((P, GA, KD, LAT)), ALU.add).then_inc(s["h_ready"], 1)
                    dve.wait_ge(s["proj_ready"], t1)
                    lk.then(v.scalar_tensor_tensor(tmp[:], ps[:, 2:4, :].rearrange("p n (j d) -> p (n j) d", d=D), ob[:, 0:1], cx, ALU.add, ALU.add))
                    v.scalar_tensor_tensor(X, tmp[:], tg[:, 0:1], X, ALU.mult, ALU.add).then_inc(s["x1_used"], 1)
                    dve.wait_ge(s["x1_used"], g + 2)
                    assert lk.k == FRONT, lk.k
                if back:
                    assert lr.k == BACK, lr.k

            group_turns(dve, a_turn)
            dve.wait_ge(s["x2_ready"], NGA + 1)

            def b_copy(t, b):
                dve.wait_ge(s["tile_turned"], t + 1)
                v.tensor_copy(XTt[:, b, :], ps[:, b, 0:D]).then_inc(s["tile_copied"], 1)

            def b_h(t, b):
                dve.wait_ge(s["tile_silu"], t + 1)
                v.tensor_tensor(h0_t[:, b, :], su_t[:, b, :], ps[:, 2 + b, P:2 * P], ALU.mult).then_inc(s["tile_h"], 1)

            for t in range(3):
                b_copy(t, t % 2)
            for t in range(2):
                b_h(t, t)
            with dve.Fori(0, (NT0 - 4) // 2) as i:
                for k in range(2):
                    b_copy(2 * i + (k + 3), 1 - k)
                    b_h(2 * i + (k + 2), k)
            b_copy(NT0 - 1, 1)
            b_h(NT0 - 2, 0)
            b_h(NT0 - 1, 1)

            dve.wait_ge(s["tile_y"], NT0)
            v.tensor_copy(cnt[:, 0:E1], base[E1][:]).then_inc(s["setup_dve"], 1)
            v.memset(mask[:], 0.0).then_inc(s["setup_dve"], 1)
            v.memset(VT, 1.0).then_inc(s["setup_dve"], 1)
            v.memset(QK[:, 1, :].bitcast(F32), 1.0).then_inc(s["setup_dve"], 1)
            dve.wait_ge(s["setup_dve"], 13)
            dve.sem_inc(s["phase_done"], 1)
            PAIR = 16
            GATE = 2

            def item_rows(t):
                return xs[:, bass.ds(t, 1), :].rearrange("p a d -> p (a d)")

            def add_expert(t, b, x):
                return v.scalar_tensor_tensor(item_rows(t), gC[:, b, x, :], wts[:, bass.ds(t, 1), x:x + 1].rearrange("p a d -> p (a d)"),
                                              item_rows(t), ALU.mult, ALU.add)

            def c_turn(t, k):
                b = k % 2
                pair = k // 2 * 2
                gate = k % 2 == 1 and item(t - 3)
                choice = k % 2 == 0 and item(t - 4)
                E = E1
                if gate:
                    lk.turn((t - 3) // 2, PAIR)
                if choice:
                    lk.turn((t - 4) // 2, PAIR, GATE)
                l_, k_, e_, d_ = lb[:, 0:2, 0:E], key[:, 0:2, 0:E], ex[:, 0:2, 0:E], den[:, 0:2]
                o_, ox, c_, rk_ = oh[:, 0:2, :, 0:E], ohx[:, 0:2, :, 0:E], cnt[:, 0:E], rk[:, 0:2, 0:E]

                def head(h):
                    if item(t + 2):
                        dve.wait_ge(s["s_ready"], t * NH + (2 * NH + h + 1))
                        v.tensor_reduce(mraw[:, b, h, :], ps[:, h % 2, :].rearrange("p (c l) -> p c l", c=2), AX, ALU.max).then_inc(s["s_max"], 1)

                if item(t + 1):
                    dve.wait_ge(s["s_max"], t * NH + 2 * NH)
                    mr = mraw[:, 1 - b].rearrange("p a c -> p (a c)")
                    v.tensor_scalar(nmr[:, 0, :], mr, -1.0, None, ALU.mult).then_inc(s["m_high"], 1)
                if choice:
                    dve.wait_ge(s["ex_ready"], (t - 4) // 2 + (NGA + 1))
                    m_sum = lk.mark(v.tensor_reduce(d_, e_, AX, ALU.add))
                if item(t + 4):
                    dve.wait_ge(s[f"gathered{b}"], (t + 4) // 2 * 32 + 32)
                    add_expert(t + 4, b, 0).then_inc(s["row_sum0"], 1)
                head(0)
                if item(t + 1):
                    dve.wait_ge(s["m_high"], t + 2)
                    v.scalar_tensor_tensor(nmr[:, 1, :], mr, -1.0, nmr[:, 0, :].bitcast(F32), ALU.mult, ALU.subtract).then_inc(s["m_ready"], 1)
                if item(t + 4):
                    dve.wait_ge(s["row_sum0"], t + 5)
                    add_expert(t + 4, b, 1).then_inc(s["row_sum1"], 1)
                if choice:
                    dve.wait_ge(lk.sem, m_sum)
                    m_inverse = lk.mark(v.reciprocal(d_, d_))
                head(1)
                if item(t + 4):
                    dve.wait_ge(s["row_sum1"], t + 5)
                    dve.sem_inc(s["gather_used"], 1)
                    v.bn_stats(st6[:, 0, :], item_rows(t + 4)).then_inc(s["row_stats"], 1)
                if choice:
                    dve.wait_ge(lk.sem, m_inverse)
                    m_key = lk.mark(v.tensor_tensor(k_, e_, d_.unsqueeze(2).to_broadcast((P, 2, E)), ALU.mult))
                    dve.wait_ge(lk.sem, m_key)
                    alone(dve)
                    for j in range(2):
                        i = v.max(v8[:, j, :], key[:, j, 0:E])
                    m_max = lk.mark(i)
                head(2)
                if item(t + 4):
                    dve.wait_ge(s["row_stats"], t + 5)
                    alone(dve)
                    v.bn_aggr(st2[:, 0, :], st6[:, 0, :]).then_inc(s["var_ready"], 1)
                if item(t - 1):
                    dve.wait_ge(s["o_turned"], t)
                    o6 = ps[:, 6, :].rearrange("p (c h e) -> p c h e", c=2, h=NH)
                    v.reciprocal(orec, o6[:, :, :, DH]).then_inc(s["o_inverse"], 1)
                    dve.wait_ge(s["o_inverse"], t)
                    v.tensor_tensor(oN.rearrange("p (c h d) -> p c h d", c=2, h=NH), o6[:, :, :, 0:DH],
                                    orec.unsqueeze(3).to_broadcast((P, 2, NH, DH)), ALU.mult).then_inc(s["o_norm"], 1)
                if choice:
                    dve.wait_ge(lk.sem, m_max)
                    alone(dve)
                    for j in range(2):
                        i = v.max_index(i8[:, j, :], v8[:, j, :], key[:, j, 0:E])
                    m_index = lk.mark(i)
                head(3)
                if choice:
                    dve.wait_ge(lk.sem, m_index)
                    alone(dve)
                    ig = idxf[:, bass.ds(t - 4, 2), :]
                    m_choice = lk.mark(v.tensor_copy(ig, i8[:, 0:2, 0:2]))
                head(4)
                if item(t - 1):
                    dve.wait_ge(s["ot_ready"], t)
                    v.scalar_tensor_tensor(item_rows(t - 1), ps[:, 6, 0:D], tgg[:, 0:1], item_rows(t - 1), ALU.mult, ALU.add).then_inc(s["x_sum"], 1)
                if choice:
                    dve.wait_ge(lk.sem, m_choice)
                    m_hot = lk.mark(v.tensor_tensor(o_, iota_f[:, 0:E].unsqueeze(1).unsqueeze(1).to_broadcast((P, 2, 2, E)),
                                                    ig.unsqueeze(3).to_broadcast((P, 2, 2, E)), ALU.is_equal))
                if item(t + 4):
                    dve.wait_ge(s["rstd_ready"], t + (2 * NGA + 5))
                    v.tensor_scalar(xl[:, b, :], item_rows(t + 4), st2[:, 0, 0:1], rstd[:, 0:1], ALU.subtract, ALU.mult).then_inc(s["xl_ready"], 1)
                head(5)
                if item(t - 1):
                    dve.wait_ge(s["x_sum"], t)
                    alone(dve)
                    v.bn_stats(st6[:, 1, :], item_rows(t - 1)).then_inc(s["x_stats"], 1)
                if choice:
                    dve.wait_ge(lk.sem, m_hot)
                    v.tensor_tensor(mask[:, 0:2, 0:E], o_[:, :, 0, :], o_[:, :, 1, :], ALU.add).then_inc(s["mask_ready"], 1)
                    m_weighed = lk.mark(v.tensor_tensor(ox, o_, k_.unsqueeze(2).to_broadcast((P, 2, 2, E)), ALU.mult))
                if gate:
                    dve.wait_ge(s["logits_ready"], (t - 3) // 2 + (NGA + 1))
                    m_logits = lk.mark(v.tensor_tensor(l_, ps[:, 7, 0:2 * E].rearrange("p (j e) -> p j e", e=E),
                                                       gbs[:, 0:E].unsqueeze(1).to_broadcast((P, 2, E)), ALU.add))
                head(6)
                if item(t - 1):
                    dve.wait_ge(s["x_stats"], t)
                    alone(dve)
                    v.bn_aggr(st2[:, 1, :], st6[:, 1, :]).then_inc(s["x_var"], 1)
                if gate:
                    dve.wait_ge(lk.sem, m_logits)
                    m_largest = lk.mark(v.tensor_reduce(lmx[:, 0:2], l_, AX, ALU.max))
                if item(t + 4):
                    dve.wait_ge(s["q_high"], t + 5)
                    v.tensor_tensor(split[:, b, 1, :], xl[:, b, :], split[:, b, 0, :].bitcast(F32), ALU.subtract).then_inc(s["q_ready"], 1)
                if choice:
                    dve.wait_ge(lk.sem, m_weighed)
                    m_sel = lk.mark(v.tensor_reduce(sel[:, 0:2, :], ox, AX, ALU.add))
                head(7)
                if gate:
                    dve.wait_ge(lk.sem, m_largest)
                    v.tensor_tensor(e_, l_, lmx[:, 0:2].unsqueeze(2).to_broadcast((P, 2, E)), ALU.subtract).then_inc(s["dif_ready"], 1)
                    assert lk.k == GATE
                if choice:
                    dve.wait_ge(s["rank_ready"], (t - 4) // 2 + (NGA + 1))
                    psK = ps[:, 7, 0:3 * E].rearrange("p (j e) -> p j e", e=E)
                    m_rank = lk.mark(v.tensor_tensor(rk_, psK[:, 0:2, :], c_.unsqueeze(1).to_broadcast((P, 2, E)), ALU.add))
                    dve.wait_ge(lk.sem, m_sel)
                    m_wts = lk.mark(v.tensor_scalar(wts[:, bass.ds(t - 4, 2), :], sel[:, 0:2, :], tg[:, 3:4], None, ALU.mult))
                    dve.wait_ge(lk.sem, m_rank)
                    m_count = lk.mark(v.tensor_tensor(c_, psK[:, 2, :], c_, ALU.add))
                    m_row = lk.mark(v.tensor_tensor(ox, o_, rk_.unsqueeze(2).to_broadcast((P, 2, 2, E)), ALU.mult))
                if item(t - 1):
                    r_ = t - 1
                    dve.wait_ge(s["x_rstd"], t + NGA)
                    if not isinstance(t, int) or r_ >= NC:
                        dve.wait_ge(s[f"scattered{((k - 1) % NC) // 2}"], r_ // NC * 64)
                    else:
                        dve.wait_ge(s["xn_free"], NGA + 1)
                    v.tensor_scalar(xn[:, (k - 1) % NC, :], item_rows(r_), st2[:, 1, 0:1], rstd[:, 1:2], ALU.subtract, ALU.mult).then_inc(s["xn_ready"], 1)
                if choice:
                    dve.wait_ge(lk.sem, m_row)
                    sg = slotf[:, bass.ds(t - 4, 2), :]
                    m_slot = lk.mark(v.tensor_reduce(sg, ox, AX, ALU.add))
                    dve.wait_ge(lk.sem, m_slot)
                    alone(dve)
                    v.tensor_copy(slotu[:, k:k + 2, :], sg).then_inc(s["slots_ready"], 1)
                if choice:
                    assert lk.k == PAIR

            item_turns(dve, c_turn)
            lk.before += B // 2 * PAIR
            lk.turn(0, 0)
            tables(lk, E1, NT1)

            def d_split(src, parts, ready, copied, done, value):
                dve.wait_ge(s[ready], value[0])
                v.tensor_copy(parts[0], src).then_inc(s[copied], 1)
                dve.wait_ge(s[copied], value[1])
                v.tensor_tensor(parts[1], src, parts[0].bitcast(F32), ALU.subtract).then_inc(s[done], 1)

            def d_turn(t, k):
                if is_tile(t + 1):
                    d_split(Ha, (Hap[:, 0], Hap[:, 1]), "l1_h1_gelu", "h1_high", "l1_h1_split", (KH * (t + 2), t + 2))
                if is_tile(t):
                    if is_tile(t - 1):
                        dve.wait_ge(s["tile_y"], NT0 + t)
                    d_split(Hb, (Hbp[:, 0], Hbp[:, 1]), "l1_h2_gelu", "h2_high", "l1_h2_split", (KH * (t + 1), t + 1))
                if is_tile(t + 3):
                    d_split(ps[:, (k + 1) % 2, 0:D], (XTp[:, 0], XTp[:, 1]), "tile_turned", "x_high", "tile_copied",
                            (NT0 + t + 4, t + 4))
                if is_tile(t - 1):
                    b = (k + 1) % 2
                    e = dve.value_load(tab[0:1, t - 1, 0:1], min_val=0, max_val=E1 - 1)
                    dve.wait_ge(s["tile_y"], NT0 + t)
                    if is_tile(t - 3):
                        dve.wait_ge(s[f"output_stored{b}"], ((t - 1) // 2) * 16)
                    v.tensor_tensor(Yt[:, b, :], ps[:, 6 + b, 0:D], b3bc[:, bass.ds(e, 1), :].rearrange("p a d -> p (a d)"),
                                    ALU.add).then_inc(s["tile_out"], 1)

            dve.wait_ge(s["w1_loaded"], 16 * 3)
            tile_turns(dve, d_turn)

            with dve.Fori(0, NGE // 2) as g2:
                for m in range(2):
                    g = 2 * g2 + m
                    dve.wait_ge(s[f"gathered{m}"], g2 * (GE * 2 * 16) + (B // 2 * 32 + GE * 2 * 16))
                    for k in range(2):
                        for j in range(GE):
                            xj = xs[:, bass.ds(g * GE + j, 1), :].rearrange("p a d -> p (a d)")
                            i = v.scalar_tensor_tensor(xj, gE[:, m, j, k, :], wts[:, bass.ds(g * GE + j, 1), k:k + 1].rearrange("p a d -> p (a d)"),
                                                       xj, ALU.mult, ALU.add)
                        i.then_inc(s["out_summed"], 1)
                        dve.wait_ge(s["out_summed"], 2 * g + (k + 1))
                    dve.sem_inc(s["gather_used"], 1)
                    dve.sem_inc(s["out_ready"], 1)

        @blk.scalar
        def _(act):
            a = nc.scalar
            act.dma_start(xs[:, 0:GA, :], x_v[:, 0:GA, :]).then_inc(s["x_loaded"], 16)
            for dst, src in constants[len(constants) // 2:]:
                act.dma_start(dst, src).then_inc(s["consts_loaded"], 16)
            act.wait_ge(s["consts_loaded"], 16 * N_CONST)
            a.activation(tg[:], gates[:, 0:4], ACT.Tanh).then_inc(s["tanh_done"], 1)

            def a_turn(g, front, back):
                if front:
                    act.wait_ge(s["theta_ready"], g + 1)
                    a.activation(thS[:], ps[0:LAT, 0:2, :].rearrange("p n (j d) -> p (n j) d", d=D), ACT.Identity, bias=thb[:, 0:1]).then_inc(s["theta_copied"], 1)
                if back:
                    act.wait_ge(s["xnt_ready"], g)
                    a.copy(xT, ps[:, 6:8, :]).then_inc(s["xnt_copied"], 1)
                    act.wait_ge(s["dif_ready"], g)
                    a.activation(ex[:], ex[:], ACT.Exp).then_inc(s["ex_ready"], 1)
                if front:
                    for j in range(GA):
                        act.wait_ge(s["max_ready"], g * GA + (j + 1))
                        for c in range(2):
                            a.activation(Pm[:, j, c, :], ps[:, j, c * D:(c + 1) * D], ACT.Exp, bias=nm[:, j, c:c + 1],
                                         accum_out=rsum[:, j, c:c + 1]).then_inc(s["p_ready"], 1)
                    for j in range(1, GA, 2):
                        act.wait_ge(s["pt_ready"], g * GA + (j + 1))
                        a.copy(PTm[:, j].rearrange("p c t -> p (c t)"), ps[:, j, :]).then_inc(s["pt_copied_a"], 1)
                if back:
                    for f in range(2):
                        act.wait_ge(s["u_ready"], 2 * g + (f - 1))
                        a.activation(hs[:, f, :], ps[:, 6, :], ACT.Silu).then_inc(s["silu_ready"], 1)
                if front:
                    act.wait_ge(s["ht_ready"], g + 1)
                    a.activation(hS[:], ps[0:LAT, 0:2, :].rearrange("p n (j d) -> p (n j) d", d=D), ACT.Relu).then_inc(s["ht_copied"], 1)

            group_turns(act, a_turn)

            def silu(t, b):
                act.wait_ge(s["ug_ready"], t + 1)
                a.activation(su_t[:, b, :], ps[:, 2 + b, 0:P], ACT.Silu).then_inc(s["tile_silu"], 1)

            def tile_out(t, b, i):
                act.wait_ge(s["tile_y"], t + 1)
                if i is not None:
                    act.wait_ge(s[f"tile_stored{b}"], i * 16)
                a.copy(Yt[:, b, :], ps[:, 4 + b, 0:D]).then_inc(s["tile_out"], 1)

            def hidden_out(t, b):
                act.wait_ge(s["tile_ht"], t + 1)
                a.copy(h0T[:, b, :], ps[:, 6 + b, 0:P]).then_inc(s["tile_ht_copied"], 1)

            silu(0, 0)
            silu(1, 1)
            for k in range(2):
                hidden_out(k, k)
                silu(k + 2, k)
                tile_out(k, k, None)
            with act.Fori(1, (NT0 - 2) // 2) as i:
                for k in range(2):
                    hidden_out(2 * i + k, k)
                    silu(2 * i + (k + 2), k)
                    tile_out(2 * i + k, k, i)
            for k in range(2):
                hidden_out(NT0 - 2 + k, k)
                tile_out(NT0 - 2 + k, k, NT0 // 2 - 1)

            def c_act_turn(t, k):
                b = k % 2
                if item(t - 1):
                    act.wait_ge(s["o_ready"], t)
                    a.copy(oU, ps[:, 4 + (1 - b), :]).then_inc(s["o_copied"], 1)
                for h in range(NH):
                    if item(t):
                        act.wait_ge(s["st_ready"], t * NH + (h + 1))
                        a.activation(PTb[:, h % 4].rearrange("p c q -> p (c q)"), ps[:, 2 + h % 2, :], ACT.Exp,
                                     scale=DH ** -0.5).then_inc(s["st_exp"], 1)
                    if h == 0 and item(t - 2):
                        n = (k + 2) % NC
                        act.wait_ge(s["xnt_ready"], t + (NGA - 1))
                        a.copy(xT[:, :, n * P:(n + 1) * P], ps[:, 7, 0:D].rearrange("p (k t) -> p k t", k=KD)).then_inc(s["xnt_copied"], 1)
                    if h == 3 and item(t + 1):
                        if item(t):
                            act.wait_ge(s["m_stacked"], t * 32 + 32)
                        act.wait_ge(s["vt_ready"], t + 2)
                        a.copy(mT[:], ps[0:2 * 2 * NH, 7, D:D + P]).then_inc(s["mt_copied"], 1)
                        a.copy(VT[:, 1 - b, :, :, 0:DH], ps[:, 7, 0:D].rearrange("p (c h d) -> p c h d", c=2, h=NH)).then_inc(s["vt_copied"], 1)
                    if h == 5 and item(t + 4):
                        if item(t + 2):
                            act.wait_ge(s[f"q_stored{b}"], (t + 4) // 2 * 32)
                        act.wait_ge(s["xl_ready"], t + (NGA + 5))
                        a.copy(split[:, b, 0, :], xl[:, b, :]).then_inc(s["q_high"], 1)
                    if h == NH - 1 and k % 2 == 1 and item(t - 3):
                        act.wait_ge(s["dif_ready"], (t - 3) // 2 + (NGA + 1))
                        a.activation(ex[:, 0:2, 0:E1], ex[:, 0:2, 0:E1], ACT.Exp).then_inc(s["ex_ready"], 1)

            item_turns(act, c_act_turn)

            def gelu(t, which):
                e = act.value_load(tab[0:1, t, 0:1], min_val=0, max_val=E1 - 1)
                bank, dst, bias = (3, Ha, b1T) if which == 1 else (5, Hb, b2T)
                if which == 2 and is_tile(t - 1):
                    act.wait_ge(s["l1_h2_split"], t)
                act.wait_ge(s[f"l1_h{which}_turned"], t + 1)
                for f in range(KH):
                    a.activation(dst[:, f, :], ps[:, bank, f * P:(f + 1) * P], ACT.Gelu,
                                 bias=bias[:, bass.ds(e, 1), f:f + 1].rearrange("p a b -> p (a b)")).then_inc(s[f"l1_h{which}_gelu"], 1)

            def copy(t, which):
                pre, bank = (pre1, 2) if which == 1 else (pre2, 4)
                act.wait_ge(s[f"l1_h{which}_ready"], t + 1)
                a.copy(pre, ps[:, bank, :]).then_inc(s[f"l1_h{which}_copied"], 1)

            def d_act_turn(t, k):
                if is_tile(t + 1):
                    gelu(t + 1, 1)
                if is_tile(t + 2):
                    copy(t + 2, 1)
                if is_tile(t):
                    gelu(t, 2)
                if is_tile(t + 1):
                    copy(t + 1, 2)

            act.wait_ge(s["w1_loaded"], 16 * 3)
            act.wait_ge(s["table_ready"], 2)
            tile_turns(act, d_act_turn)

        @blk.tensor
        def _(pe):
            mm, tr = nc.tensor.matmul, nc.tensor.transpose
            pe.wait_ge(s["setup_pool"], 2)
            pe.wait_ge(s["consts_loaded"], 16 * N_CONST)
            for q in range(2):
                for c in range(KD):
                    o = (q * 2 + c) * LAT
                    i = tr(ps[:, 7, o:o + LAT], gam_n[:, q, c * P:(c + 1) * P], ident[0:LAT, 0:LAT])
            i.then_inc(s["gb_t_ready"], 1)
            pe.wait_ge(s["setup_dve"], 9)

            def count_ranks(n, E, bank, turn):
                pe.wait_ge(s["mask_ready"], turn)
                r = ps[:, bank, 0:(n + 1) * E].rearrange("p (j e) -> p j e", e=E)
                mm(r, tri[:], mask[:, 0:n + 1, 0:E], start=True, stop=False)
                for j in range(n):
                    i = mm(r[:, j + 1:n + 1, :], ones_b[:], mask[:, j, 0:E].unsqueeze(1).to_broadcast((P, n - j, E)),
                           start=False, stop=(j == n - 1))
                i.then_inc(s["rank_ready"], 1)

            def a_pe_turn(g, front, back):
                t1 = g + 1
                if front:
                    pe.wait_ge(s["x1_used"], t1)
                    pe.wait_ge(s["xl_ready"], t1)
                    for q in range(2):
                        i = mm(ps[0:LAT, 2 + q, :], phw[:], xl[:, 2 * q:2 * q + 2, :], start=True, stop=True)
                    i.then_inc(s["phi_ready"], 1)
                    for j in range(GA):
                        for c in range(2):
                            o = (j * 2 + c) * LAT
                            i = mm(ps[:, 4, o:o + LAT], xl[:, j, c * P:(c + 1) * P], gw[:], start=True, stop=True)
                    i.then_inc(s["gt_ready"], 1)
                    pe.wait_ge(s["ctx_loaded"], t1 * 16)
                    for q in range(2):
                        i = mm(ps[0:LAT, q, :], thw[:], cx[:, 2 * q:2 * q + 2, :], start=True, stop=True)
                    i.then_inc(s["theta_ready"], 1)
                if back:
                    pe.wait_ge(s["xn_ready"], g)
                    pe.wait_ge(s["x2_ready"], g)
                    for k in range(KD):
                        for j in range(GA):
                            i = tr(ps[:, 6 + k, j * P:(j + 1) * P], xn[:, j, k * P:(k + 1) * P], ident[:])
                    i.then_inc(s["xnt_ready"], 1)
                if front:
                    pe.wait_ge(s["theta_copied"], t1)
                    pe.wait_ge(s["phi_copied"], t1)
                    for j in range(GA):
                        for c in range(2):
                            i = mm(ps[:, j, c * D:(c + 1) * D], thS[:, j, c * P:(c + 1) * P], phS[:, j, :], start=True, stop=True)
                        i.then_inc(s["scores_ready"], 1)
                        if j == 0 and back:
                            logits(g)
                elif back:
                    logits(g)
                if back:
                    count_ranks(GA, E0, 5, g)
                    pe.wait_ge(s["w0_loaded"], 8 * 16)
                    shared_up(0)
                if front:
                    for j in range(GA):
                        pe.wait_ge(s["p_ready"], g * (GA * 2) + (2 * j + 2))
                        for sc in range(2):
                            for c in range(2):
                                o = sc * D + c * P
                                i = tr(ps[:, j, o:o + P], Pm[:, j, c, sc * P:(sc + 1) * P], ident[:])
                        i.then_inc(s["pt_ready"], 1)
                    pe.wait_ge(s["pt_copied_v"], t1 * 2)
                    pe.wait_ge(s["pt_copied_a"], t1 * 2)
                    pe.wait_ge(s["gt_copied"], t1)
                    for j in range(GA):
                        for c in range(2):
                            o = (j * 2 + c) * LAT
                            for sc in range(2):
                                i = mm(ps[:, 4, o:o + LAT], PTm[:, j, sc, c * P:(c + 1) * P], gS[:, j, sc, :], start=(sc == 0), stop=(sc == 1))
                    i.then_inc(s["pv_ready"], 1)
                if back:
                    pe.wait_ge(s["hs_ready"], 2 * g - 1)
                    shared_up(1)
                if front:
                    pe.wait_ge(s["sums_ready"], t1)
                    mm(ps[:, 4, 0:2 * GA], ones[:], sums[:].rearrange("p a j -> p (a j)"), start=True, stop=True).then_inc(s["tot_ready"], 1)
                if back:
                    pe.wait_ge(s["hs_ready"], 2 * g)
                    for j in range(GA):
                        for f in range(2):
                            o = (j % 2) * D
                            i = mm(ps[:, 6 + j // 2, o:o + D], hs[:, f, j * P:(j + 1) * P], Sds[:, f, :], start=(f == 0), stop=(f == 1))
                    i.then_inc(s["y_ready"], 1)
                if front:
                    pe.wait_ge(s["h_ready"], t1)
                    alone(pe)
                    for j in range(GA):
                        for c in range(2):
                            o = (j % 2) * D + c * P
                            i = tr(ps[0:LAT, j // 2, o:o + P], tx[:, j, c, :], ident[:])
                    i.then_inc(s["ht_ready"], 1)
                    pe.wait_ge(s["ht_copied"], t1)
                    for q in range(2):
                        i = mm(ps[:, 2 + q, :], ow[:], hS[:, 2 * q:2 * q + 2, :], start=True, stop=True)
                    i.then_inc(s["proj_ready"], 1)

            def logits(g):
                pe.wait_ge(s["xnt_copied"], g)
                pe.wait_ge(s["slots_ready"], g - 1)
                for j in range(GA):
                    for k in range(KD):
                        i = mm(ps[:, 5, j * E0:(j + 1) * E0], xT[:, k, j * P:(j + 1) * P], rw[:, k, :], start=(k == 0), stop=(k == KD - 1))
                i.then_inc(s["logits_ready"], 1)

            def shared_up(f):
                for w, bank in ((Sus, 6), (Sgs, 7)):
                    for k in range(KD):
                        i = mm(ps[:, bank, :], w[:, k, f * P:(f + 1) * P], xT[:, k, :], start=(k == 0), stop=(k == KD - 1))
                i.then_inc(s["u_ready"], 1)

            group_turns(pe, a_pe_turn)

            def turn_tile(t, x, b, before, loads):
                pe.wait_ge(s[f"tile_loaded{x}"], loads * 16)
                for k in range(KD):
                    i = tr(ps[:, b, k * P:(k + 1) * P], Xin[:, x, k * P:(k + 1) * P], ident[:])
                i.then_inc(s["tile_turned"], 1)

            def expert0(t):
                return pe.value_load(tab[0:1, t, 0:1], min_val=0, max_val=E0 - 1)

            def up_gate(t, b, e):
                pe.wait_ge(s["tile_copied"], t + 1)
                for k in range(KD):
                    i = mm(ps[:, 2 + b, 0:2 * F0], XTt[:, b, k * P:(k + 1) * P],
                           Wug[:, bass.ds(e, 1), k, :, :].rearrange("p x a f -> p (x a f)"), start=(k == 0), stop=(k == KD - 1))
                i.then_inc(s["ug_ready"], 1)

            def turn_hidden(t, b):
                pe.wait_ge(s["tile_h"], t + 1)
                tr(ps[:, 6 + b, 0:P], h0_t[:, b, :], ident[:]).then_inc(s["tile_ht"], 1)

            def down(t, b, e):
                pe.wait_ge(s["tile_ht_copied"], t + 1)
                mm(ps[:, 4 + b, 0:D], h0T[:, b, :], Wds[:, bass.ds(e, 1), :].rearrange("p a d -> p (a d)"),
                   start=True, stop=True).then_inc(s["tile_y"], 1)

            pe.wait_ge(s["table_ready"], 1)
            for t in range(3):
                turn_tile(t, t, t % 2, 0, 1)
                if t > 0:
                    up_gate(t - 1, t - 1, expert0(t - 1))

            def b_turn(t, k, loads):
                e_next = expert0(t + 2) if not isinstance(t, int) or t + 2 < NT0 else None
                if loads is not None:
                    turn_tile(t + 3, (k + 3) % NX, (k + 1) % 2, 0, loads)
                turn_hidden(t, k % 2)
                if e_next is not None:
                    up_gate(t + 2, k % 2, e_next)
                down(t, k % 2, expert0(t))

            with pe.Fori(0, NT0 // NX - 1) as i4:
                for k in range(NX):
                    b_turn(NX * i4 + k, k, i4 + (1 if k < 1 else 2))
            for t in range(NT0 - NX, NT0):
                b_turn(t, t % NX, NT0 // NX if t + 3 < NT0 else None)

            pe.wait_ge(s["phase_done"], 1)

            def c_pe_turn(t, k):
                b = k % 2
                if item(t - 2):
                    n = (k + 2) % NC
                    pe.wait_ge(s["xn_ready"], t + (NGA - 1))
                    for x in range(KD):
                        i = tr(ps[:, 7, x * P:(x + 1) * P], xn[:, n, x * P:(x + 1) * P], ident[:])
                    i.then_inc(s["xnt_ready"], 1)
                def scores(h):
                    n = (k + 2) % NC
                    if h == 0:
                        pe.wait_ge(s[f"k_stacked{b}"], (t + 2) // 2 * 48 + 48)
                        pe.wait_ge(s[f"q_stacked{b}"], (t + 2) // 2 * 48 + 48)
                    if h >= 2 or item(t + 1):
                        pe.wait_ge(s["s_max"], t * NH + (2 * NH + h - 1))
                    for c in range(2):
                        i = mm(ps[:, h % 2, c * D:(c + 1) * D], QS[0:NK, n, h, c * P:(c + 1) * P], KS[0:NK, n, h, :], start=True, stop=True)
                    i.then_inc(s["s_ready"], 1)

                for h in range(NH + 1):
                    if h == 0 and item(t + 2):
                        scores(0)
                    if h < NH and item(t):
                        if h == 0:
                            pe.wait_ge(s["m_stacked"], t * 32 + 32)
                        if h >= 2 or item(t - 1):
                            pe.wait_ge(s["st_exp"], t * NH + (h - 1))
                        for c in range(2):
                            i = mm(ps[:, 2 + h % 2, c * D:(c + 1) * D], KS[0:NK + 2, k, h, c * P:(c + 1) * P], QS[0:NK + 2, k, h, :], start=True, stop=True)
                        i.then_inc(s["st_ready"], 1)
                    if h < NH - 1 and item(t + 2):
                        scores(h + 1)
                    if h > 0 and h % 2 == 0 and item(t):
                        if h == 2:
                            pe.wait_ge(s["vt_copied"], t + 1)
                            if item(t - 2):
                                pe.wait_ge(s["o_copied"], t - 1)
                        pe.wait_ge(s["st_exp"], t * NH + h)
                        for lc in range(2):
                            for v_h in (h - 2, h - 1):
                                p_, o = v_h % 4 * VE, v_h // 4 * D
                                i = mm(ps[p_:p_ + VE, 4 + b, o:o + D], VT[:, b, lc, v_h, :], PTb[:, v_h % 4, lc, :],
                                       start=(lc == 0), stop=(lc == 1))
                        if h == NH:
                            i.then_inc(s["o_ready"], 1)
                    if h == 1 and item(t - 1):
                        pe.wait_ge(s["o_copied"], t)
                        if item(t - 2):
                            pe.wait_ge(s["x_sum"], t - 1)
                        for c in range(2):
                            for q in range(2):
                                o = (c * 2 + q) * P
                                i = tr(ps[:, 6, o:o + P], oU[:, q * D + c * P:q * D + (c + 1) * P], ident[:])
                        i.then_inc(s["o_turned"], 1)
                    if h == 2 and item(t + 1):
                        if item(t - 2):
                            pe.wait_ge(s["xnt_copied"], t + (NGA - 1))
                        elif item(t):
                            pe.wait_ge(s["vt_copied"], t + 1)
                        pe.wait_ge(s["m_ready"], t + 2)
                        alone(pe)
                        tr(ps[0:2 * 2 * NH, 7, D:D + P], nmr[:].bitcast(F32).rearrange("p t a -> p (t a)"), ident[:])
                        n = (k + 1) % NC
                        pe.wait_ge(s[f"v_loaded{1 - b}"], (t + 1) // 2 * 16 + 16)
                        for c in range(2):
                            i = tr(ps[:, 7, c * P:(c + 1) * P], cx[:, n, c * P:(c + 1) * P], ident[:])
                        i.then_inc(s["vt_ready"], 1)
                    if h == 4 and k % 2 == 1 and item(t - 3):
                        pe.wait_ge(s["xnt_copied"], t + (NGA - 1))
                        if item(t + 1):
                            pe.wait_ge(s["vt_copied"], t + 2)
                        pe.wait_ge(s["slots_ready"], (t - 3) // 2 + NGA)
                        for j in range(2):
                            n = ((k + 1) % NC + j) * P
                            for x in range(KD):
                                i = mm(ps[:, 7, j * E1:(j + 1) * E1], xT[:, x, n:n + P], gwt[:, x, :], start=(x == 0), stop=(x == KD - 1))
                        i.then_inc(s["logits_ready"], 1)
                    if h == 3 and item(t - 1):
                        pe.wait_ge(s["o_norm"], t)
                        for c in range(2):
                            i = tr(ps[:, 6, c * P:(c + 1) * P], oN[:, c * P:(c + 1) * P], ident[:])
                        i.then_inc(s["ot_ready"], 1)
                    if h == 7 and k % 2 == 0 and item(t - 4):
                        if item(t + 1):
                            pe.wait_ge(s["vt_copied"], t + 2)
                        elif item(t - 2):
                            pe.wait_ge(s["xnt_copied"], t + (NGA - 1))
                        count_ranks(2, E1, 7, (t - 4) // 2 + (NGA + 1))

            item_turns(pe, c_pe_turn)

            ring = WR[:].rearrange("p (r n) -> p r n", r=RING)

            def product(out, parts, n_k, place, at, width):
                i = None
                for k in range(n_k):
                    for x_part, w_part in ((0, 0), (1, 0), (0, 1)):
                        o = w_part * WX + at + k * width
                        i = mm(out, parts(x_part, k), ring[:, bass.ds(place, 1), o:o + width].rearrange("p r n -> p (r n)"),
                               start=(k == 0 and x_part == 0 and w_part == 0), stop=(k == n_k - 1 and w_part == 1))
                return i

            def place_of(t):
                return pe.value_load(tab[0:1, t, 2:3], min_val=0, max_val=RING - 1)

            def hidden1(t, e, place):
                pe.wait_ge(s["w_split"], e + NGA)
                pe.wait_ge(s["tile_copied"], NT0 + t + 1)
                product(ps[:, 2, :], lambda part, k: XTp[:, part, k * P:(k + 1) * P], KD, place, 0, H1).then_inc(s["l1_h1_ready"], 1)

            def hidden2(t, place):
                pe.wait_ge(s["l1_h1_split"], t + 1)
                product(ps[:, 4, :], lambda part, k: Hap[:, part, k, :], KH, place, KD * H1, H1).then_inc(s["l1_h2_ready"], 1)

            def hidden3(t, b, place):
                pe.wait_ge(s["l1_h2_split"], t + 1)
                product(ps[:, 6 + b, 0:D], lambda part, k: Hbp[:, part, k, :], KH, place, (KD + KH) * H1, D).then_inc(s["tile_y"], 1)

            def turn_pre(t, which):
                pre, bank = (pre1, 3) if which == 1 else (pre2, 5)
                pe.wait_ge(s[f"l1_h{which}_copied"], t + 1)
                for f in range(KH):
                    i = tr(ps[:, bank, f * P:(f + 1) * P], pre[:, f * P:(f + 1) * P], ident[:])
                i.then_inc(s[f"l1_h{which}_turned"], 1)

            def p_turn(t, k):
                if is_tile(t + 2):
                    e1 = pe.value_load(tab[0:1, t + 2, 0:1], min_val=0, max_val=E1 - 1)
                    place1 = place_of(t + 2)
                if is_tile(t + 1):
                    turn_pre(t + 1, 1)
                if is_tile(t + 2):
                    hidden1(t + 2, e1, place1)
                place2, place3 = (place_of(u) if is_tile(u) else None for u in (t + 1, t - 1))
                if is_tile(t + 3):
                    turn_tile(t + 3, (k + 3) % NX, (k + 1) % 2, NT0, loads1(t + 3, k))
                if is_tile(t):
                    turn_pre(t, 2)
                if is_tile(t - 1):
                    hidden3(t - 1, (k + 1) % 2, place3)
                if is_tile(t + 1):
                    hidden2(t + 1, place2)

            def loads1(t, k):
                return NT0 // NX + t // NX + 1

            pe.wait_ge(s["table_ready"], 2)
            tile_turns(pe, p_turn)




def kernel(**inputs):
    import numpy as _np
    import concourse.bacc as _bacc
    from concourse import mybir as _mybir
    from concourse.bass_utils import run_bass_kernel_spmd as _run

    i = {k: _np.asarray(v) for k, v in inputs.items()}

    def by_feature(b):
        return b.reshape(b.shape[0], -1, P).transpose(2, 0, 1)

    arrays = {
        "x": i["x"], "ctx": i["ctx_2048"], "g_xattn": i["g_xattn"], "g_ffn": i["g_ffn"],
        "theta_wT": i["L0_xattn_theta_w"].T, "theta_b": i["L0_xattn_theta_b"],
        "phi_wT": i["L0_xattn_phi_w"].T, "phi_b": i["L0_xattn_phi_b"],
        "g_wT": i["L0_xattn_g_w"].T, "g_b": i["L0_xattn_g_b"],
        "ln_gamma": i["L0_xattn_ln_gamma"], "ln_beta": i["L0_xattn_ln_beta"],
        "out_wT": i["L0_xattn_out_w"].T, "out_b": i["L0_xattn_out_b"],
        "router_wT": i["L0_ffn_router_w"].T, "router_bias": i["L0_ffn_router_bias"],
        "Wu0": i["L0_ffn_Wu"], "Wg0": i["L0_ffn_Wg"], "Wd0": i["L0_ffn_Wd"],
        "Su": i["L0_ffn_Su"], "Sg": i["L0_ffn_Sg"], "Sd": i["L0_ffn_Sd"],
        "gamma1": i["L1_xattn_gamma"].reshape(1, 1),
        "W1": i["L1_ffn_W1"], "b1": by_feature(i["L1_ffn_b1"]), "W2": i["L1_ffn_W2"], "b2": by_feature(i["L1_ffn_b2"]),
        "W3": i["L1_ffn_W3"], "b3": i["L1_ffn_b3"], "gate_w": i["L1_ffn_Wg"], "gate_b": i["L1_ffn_bg"],
    }
    arrays = {k: _np.ascontiguousarray(v) for k, v in arrays.items()}
    nc = _bacc.Bacc("TRN2", target_bir_lowering=False, num_devices=1)
    args = {k: nc.dram_tensor(f"in_{k}", v.shape, _mybir.dt.from_np(v.dtype), kind="ExternalInput").ap()
            for k, v in arrays.items()}
    out = nc.dram_tensor("out", i["x"].shape, _mybir.dt.float32, kind="ExternalOutput").ap()
    flamingo_kernel(nc, **args, out=out)
    r = _run(nc, [{f"in_{k}": v for k, v in arrays.items()}], core_ids=[0])
    return r.results[0]["out"]
```
